# Optimizing a Trainium2 kernel written in Bass

```python
import numpy as np
import jax
import jax.numpy as jnp

def _softmax(x, axis=-1):
    return jax.nn.softmax(x, axis=axis)

def _gelu(x):
    return jax.nn.gelu(x, approximate=True)

def _silu(x):
    return jax.nn.silu(x)

def _sigmoid(x):
    return jax.nn.sigmoid(x)

def _layernorm(x, axis=-1, eps=1e-05):
    m = jnp.mean(x, axis=axis, keepdims=True)
    v = jnp.var(x, axis=axis, keepdims=True)
    return (x - m) / jnp.sqrt(v + eps)

def _scatter_add(tgt, idx, src, axis=0):
    return tgt.at[idx].add(src)

def _segment_sum(src, seg, n):
    return jax.ops.segment_sum(src, seg, n)
kernel_name = 'mk_decoder_preln_d2_seqx_r8_fa7af5'

def setup_inputs(seed: int=0):
    np.random.seed(seed)
    _w = jnp.asarray

    def _rec_inputs():
        import jax
        import jax.numpy as jnp
        _rk = jax.random.key(seed)
        x = -0.0002928 + 1 * jax.random.normal(jax.random.fold_in(_rk, 1), (32, 64, 512), jnp.float32)
        _lenS = 64 - jax.random.randint(jax.random.fold_in(_rk, 7), (32,), 0, max(1, 64 // 4) + 1, jnp.int32)
        _lenS2 = 64 - jax.random.randint(jax.random.fold_in(_rk, 8), (32,), 0, max(1, 64 // 4) + 1, jnp.int32)
        _ctx_4096P = jax.random.normal(jax.random.fold_in(_rk, 11), (32, 16, 512), jnp.float32)
        _ctx_4096c = jax.random.dirichlet(jax.random.fold_in(_rk, 511), 0.3 * jnp.ones((16,), jnp.float32), (32, 64))
        _ctx_4096t = jnp.einsum('bsk,bkd->bsd', _ctx_4096c, _ctx_4096P)
        _ctx_4096t = _ctx_4096t * jax.lax.rsqrt(jnp.mean(jnp.square(_ctx_4096t)) + 1e-12) * 0.953939
        ctx_4096 = -2.8382e-05 + 0.999851 * (_ctx_4096t + 0.3 * jax.random.normal(jax.random.fold_in(_rk, 611), (32, 64, 512), jnp.float32))
        _validS = jnp.arange(64)[None, :] < _lenS[:, None]
        _validS2 = jnp.arange(64)[None, :] < _lenS2[:, None]
        _causal = jnp.tril(jnp.ones((64, 64), dtype=bool))
        mask_1x1xSxS2_ff0 = jnp.where(jnp.ones((1, 1, 64, 64), dtype=bool), 0.0, -1000000000.0).astype(jnp.float32)
        mask_SxS2_bk0 = jnp.logical_not(jnp.broadcast_to(_validS2[0:1, :], (64, 64)))
        return (x, ctx_4096, mask_1x1xSxS2_ff0, mask_SxS2_bk0)
    x, ctx_4096, mask_1x1xSxS2_ff0, mask_SxS2_bk0 = _rec_inputs()

    def _L0_attn_setup():
        import jax, jax.numpy as jnp
        import numpy as np
        HIDDEN = 512
        N_HEADS = 32
        N_KV_HEADS = 8
        HEAD_DIM = HIDDEN // N_HEADS
        N_REP = N_HEADS // N_KV_HEADS
        KV_DIM = N_KV_HEADS * HEAD_DIM

        def _kaiming_uniform(key, out_f, in_f):
            bound = 1.0 / np.sqrt(in_f)
            return jax.random.uniform(key, (out_f, in_f), jnp.float32, -bound, bound)

        def bitnet_linear(x, weight, scale_param):
            s = jnp.maximum(jnp.mean(jnp.abs(weight), axis=1), 1e-08)
            binary_w = jnp.sign(weight / s[:, None])
            y = jnp.einsum('bsi,oi->bso', x, binary_w)
            y = y * (s * scale_param)[None, None, :]
            return jnp.nan_to_num(y, nan=0.0, posinf=1000000.0, neginf=-1000000.0)
        key = jax.random.key(seed)
        ks = jax.random.split(key, 5)
        return {'hidden_states': jax.random.normal(ks[0], (1, 256, HIDDEN), jnp.float32), 'q_weight': _kaiming_uniform(ks[1], HIDDEN, HIDDEN), 'q_scale': jnp.ones((HIDDEN,), jnp.float32), 'k_weight': _kaiming_uniform(ks[2], KV_DIM, HIDDEN), 'k_scale': jnp.ones((KV_DIM,), jnp.float32), 'v_weight': _kaiming_uniform(ks[3], KV_DIM, HIDDEN), 'v_scale': jnp.ones((KV_DIM,), jnp.float32), 'o_weight': _kaiming_uniform(ks[4], HIDDEN, HIDDEN), 'o_scale': jnp.ones((HIDDEN,), jnp.float32)}
    _L0_attn_all = _L0_attn_setup()
    _L0_attn_in = {k: v for k, v in _L0_attn_all.items() if k in ('q_weight', 'q_scale', 'k_weight', 'k_scale', 'v_weight', 'v_scale', 'o_weight', 'o_scale')}
    del _L0_attn_all

    def _L0_xattn_setup():
        import jax, jax.numpy as jnp
        import numpy as np
        B, Q, K, D = (1, 128, 6404, 512)
        H, KVH, HD = (32, 8, 128)
        GROUPS = H // KVH
        EPS = 1e-05

        def _rmsnorm(x, w):
            xf = x.astype(jnp.float32)
            var = jnp.mean(xf * xf, axis=-1, keepdims=True)
            return (xf * jax.lax.rsqrt(var + EPS)).astype(x.dtype) * w
        key = jax.random.key(seed)
        ks = jax.random.split(key, 8)
        s = 0.02
        return {'hidden_states': jax.random.normal(ks[0], (B, Q, D), jnp.float32), 'cross_attention_states': jax.random.normal(ks[1], (B, K, D), jnp.float32), 'attention_mask': jnp.zeros((B, 1, Q, K), jnp.float32), 'Wq': jax.random.normal(ks[2], (H * HD, D), jnp.float32) * s, 'Wk': jax.random.normal(ks[3], (KVH * HD, D), jnp.float32) * s, 'Wv': jax.random.normal(ks[4], (KVH * HD, D), jnp.float32) * s, 'Wo': jax.random.normal(ks[5], (D, H * HD), jnp.float32) * s, 'q_norm_w': jnp.ones((HD,), jnp.float32), 'k_norm_w': jnp.ones((HD,), jnp.float32)}
    _L0_xattn_all = _L0_xattn_setup()
    _L0_xattn_in = {k: v for k, v in _L0_xattn_all.items() if k in ('Wq', 'Wk', 'Wv', 'Wo', 'q_norm_w', 'k_norm_w')}
    del _L0_xattn_all

    def _L0_ffn_setup():
        import jax, jax.numpy as jnp
        import numpy as np
        DIM = 512
        INTER = 1792
        SPARSITY = 32
        RANK = 16
        key = jax.random.key(seed)
        ks = jax.random.split(key, 5)
        B, T = (32, 1)
        x = jax.random.normal(ks[0], (B, T, DIM), dtype=jnp.float32)
        c1_w = jax.random.normal(ks[1], (RANK, DIM), dtype=jnp.float32) * (1.0 / np.sqrt(DIM))
        c2_w = jax.random.normal(ks[2], (INTER, RANK), dtype=jnp.float32) * (1.0 / np.sqrt(RANK))
        w1 = jax.random.normal(ks[3], (INTER, DIM), dtype=jnp.float32) * (1.0 / np.sqrt(DIM))
        w2t = jax.random.normal(ks[4], (INTER, DIM), dtype=jnp.float32) * (1.0 / np.sqrt(INTER))
        return {'x': x, 'c1_w': c1_w, 'c2_w': c2_w, 'w1': w1, 'w2t': w2t}
    _L0_ffn_all = _L0_ffn_setup()
    _L0_ffn_in = {k: v for k, v in _L0_ffn_all.items() if k in ('c1_w', 'c2_w', 'w1', 'w2t')}
    del _L0_ffn_all

    def _L1_attn_setup():
        import math
        import jax, jax.numpy as jnp
        import numpy as np
        NUM_HEADS = 32
        HIDDEN = 512
        HEAD_DIM = HIDDEN // NUM_HEADS
        NEG_INF = -1e+30

        def _alibi_slopes(n: int) -> jnp.ndarray:
            cp2 = 2 ** math.floor(math.log2(n))
            base = 2.0 ** (-2.0 ** (-(math.log2(cp2) - 3)))
            slopes = base ** np.arange(1, cp2 + 1, dtype=np.float64)
            if cp2 != n:
                extra_base = 2.0 ** (-2.0 ** (-(math.log2(2 * cp2) - 3)))
                rem = min(cp2, n - cp2)
                extra = extra_base ** np.arange(1, 1 + 2 * rem, 2, dtype=np.float64)
                slopes = np.concatenate([slopes, extra])
            return jnp.asarray(slopes, dtype=jnp.float32)
        key = jax.random.key(seed)
        k1, k2, k3 = jax.random.split(key, 3)
        B, S = (2, 256)
        hidden_states = jax.random.normal(k1, (B, S, HIDDEN), dtype=jnp.float32)
        Wqkv = jax.random.normal(k2, (HIDDEN, NUM_HEADS * HEAD_DIM + 2 * HEAD_DIM), dtype=jnp.float32) * 0.02
        Wo = jax.random.normal(k3, (HIDDEN, HIDDEN), dtype=jnp.float32) * 0.02
        return {'hidden_states': hidden_states, 'Wqkv': Wqkv, 'Wo': Wo}
    _L1_attn_all = _L1_attn_setup()
    _L1_attn_in = {k: v for k, v in _L1_attn_all.items() if k in ('Wqkv', 'Wo')}
    del _L1_attn_all

    def _L1_xattn_setup():
        import jax, jax.numpy as jnp
        import numpy as np
        N_HEAD = 32
        D_MODEL = 512
        N_KV_GROUPS = 8
        D_HEAD = D_MODEL // N_HEAD
        H_PER_G = N_HEAD // N_KV_GROUPS
        KV_DIM = N_KV_GROUPS * D_HEAD
        B, S = (2, 256)
        key = jax.random.key(seed)
        ks = jax.random.split(key, 8)
        q = jax.random.normal(ks[0], (B, S, D_MODEL), dtype=jnp.float32)
        k = jax.random.normal(ks[1], (B, S, D_MODEL), dtype=jnp.float32)
        v = jax.random.normal(ks[2], (B, S, D_MODEL), dtype=jnp.float32)
        mask = jnp.tril(jnp.ones((S, S), dtype=bool))
        w_q = jax.random.uniform(ks[3], (D_MODEL, D_MODEL), dtype=jnp.float32) * 0.02
        w_k = jax.random.uniform(ks[4], (KV_DIM, D_MODEL), dtype=jnp.float32) * 0.02
        w_v = jax.random.uniform(ks[5], (KV_DIM, D_MODEL), dtype=jnp.float32) * 0.02
        w_out = jax.random.uniform(ks[6], (D_MODEL, D_MODEL), dtype=jnp.float32) * 0.02
        return {'q': q, 'k': k, 'v': v, 'w_q': w_q, 'w_k': w_k, 'w_v': w_v, 'w_out': w_out, 'mask': mask}
    _L1_xattn_all = _L1_xattn_setup()
    _L1_xattn_in = {k: v for k, v in _L1_xattn_all.items() if k in ('w_q', 'w_k', 'w_v', 'w_out')}
    del _L1_xattn_all

    def _L1_ffn_setup():
        import jax, jax.numpy as jnp
        import numpy as np
        B, S, IN, OUT = (4, 256, 512, 512)
        E, K, R = (8, 2, 16)
        CAP_FACTOR = 3.0
        ALPHA = 1.0 / R
        LN_EPS = 1e-05
        key = jax.random.key(seed)
        ks = jax.random.split(key, 6)
        return {'x': jax.random.normal(ks[0], (B, S, IN), dtype=jnp.float32), 'weight': jax.random.normal(ks[1], (OUT, IN), dtype=jnp.float32) * 0.02, 'lora_A': jax.random.normal(ks[2], (E, IN, R), dtype=jnp.float32) / np.sqrt(R), 'lora_B': jax.random.normal(ks[3], (E, R, OUT), dtype=jnp.float32) * 0.02, 'gw1': jax.random.normal(ks[4], (4 * E, IN), dtype=jnp.float32) * 0.02, 'gb1': jnp.zeros((4 * E,), dtype=jnp.float32), 'ln_gamma': jnp.ones((4 * E,), dtype=jnp.float32), 'ln_beta': jnp.zeros((4 * E,), dtype=jnp.float32), 'gw2': jax.random.normal(ks[5], (E, 4 * E), dtype=jnp.float32) * 0.02, 'gb2': jnp.zeros((E,), dtype=jnp.float32)}
    _L1_ffn_all = _L1_ffn_setup()
    _L1_ffn_in = {k: v for k, v in _L1_ffn_all.items() if k in ('weight', 'lora_A', 'lora_B', 'gw1', 'gb1', 'ln_gamma', 'ln_beta', 'gw2', 'gb2')}
    del _L1_ffn_all
    return {'x': x, 'ctx_4096': ctx_4096, 'mask_1x1xSxS2_ff0': mask_1x1xSxS2_ff0, 'mask_SxS2_bk0': mask_SxS2_bk0, 'L0_attn_q_weight': _L0_attn_in['q_weight'], 'L0_attn_q_scale': _L0_attn_in['q_scale'], 'L0_attn_k_weight': _L0_attn_in['k_weight'], 'L0_attn_k_scale': _L0_attn_in['k_scale'], 'L0_attn_v_weight': _L0_attn_in['v_weight'], 'L0_attn_v_scale': _L0_attn_in['v_scale'], 'L0_attn_o_weight': _L0_attn_in['o_weight'], 'L0_attn_o_scale': _L0_attn_in['o_scale'], 'L0_xattn_Wq': _L0_xattn_in['Wq'], 'L0_xattn_Wk': _L0_xattn_in['Wk'], 'L0_xattn_Wv': _L0_xattn_in['Wv'], 'L0_xattn_Wo': _L0_xattn_in['Wo'], 'L0_xattn_q_norm_w': _L0_xattn_in['q_norm_w'], 'L0_xattn_k_norm_w': _L0_xattn_in['k_norm_w'], 'L0_ffn_c1_w': _L0_ffn_in['c1_w'], 'L0_ffn_c2_w': _L0_ffn_in['c2_w'], 'L0_ffn_w1': _L0_ffn_in['w1'], 'L0_ffn_w2t': _L0_ffn_in['w2t'], 'L1_attn_Wqkv': _L1_attn_in['Wqkv'], 'L1_attn_Wo': _L1_attn_in['Wo'], 'L1_xattn_w_q': _L1_xattn_in['w_q'], 'L1_xattn_w_k': _L1_xattn_in['w_k'], 'L1_xattn_w_v': _L1_xattn_in['w_v'], 'L1_xattn_w_out': _L1_xattn_in['w_out'], 'L1_ffn_weight': _L1_ffn_in['weight'], 'L1_ffn_lora_A': _L1_ffn_in['lora_A'], 'L1_ffn_lora_B': _L1_ffn_in['lora_B'], 'L1_ffn_gw1': _L1_ffn_in['gw1'], 'L1_ffn_gb1': _L1_ffn_in['gb1'], 'L1_ffn_ln_gamma': _L1_ffn_in['ln_gamma'], 'L1_ffn_ln_beta': _L1_ffn_in['ln_beta'], 'L1_ffn_gw2': _L1_ffn_in['gw2'], 'L1_ffn_gb2': _L1_ffn_in['gb2']}

def reference(x, ctx_4096, mask_1x1xSxS2_ff0, mask_SxS2_bk0, L0_attn_q_weight, L0_attn_q_scale, L0_attn_k_weight, L0_attn_k_scale, L0_attn_v_weight, L0_attn_v_scale, L0_attn_o_weight, L0_attn_o_scale, L0_xattn_Wq, L0_xattn_Wk, L0_xattn_Wv, L0_xattn_Wo, L0_xattn_q_norm_w, L0_xattn_k_norm_w, L0_ffn_c1_w, L0_ffn_c2_w, L0_ffn_w1, L0_ffn_w2t, L1_attn_Wqkv, L1_attn_Wo, L1_xattn_w_q, L1_xattn_w_k, L1_xattn_w_v, L1_xattn_w_out, L1_ffn_weight, L1_ffn_lora_A, L1_ffn_lora_B, L1_ffn_gw1, L1_ffn_gb1, L1_ffn_ln_gamma, L1_ffn_ln_beta, L1_ffn_gw2, L1_ffn_gb2):
    import jax
    import jax.numpy as jnp

    def _L0_attn_ref(hidden_states, q_weight, q_scale, k_weight, k_scale, v_weight, v_scale, o_weight, o_scale):
        import jax, jax.numpy as jnp
        import numpy as np
        HIDDEN = 512
        N_HEADS = 32
        N_KV_HEADS = 8
        HEAD_DIM = HIDDEN // N_HEADS
        N_REP = N_HEADS // N_KV_HEADS
        KV_DIM = N_KV_HEADS * HEAD_DIM

        def _kaiming_uniform(key, out_f, in_f):
            bound = 1.0 / np.sqrt(in_f)
            return jax.random.uniform(key, (out_f, in_f), jnp.float32, -bound, bound)

        def bitnet_linear(x, weight, scale_param):
            s = jnp.maximum(jnp.mean(jnp.abs(weight), axis=1), 1e-08)
            binary_w = jnp.sign(weight / s[:, None])
            y = jnp.einsum('bsi,oi->bso', x, binary_w)
            y = y * (s * scale_param)[None, None, :]
            return jnp.nan_to_num(y, nan=0.0, posinf=1000000.0, neginf=-1000000.0)
        b, s, _ = hidden_states.shape
        q = bitnet_linear(hidden_states, q_weight, q_scale)
        k = bitnet_linear(hidden_states, k_weight, k_scale)
        v = bitnet_linear(hidden_states, v_weight, v_scale)
        q = q.reshape(b, s, N_HEADS, HEAD_DIM).transpose(0, 2, 1, 3)
        k = k.reshape(b, s, N_KV_HEADS, HEAD_DIM).transpose(0, 2, 1, 3)
        v = v.reshape(b, s, N_KV_HEADS, HEAD_DIM).transpose(0, 2, 1, 3)
        k = jnp.repeat(k, N_REP, axis=1)
        v = jnp.repeat(v, N_REP, axis=1)
        scores = jnp.einsum('bhqd,bhkd->bhqk', q, k) / np.sqrt(HEAD_DIM)
        attn = jax.nn.softmax(scores, axis=-1)
        out = jnp.einsum('bhqk,bhkd->bhqd', attn, v)
        out = out.transpose(0, 2, 1, 3).reshape(b, s, HIDDEN)
        return bitnet_linear(out, o_weight, o_scale)

    def _L0_xattn_ref(hidden_states, cross_attention_states, attention_mask, Wq, Wk, Wv, Wo, q_norm_w, k_norm_w):
        import jax, jax.numpy as jnp
        import numpy as np
        B, Q, K, D = (1, 128, 6404, 512)
        H, KVH, HD = (32, 8, 128)
        GROUPS = H // KVH
        EPS = 1e-05

        def _rmsnorm(x, w):
            xf = x.astype(jnp.float32)
            var = jnp.mean(xf * xf, axis=-1, keepdims=True)
            return (xf * jax.lax.rsqrt(var + EPS)).astype(x.dtype) * w
        bsz, q_len, _ = hidden_states.shape
        kv_len = cross_attention_states.shape[1]
        q = (hidden_states @ Wq.T).reshape(bsz, q_len, H, HD).transpose(0, 2, 1, 3)
        k = (cross_attention_states @ Wk.T).reshape(bsz, kv_len, KVH, HD).transpose(0, 2, 1, 3)
        v = (cross_attention_states @ Wv.T).reshape(bsz, kv_len, KVH, HD).transpose(0, 2, 1, 3)
        q = _rmsnorm(q, q_norm_w)
        k = jnp.repeat(k, GROUPS, axis=1)
        v = jnp.repeat(v, GROUPS, axis=1)
        k = _rmsnorm(k, k_norm_w)
        scale = 1.0 / np.sqrt(HD)
        scores = jnp.einsum('bhqd,bhkd->bhqk', q, k) * scale
        scores = scores + attention_mask[:, :, :, :kv_len]
        probs = jax.nn.softmax(scores.astype(jnp.float32), axis=-1).astype(q.dtype)
        out = jnp.einsum('bhqk,bhkd->bhqd', probs, v)
        out = out.transpose(0, 2, 1, 3).reshape(bsz, q_len, H * HD)
        return out @ Wo.T

    def _L0_ffn_ref(x, c1_w, c2_w, w1, w2t):
        import jax, jax.numpy as jnp
        import numpy as np
        DIM = 512
        INTER = 1792
        SPARSITY = 32
        RANK = 16
        B, T, M = x.shape
        xf = x.reshape(B * T, M)
        inter = xf @ c1_w.T @ c2_w.T
        n_blocks = INTER // SPARSITY
        blk = inter.reshape(B * T, n_blocks, SPARSITY)
        idx = jnp.argmax(blk, axis=-1) + jnp.arange(0, INTER, SPARSITY)
        w1_g = w1[idx]
        w2_g = w2t[idx]
        h = jax.nn.relu(jnp.einsum('bkm,bm->bk', w1_g, xf))
        out = jnp.einsum('bk,bkm->bm', h, w2_g)
        return out.reshape(B, T, M)

    def _L1_attn_ref(hidden_states, Wqkv, Wo):
        import math
        import jax, jax.numpy as jnp
        import numpy as np
        NUM_HEADS = 32
        HIDDEN = 512
        HEAD_DIM = HIDDEN // NUM_HEADS
        NEG_INF = -1e+30

        def _alibi_slopes(n: int) -> jnp.ndarray:
            cp2 = 2 ** math.floor(math.log2(n))
            base = 2.0 ** (-2.0 ** (-(math.log2(cp2) - 3)))
            slopes = base ** np.arange(1, cp2 + 1, dtype=np.float64)
            if cp2 != n:
                extra_base = 2.0 ** (-2.0 ** (-(math.log2(2 * cp2) - 3)))
                rem = min(cp2, n - cp2)
                extra = extra_base ** np.arange(1, 1 + 2 * rem, 2, dtype=np.float64)
                slopes = np.concatenate([slopes, extra])
            return jnp.asarray(slopes, dtype=jnp.float32)
        B, S, H = hidden_states.shape
        nH, d = (NUM_HEADS, HEAD_DIM)
        scale = d ** (-0.5)
        qkv = hidden_states @ Wqkv
        q = qkv[..., :nH * d].reshape(B, S, nH, d)
        k = qkv[..., nH * d:nH * d + d]
        v = qkv[..., nH * d + d:]
        scores = jnp.einsum('bqhd,bkd->bhqk', q, k) * scale
        pos_q = jnp.arange(S)[:, None]
        pos_k = jnp.arange(S)[None, :]
        slopes = _alibi_slopes(nH)
        alibi = slopes[:, None, None] * (pos_k - pos_q).astype(jnp.float32)
        causal = pos_k <= pos_q
        scores = jnp.where(causal[None, None], scores + alibi[None], NEG_INF)
        probs = jax.nn.softmax(scores, axis=-1)
        attn = jnp.einsum('bhqk,bkd->bqhd', probs, v).reshape(B, S, H)
        return attn @ Wo

    def _L1_xattn_ref(q, k, v, w_q, w_k, w_v, w_out, mask):
        import jax, jax.numpy as jnp
        import numpy as np
        N_HEAD = 32
        D_MODEL = 512
        N_KV_GROUPS = 8
        D_HEAD = D_MODEL // N_HEAD
        H_PER_G = N_HEAD // N_KV_GROUPS
        KV_DIM = N_KV_GROUPS * D_HEAD
        B, S = (2, 256)
        b, n, _ = q.shape
        s = k.shape[1]
        query = q @ w_q.T
        key = k @ w_k.T
        value = v @ w_v.T
        query = query.reshape(b, n, N_HEAD, D_HEAD).transpose(0, 2, 1, 3)
        query = query.reshape(b, N_KV_GROUPS, H_PER_G, n, D_HEAD)
        key = key.reshape(b, s, N_KV_GROUPS, D_HEAD).transpose(0, 2, 1, 3)
        value = value.reshape(b, s, N_KV_GROUPS, D_HEAD).transpose(0, 2, 1, 3)
        scores = jnp.einsum('bghnd,bgsd->bghns', query, key) / D_HEAD ** 0.5
        scores = jnp.where(mask, scores, jnp.finfo(scores.dtype).min)
        attention = jax.nn.softmax(scores, axis=-1)
        out = jnp.einsum('bghns,bgsd->bghnd', attention, value)
        out = out.transpose(0, 3, 1, 2, 4).reshape(b, n, D_MODEL)
        return out @ w_out.T

    def _L1_ffn_ref(x, weight, lora_A, lora_B, gw1, gb1, ln_gamma, ln_beta, gw2, gb2):
        import jax, jax.numpy as jnp
        import numpy as np
        B, S, IN, OUT = (4, 256, 512, 512)
        E, K, R = (8, 2, 16)
        CAP_FACTOR = 3.0
        ALPHA = 1.0 / R
        LN_EPS = 1e-05
        orig_shape = x.shape
        xf = x.reshape(-1, orig_shape[-1])
        N = xf.shape[0]
        capacity = int(CAP_FACTOR * N / E)
        h = xf @ gw1.T + gb1
        mu = jnp.mean(h, axis=-1, keepdims=True)
        var = jnp.mean((h - mu) ** 2, axis=-1, keepdims=True)
        h = (h - mu) * jax.lax.rsqrt(var + LN_EPS) * ln_gamma + ln_beta
        h = jax.nn.relu(h)
        gates = h @ gw2.T + gb2
        top_v, top_i = jax.lax.top_k(gates, K)
        top_g = jax.nn.softmax(top_v, axis=-1)
        onehot = (top_i[..., None] == jnp.arange(E)).astype(xf.dtype)
        counts = onehot.sum(axis=0)
        allowed = (counts <= capacity).astype(xf.dtype)
        w = jnp.einsum('nke,nk,ke->ne', onehot, top_g, allowed)
        main = xf @ weight.T
        tmp = jnp.einsum('ni,eir->enr', xf, lora_A)
        tmp = tmp * w.T[:, :, None]
        lora = jnp.einsum('enr,ero->no', tmp, lora_B) * ALPHA
        out = main + lora
        return out.reshape(*orig_shape[:-1], weight.shape[0])
    x = x + _L0_attn_ref(_layernorm(x, axis=-1), L0_attn_q_weight, L0_attn_q_scale, L0_attn_k_weight, L0_attn_k_scale, L0_attn_v_weight, L0_attn_v_scale, L0_attn_o_weight, L0_attn_o_scale)
    x = x + _L0_xattn_ref(_layernorm(x, axis=-1), ctx_4096, mask_1x1xSxS2_ff0, L0_xattn_Wq, L0_xattn_Wk, L0_xattn_Wv, L0_xattn_Wo, L0_xattn_q_norm_w, L0_xattn_k_norm_w)
    x = x + _L0_ffn_ref(_layernorm(x, axis=-1), L0_ffn_c1_w, L0_ffn_c2_w, L0_ffn_w1, L0_ffn_w2t)
    x = x + _L1_attn_ref(_layernorm(x, axis=-1), L1_attn_Wqkv, L1_attn_Wo)
    x = x + _L1_xattn_ref(_layernorm(x, axis=-1), ctx_4096, ctx_4096, L1_xattn_w_q, L1_xattn_w_k, L1_xattn_w_v, L1_xattn_w_out, mask_SxS2_bk0)
    x = x + _L1_ffn_ref(_layernorm(x, axis=-1), L1_ffn_weight, L1_ffn_lora_A, L1_ffn_lora_B, L1_ffn_gw1, L1_ffn_gb1, L1_ffn_ln_gamma, L1_ffn_ln_beta, L1_ffn_gw2, L1_ffn_gb2)
    return x

_drawn_inputs = setup_inputs


def setup_inputs(seed=0):
    import zlib

    import numpy as np

    out = dict(_drawn_inputs(seed))
    spreads = {'L0_attn_q_scale': (1.0, 0.6),
     'L0_attn_k_scale': (1.0, 0.6),
     'L0_attn_v_scale': (1.0, 0.6),
     'L0_attn_o_scale': (1.0, 0.6),
     'L0_xattn_q_norm_w': (1.0, 0.2),
     'L0_xattn_k_norm_w': (1.0, 0.2),
     'L1_ffn_gb1': (0.0, 0.8),
     'L1_ffn_ln_gamma': (1.0, 0.6),
     'L1_ffn_ln_beta': (0.0, 0.8),
     'L1_ffn_gb2': (0.0, 0.531)}
    factors = {'L0_attn_q_weight': 3.397,
     'L0_attn_k_weight': 3.268,
     'L1_xattn_w_q': 8.0,
     'L1_xattn_w_k': 8.0,
     'L1_xattn_w_out': 4.093,
     'L1_ffn_lora_A': 4.616,
     'L1_ffn_lora_B': 4.639,
     'L1_ffn_gw1': 6.019,
     'L1_ffn_gw2': 5.584}
    for name, (base, spread) in spreads.items():
        noise = np.random.default_rng([zlib.crc32(name.encode()), seed]).standard_normal(out[name].shape)
        drawn = base * np.exp(spread * noise) if base else spread * noise
        out[name] = jnp.asarray(drawn.astype(out[name].dtype))
    for name, factor in factors.items():
        out[name] = (out[name] * factor).astype(out[name].dtype)
    return out
```

```python
from contextlib import ExitStack

import numpy as np

import concourse.bass as bass
from concourse import mybir

F32 = mybir.dt.float32
F32R = mybir.dt.float32r
U8 = mybir.dt.uint8
ALU = mybir.AluOpType
ACT = mybir.ActivationFunctionType
AX_X = mybir.AxisListType.X

P = 128
D = 512
KC = D // P
TOK = 2048
TILES = TOK // P
ST = 4
STOK = ST * P
NST = TILES // ST
SEQ = 64
SB = STOK // SEQ
HD = 16
CH = P // HD
LN_EPS = 1e-5


class Sig:

    def __init__(self, sem, base, per):
        self.sem, self.base, self.per = sem, base, per

    def at(self, i, k):
        return i * self.per + (self.base + k)

    def before(self, i):
        return i * self.per + self.base


class Signals:

    def __init__(self, ctx, nc, names):
        self.sems = {name: ctx.enter_context(nc.semaphore(name)) for name in names}
        self.total = {name: 1 for name in names}

    def get(self, name, per, passes):
        sig = Sig(self.sems[name], self.total[name], per)
        self.total[name] += per * passes
        return sig


class Memory:

    def __init__(self, ctx, nc, prefix, signals):
        self.ctx, self.nc, self.prefix, self.signals = ctx, nc, prefix, signals

    def sb(self, name, shape, dt=F32):
        return self.ctx.enter_context(self.nc.sbuf_tensor(f"{self.prefix}_{name}", shape, dt))

    def ps(self, name):
        return self.ctx.enter_context(self.nc.psum_tensor(f"{self.prefix}_{name}", [P, 512], F32))

    def sig(self, name, per=1, passes=NST):
        return self.signals.get(name, per, passes)


def products(eng, out, pairs):
    steps = []
    for lhs, rhs in pairs:
        if isinstance(lhs, tuple) and isinstance(rhs, tuple):
            steps += [(lhs[0], rhs[0]), (lhs[0], rhs[1]), (lhs[1], rhs[0])]
        elif isinstance(lhs, tuple):
            steps += [(lhs[0], rhs), (lhs[1], rhs)]
        elif isinstance(rhs, tuple):
            steps += [(lhs, rhs[0]), (lhs, rhs[1])]
        else:
            steps += [(lhs, rhs)]
    for n, (a, b) in enumerate(steps):
        last = eng.matmul(out, a, b, start=(n == 0), stop=(n == len(steps) - 1))
    return last


def x_tile(X, i, t):
    return X[:, bass.ds((i * ST + t) * D, D)]


class LayerNorm:

    def __init__(self, mem, X, ident, eps, wrap=0, width=STOK, xn=None, passes=NST):
        self.X, self.ident, self.eps, self.wrap = X, ident, eps, wrap
        self.stats = mem.sb("ln_stats", [P, ST, 6])
        self.mv = mem.sb("ln_mean_var", [P, ST, 2])
        self.sd = mem.sb("ln_sd", [P, ST])
        self.rstd = mem.sb("ln_rstd", [P, ST])
        self.off = 0
        self.xn = mem.sb("xn", [P, ST, D]) if xn is None else xn
        self.hi = mem.sb("xnT_hi", [P, KC, width + wrap], F32R)
        self.lo = mem.sb("xnT_lo", [P, KC, width + wrap], F32R)
        self.stat = mem.sig("ln_stat", ST + ST + 1)
        self.sd_ready = mem.sig("ln_sd_ready")
        self.xn_ready = mem.sig("xn_ready", ST)
        self.turned = mem.sig("xn_turned", ST)
        self.hi_ready = mem.sig("xnT_hi_ready", ST + (1 if wrap else 0))
        self.lo_ready = mem.sig("xnT_lo_ready", ST + (1 if wrap else 0))

    def vector_norm(self, eng, i):
        for t in range(ST):
            eng.bn_stats(self.stats[:, t, :], x_tile(self.X, i, t)).then_inc(self.stat.sem, 1)
        eng.wait_ge(self.stat.sem, self.stat.at(i, ST))
        eng.memset(self.rstd[:, :], 0.0)
        for t in range(ST):
            eng.bn_aggr(self.mv[:, t, :], self.stats[:, t, :]).then_inc(self.stat.sem, 1)
        eng.wait_ge(self.sd_ready.sem, self.sd_ready.at(i, 1))
        eng.reciprocal(self.rstd[:, :], self.sd[:, :]).then_inc(self.stat.sem, 1)
        eng.wait_ge(self.stat.sem, self.stat.at(i, 2 * ST + 1))
        eng.wait_ge(self.turned.sem, self.turned.before(i))
        for t in range(ST):
            eng.tensor_scalar(self.xn[:, t, :], x_tile(self.X, i, t), self.mv[:, t, 0:1],
                              self.rstd[:, t:t + 1], ALU.subtract, ALU.mult)\
               .then_inc(self.xn_ready.sem, 1)

    def scalar_sd(self, eng, i):
        eng.wait_ge(self.stat.sem, self.stat.at(i, 2 * ST))
        eng.activation(self.sd[:, :], self.mv[:, :, 1], ACT.Sqrt, bias=self.eps[:, 0:1])\
           .then_inc(self.sd_ready.sem, 1)

    def tensor_turn(self, eng, i, t, bank):
        eng.wait_ge(self.xn_ready.sem, self.xn_ready.at(i, t + 1))
        for k in range(KC):
            last = eng.transpose(bank[:, k * P:(k + 1) * P], self.xn[:, t, k * P:(k + 1) * P],
                                 self.ident[:, :])
        last.then_inc(self.turned.sem, 1)

    def _part(self, a, t):
        return a[:, :, self.off + t * P:self.off + (t + 1) * P]

    def scalar_hi(self, eng, i, t, bank):
        eng.wait_ge(self.turned.sem, self.turned.at(i, t + 1))
        eng.activation(self._part(self.hi, t), bank[:, :].rearrange("p (k n) -> p k n", k=KC),
                       ACT.Copy).then_inc(self.hi_ready.sem, 1)

    def vector_lo(self, eng, i, t, bank):
        eng.wait_ge(self.hi_ready.sem, self.hi_ready.at(i, t + 1))
        eng.tensor_tensor(self._part(self.lo, t), bank[:, :].rearrange("p (k n) -> p k n", k=KC),
                          self._part(self.hi, t).bitcast(F32), ALU.subtract)\
           .then_inc(self.lo_ready.sem, 1)

    def scalar_wrap(self, eng, i):
        eng.wait_ge(self.hi_ready.sem, self.hi_ready.at(i, 1))
        eng.activation(self.hi[:, :, STOK:], self.hi[:, :, 0:self.wrap].bitcast(F32), ACT.Copy)\
           .then_inc(self.hi_ready.sem, 1)

    def vector_wrap(self, eng, i):
        eng.wait_ge(self.lo_ready.sem, self.lo_ready.at(i, 1))
        eng.tensor_copy(self.lo[:, :, STOK:], self.lo[:, :, 0:self.wrap].bitcast(F32))\
           .then_inc(self.lo_ready.sem, 1)


def small_attention(nc, signals, kind, X, consts, dram, prefix):
    ident, eps, ones, headmask = consts["ident"], consts["eps"], consts["ones"], consts["headmask"]
    sign, alibi, cross = kind == "sign", kind == "alibi", kind == "cross"
    KW = P if alibi else D
    NK = 1 if alibi else KC
    NU = KC * ST
    RING = 5
    TR = 3
    LASTSLOT = NU + TR + 2
    with ExitStack() as ctx:
        mem = Memory(ctx, nc, prefix, signals)
        dq, dk, dv, do = dram["q"], dram["k"], dram["v"], dram["o"]
        parts = 1 if sign else 2
        Wq = [mem.sb(f"Wq{n}", [P, KC, D], F32R) for n in range(parts)]
        Wk = [mem.sb(f"Wk{n}", [P, KC, KW], F32R) for n in range(parts)]
        Wv = [mem.sb(f"Wv{n}", [P, KC, P], F32R) for n in range(parts)]
        Wo = [mem.sb(f"Wo{n}", [P, KC, D], F32R) for n in range(parts)]
        ln = LayerNorm(mem, X, ident, eps, wrap=SEQ if not cross else 0)
        if cross:
            cth = mem.sb("ctxT_hi", [P, KC, STOK + SEQ], F32R)
            ctl = mem.sb("ctxT_lo", [P, KC, STOK + SEQ], F32R)
            m01 = mem.sb("mask01", [P, SEQ])
            mbias = mem.sb("mask_bias", [P, SEQ])
            mraw = mem.sb("mask_raw", [P, SEQ], U8)
        qT = mem.sb("qT", [P, KC, STOK])
        krep = mem.sb("krep", [P, 2, STOK])
        NB = 1 if alibi else 2
        Kbd = mem.sb("Kbd", [P, NB, SB, CH, SEQ])
        Vbd = mem.sb("Vbd", [P, SB, 8, 2 * HD])
        T = mem.sb("T", [P, RING, CH, SEQ])
        mx = mem.sb("row_max", [P, 2, CH])
        rs = mem.sb("row_sum", [P, 2, CH])
        ri = mem.sb("row_inv", [P, RING, CH])
        PT = mem.sb("PT", [P, 2, 4, P])
        oh = ln.hi if cross else mem.sb("oT_hi", [P, KC, STOK], F32R)
        ol = ln.lo if cross else mem.sb("oT_lo", [P, KC, STOK], F32R)
        if alibi:
            table = mem.sb("alibi", [P, KC, CH, SEQ])
        if sign:
            qs = mem.sb("q_scale", [P, KC])
            ks = mem.sb("k_scale", [P, KC])
            vs = mem.sb("v_scale", [P, KC])
            osc = mem.sb("o_scale", [P, D])
            kmask = mem.sb("k_mask", [P, KC, CH])
            ysc = mem.sb("y_scaled", [P, D])
            scraw = mem.sb("scales_raw", [P, 3, KC])
            scp = mem.sb("scales_mean", [P, 3, KC])
        G = [mem.ps(f"G{n}") for n in range(2)]
        S = [mem.ps(f"S{n}") for n in range(2)]
        TP = [mem.ps(f"TP{n}") for n in range(2)]
        OT = [mem.ps(f"OT{n}") for n in range(2)]

        n_landed = 16 * (4 + (2 if alibi else 0) + (5 if sign else 0) + (2 if cross else 0))
        PRE = 9 if sign else 3 if cross else 1
        w_raw = mem.sig("weights_landed", n_landed, 1)
        w_hi = mem.sig("weights_hi", 4, 1)
        w_abs = mem.sig("weights_abs", 4 if sign else 0, 1)
        w_lo = mem.sig("weights_lo", 0 if sign else 4, 1)
        pre = mem.sig("prologue_vector", PRE, 1)
        pre_pool = mem.sig("prologue_pool", 1, 1)
        pre_pe = mem.sig("prologue_pe", 1 if sign else 0, 1)
        q_done = mem.sig("q_product", KC)
        q_ready = mem.sig("q_ready", KC)
        k_done = mem.sig("k_product", NK)
        krep_ready = mem.sig("krep_ready", NK)
        kbd_pool = mem.sig("kbd_by_pool", NK)
        kbd_vec = mem.sig("kbd_by_vector", NK)
        v_done = mem.sig("v_product", ST)
        v_ready = mem.sig("v_ready", ST)
        s_done = mem.sig("scores", NU)
        s_read = mem.sig("scores_read", 0 if sign else NU)
        vec = mem.sig("vector_chain", 2 * NU)
        sub_ready = mem.sig("shifted", NU)
        exp_ready = mem.sig("exponentials", NU)
        inv_ready = mem.sig("inverse_sums", NU)
        biased = mem.sig("biased", NU if cross else 0)
        norm_ready = mem.sig("probabilities", NU)
        t_done = mem.sig("probs_turned", NU)
        pt_ready = mem.sig("PT_ready", NU)
        pv_done = mem.sig("values_product", NU)
        oh_ready = mem.sig("oT_hi_ready", KC)
        ol_ready = mem.sig("oT_lo_ready", KC)
        y_done = mem.sig("y_product", ST)
        y_added = mem.sig("y_added", ST * (2 if sign else 1))
        if cross:
            ctx_landed = mem.sig("ctx_landed", 16)
            cth_ready = mem.sig("ctx_hi_ready", 2)
            ctl_ready = mem.sig("ctx_lo_ready", 2)

        KbF = Kbd[:, :, :, :, :].rearrange("p a b h s -> p (a b h s)")
        qTF = qT[:, :, :].rearrange("p k n -> p (k n)")
        rq = KbF[:, 0:KC * D].rearrange("p (k n) -> p k n", k=KC)
        ro = KbF[:, KC * D:2 * KC * D].rearrange("p (k n) -> p k n", k=KC)
        kv_room = qTF if alibi else KbF[:, 2 * KC * D:]
        rk = kv_room[:, 0:KC * KW].rearrange("p (k n) -> p k n", k=KC)
        rv = kv_room[:, KC * KW:KC * KW + KC * P].rearrange("p (k n) -> p k n", k=KC)
        rvw = ln.xn
        raws = [(rq, Wq, dq), (rk, Wk, dk), (rv, Wv, dv), (ro, Wo, do)]

        def pair(w, f):
            return f(w[0]) if sign else (f(w[0]), f(w[1]))

        kv_hi, kv_lo = (cth, ctl) if cross else (ln.hi, ln.lo)

        uses = [(ln.lo_ready, t + 1) for t in range(ST)]
        uses += [(q_ready, c + 1) for c in range(KC)]
        uses += [(krep_ready, c + 1) for c in range(min(NK, 2))]
        uses += [(v_ready, t + 1) for t in range(ST)]
        uses += [(krep_ready, c + 1) for c in range(2, NK)]
        uses += [(y_added, (t + 1) * (2 if sign else 1)) for t in range(ST)]

        block = ctx.enter_context(nc.Block())

        @block.sync
        def _(eng):
            for raw, _, d in raws:
                eng.dma_start(raw, d).then_inc(w_raw.sem, 16)
            extra = []
            if alibi:
                extra = [(table[0:SEQ, :, :, :], dram["alibi"]), (table[SEQ:P, :, :, :], dram["alibi"])]
            if sign:
                extra = [(scraw[:, n, :], dram["scales"][n]) for n in range(3)]
                extra += [(osc[:, :], dram["o_scale"].partition_broadcast(P)), (rvw[:, :, :], dram["v_rep"])]
            if cross:
                extra = [(mraw[0:SEQ, :], dram["mask"]), (mraw[SEQ:P, :], dram["mask"])]
            for a, b in extra:
                eng.dma_start(a, b).then_inc(w_raw.sem, 16)
            if cross:
                with eng.Fori(0, NST) as i:
                    eng.wait_ge(ln.turned.sem, ln.turned.before(i))
                    eng.dma_start(ln.xn[:, :, :], dram["ctxT"][:, :, bass.ds(i * STOK, STOK)])\
                       .then_inc(ctx_landed.sem, 16)

        def stage_context(i, eng, part):
            raw = ln.xn
            if part == "hi":
                eng.wait_ge(ctx_landed.sem, ctx_landed.at(i, 16))
                eng.wait_ge(v_done.sem, v_done.before(i))
                eng.wait_ge(k_done.sem, k_done.before(i))
                eng.activation(cth[:, :, 0:STOK], raw[:, :, :], ACT.Copy).then_inc(cth_ready.sem, 1)
                eng.activation(cth[:, :, STOK:], raw[:, :, 0:SEQ], ACT.Copy).then_inc(cth_ready.sem, 1)
            else:
                eng.wait_ge(cth_ready.sem, cth_ready.at(i, 2))
                eng.tensor_tensor(ctl[:, :, 0:STOK], raw[:, :, :], cth[:, :, 0:STOK].bitcast(F32),
                                  ALU.subtract).then_inc(ctl_ready.sem, 1)
                eng.tensor_tensor(ctl[:, :, STOK:], raw[:, :, 0:SEQ], cth[:, :, STOK:].bitcast(F32),
                                  ALU.subtract).then_inc(ctl_ready.sem, 1)

        @block.scalar
        def _(eng):
            eng.wait_ge(w_raw.sem, w_raw.at(0, n_landed))
            for raw, w, _ in raws:
                eng.activation(w[0][:, :, :], raw, ACT.Sign if sign else ACT.Copy).then_inc(w_hi.sem, 1)
            if sign:
                eng.wait_ge(w_hi.sem, w_hi.at(0, 4))
                for raw in (rq, rk, rvw, ro):
                    eng.activation(raw[:, :, :], raw[:, :, :], ACT.Abs).then_inc(w_abs.sem, 1)
            with eng.Fori(0, NST) as i:
                if cross:
                    stage_context(i, eng, "hi")
                ln.scalar_sd(eng, i)
                for t in range(ST):
                    ln.scalar_hi(eng, i, t, G[t % 2])
                if not cross:
                    ln.scalar_wrap(eng, i)
                for c in range(KC):
                    eng.wait_ge(q_done.sem, q_done.at(i, c + 1))
                    if sign:
                        eng.activation(qT[:, c, :], G[c % 2][:, :], ACT.Copy, scale=qs[:, c:c + 1])\
                           .then_inc(q_ready.sem, 1)
                    else:
                        eng.activation(qT[:, c, :], G[c % 2][:, :], ACT.Copy, scale=HD ** -0.5)\
                           .then_inc(q_ready.sem, 1)

                def keep_krep(c):
                    eng.wait_ge(k_done.sem, k_done.at(i, c + 1))
                    if c >= 2:
                        eng.wait_ge(kbd_pool.sem, kbd_pool.at(i, c - 1))
                        eng.wait_ge(kbd_vec.sem, kbd_vec.at(i, c - 1))
                    use = ST + KC + c + (ST if c >= 2 else 0)
                    eng.activation(krep[:, c % 2, :], G[use % 2][:, :], ACT.Copy)\
                       .then_inc(krep_ready.sem, 1)

                for c in range(min(NK, 2)):
                    keep_krep(c)
                for t in range(ST):
                    bank = G[(ST + KC + min(NK, 2) + t) % 2]
                    eng.wait_ge(v_done.sem, v_done.at(i, t + 1))
                    va = bank[:, 0:P].rearrange("p (g d) -> p g d", d=HD)
                    vb = bank[:, P:2 * P].rearrange("p (g d) -> p g d", d=HD)
                    for lo, hi, src, b, at in ((0, SEQ, va, 2 * t, 0), (SEQ, P, va, 2 * t + 1, HD),
                                               (0, SEQ, vb, 2 * t + 1, 0), (SEQ, P, vb, (2 * t + 2) % SB, HD)):
                        last = eng.activation(Vbd[lo:hi, b, :, at:at + HD], src[lo:hi, :, :], ACT.Copy)
                    last.then_inc(v_ready.sem, 1)
                for s in range(LASTSLOT + 2):
                    e = s - 1 if cross else s
                    if 0 <= e < NU:
                        eng.wait_ge(sub_ready.sem, sub_ready.at(i, e + 1))
                        row = T[:, e % RING, :, :]
                        eng.activation(row, row, ACT.Exp).then_inc(exp_ready.sem, 1)
                    if s % 4 == 3 and 2 + s // 4 < NK:
                        keep_krep(2 + s // 4)
                    u = s - TR
                    if 0 <= u < NU:
                        eng.wait_ge(t_done.sem, t_done.at(i, u + 1))
                        if u >= 2:
                            eng.wait_ge(pv_done.sem, pv_done.at(i, u - 1))
                        else:
                            eng.wait_ge(pv_done.sem, pv_done.before(i))
                        eng.activation(PT[:, u % 2, :, :],
                                       TP[u % 2][:, :].rearrange("p (j n) -> p j n", j=4), ACT.Copy)\
                           .then_inc(pt_ready.sem, 1)
                    c = (s - TR - 5) // 4
                    if s - TR - 5 == 4 * c and 0 <= c < KC:
                        eng.wait_ge(pv_done.sem, pv_done.at(i, 4 * c + 4))
                        eng.activation(oh[:, c, :], OT[c % 2][:, :], ACT.Copy,
                                       scale=vs[:, c:c + 1] if sign else 1.0).then_inc(oh_ready.sem, 1)

        @block.gpsimd
        def _(eng):
            eng.memset(Vbd[:, :, :, :], 0.0).then_inc(pre_pool.sem, 1)
            if not sign:
                for n, (raw, w, _) in enumerate(raws):
                    eng.wait_ge(w_hi.sem, w_hi.at(0, n + 1))
                    eng.tensor_tensor(w[1][:, :, :], raw, w[0][:, :, :].bitcast(F32), ALU.subtract)\
                       .then_inc(w_lo.sem, 1)
            with eng.Fori(0, NST) as i:
                if cross:
                    stage_context(i, eng, "lo")

                def spread_keys(c):
                    eng.wait_ge(krep_ready.sem, krep_ready.at(i, c + 1))
                    if c >= 2:
                        eng.wait_ge(s_done.sem, s_done.at(i, 4 * (c - 1)))
                    else:
                        eng.wait_ge(s_done.sem, s_done.before(i))
                    if sign:
                        eng.wait_ge(pre.sem, pre.at(0, PRE))
                    if not sign:
                        eng.wait_ge(w_lo.sem, w_lo.at(0, 4))
                    src = krep[:, c % 2, :].rearrange("p (b s) -> p b s", b=SB)
                    for h in range(CH // 2):
                        m = kmask[:, c, h:h + 1] if sign else headmask[:, h:h + 1]
                        if h == 0:
                            eng.tensor_tensor(Kbd[:, c % NB, :, h, :], src,
                                              m.unsqueeze(2).to_broadcast([P, SB, SEQ]), ALU.mult)
                            continue
                        last = eng.tensor_scalar(Kbd[:, c % NB, :, h, :], src, m, 0.0, ALU.mult, ALU.add)
                    last.then_inc(kbd_pool.sem, 1)

                for c in range(min(NK, 2)):
                    spread_keys(c)
                for s in range(NU + 2):
                    if cross and s < NU:
                        eng.wait_ge(s_read.sem, s_read.at(i, s + 1))
                        row = T[:, s % RING, :, :]
                        eng.tensor_tensor(row, row, mbias[:, :].unsqueeze(1).to_broadcast([P, CH, SEQ]),
                                          ALU.add).then_inc(biased.sem, 1)
                    u = s - 2
                    if 0 <= u < NU:
                        eng.wait_ge(inv_ready.sem, inv_ready.at(i, u + 1))
                        row = T[:, u % RING, :, :]
                        eng.tensor_tensor(row, row, ri[:, u % RING, :].unsqueeze(2).to_broadcast([P, CH, SEQ]),
                                          ALU.mult).then_inc(norm_ready.sem, 1)
                    if s % 4 == 3 and 2 + s // 4 < NK:
                        spread_keys(2 + s // 4)

        @block.vector
        def _(eng):
            count = [0]

            def step(ins):
                count[0] += 1
                ins.then_inc(pre.sem, 1)
                eng.wait_ge(pre.sem, pre.at(0, count[0]))

            if sign:
                eng.wait_ge(pre_pe.sem, pre_pe.at(0, 1))
                qkv = G[0][:, 0:3 * KC].rearrange("p (n c) -> p n c", n=3)
                step(eng.tensor_scalar(scp[:, :, :], qkv, 1.0 / D, 1e-8, ALU.mult, ALU.max))
                step(eng.tensor_tensor(scp[:, :, :], scp[:, :, :], scraw[:, :, :], ALU.mult))
                step(eng.tensor_scalar(qs[:, :], scp[:, 0, :], HD ** -0.5, None, ALU.mult))
                step(eng.tensor_copy(ks[:, :], scp[:, 1, :]))
                step(eng.tensor_copy(vs[:, :], scp[:, 2, :]))
                step(eng.tensor_tensor(kmask[:, :, :], ks[:, :].unsqueeze(2).to_broadcast([P, KC, CH]),
                                       headmask[:, :].unsqueeze(1).to_broadcast([P, KC, CH]), ALU.mult))
                step(eng.tensor_scalar(ysc[:, :], G[1][:, :], 1.0 / D, 1e-8, ALU.mult, ALU.max))
                step(eng.tensor_tensor(osc[:, :], osc[:, :], ysc[:, :], ALU.mult))
            if cross:
                eng.wait_ge(w_raw.sem, w_raw.at(0, n_landed))
                step(eng.tensor_copy(m01[:, :], mraw[:, :]))
                step(eng.tensor_scalar(mbias[:, :], m01[:, :], 1.0, float(np.finfo(np.float32).max),
                                       ALU.subtract, ALU.mult))
            if alibi:
                eng.wait_ge(w_raw.sem, w_raw.at(0, n_landed))
            step(eng.memset(ri[:, :, :], 0.0))
            assert count[0] == PRE, count[0]
            with eng.Fori(0, NST) as i:
                if cross:
                    eng.wait_ge(ctl_ready.sem, ctl_ready.at(i, 2))
                ln.vector_norm(eng, i)
                for t in range(ST):
                    ln.vector_lo(eng, i, t, G[t % 2])
                if not cross:
                    ln.vector_wrap(eng, i)
                links = [0]

                def chain(ins):
                    links[0] += 1
                    ins.then_inc(vec.sem, 1)
                    return links[0]

                def spread_keys(c):
                    eng.wait_ge(krep_ready.sem, krep_ready.at(i, c + 1))
                    if c >= 2:
                        eng.wait_ge(s_done.sem, s_done.at(i, 4 * (c - 1)))
                    else:
                        eng.wait_ge(s_done.sem, s_done.before(i))
                    if not sign:
                        eng.wait_ge(w_lo.sem, w_lo.at(0, 4))
                    src = krep[:, c % 2, :].rearrange("p (b s) -> p b s", b=SB)
                    for h in range(CH // 2, CH):
                        m = kmask[:, c, h:h + 1] if sign else headmask[:, h:h + 1]
                        last = eng.tensor_scalar(Kbd[:, c % NB, :, h, :], src, m, None, ALU.mult)
                    last.then_inc(kbd_vec.sem, 1)

                for c in range(min(NK, 2)):
                    spread_keys(c)

                def take_scores(u):
                    eng.wait_ge(s_done.sem, s_done.at(i, u + 1))
                    if u >= RING:
                        eng.wait_ge(t_done.sem, t_done.at(i, u - RING + 1))
                    else:
                        eng.wait_ge(t_done.sem, t_done.before(i))
                    src = S[u % 2][:, :].rearrange("p (h s) -> p h s", h=CH)
                    row = T[:, u % RING, :, :]
                    if alibi:
                        eng.tensor_tensor(row, src, table[:, u // ST, :, :], ALU.add)\
                           .then_inc(s_read.sem, 1)
                    elif cross:
                        eng.tensor_tensor(row, src, m01[:, :].unsqueeze(1).to_broadcast([P, CH, SEQ]),
                                          ALU.mult).then_inc(s_read.sem, 1)

                def shift(u):
                    row = T[:, u % RING, :, :]
                    src = row
                    if cross:
                        eng.wait_ge(biased.sem, biased.at(i, u + 1))
                    elif alibi:
                        eng.wait_ge(s_read.sem, s_read.at(i, u + 1))
                    else:
                        src = S[u % 2][:, :].rearrange("p (h s) -> p h s", h=CH)
                    n = chain(eng.reduce_max(mx[:, u % 2, :], src, AX_X))
                    eng.wait_ge(vec.sem, vec.at(i, n))
                    last = eng.tensor_tensor(row, src, mx[:, u % 2, :].unsqueeze(2).to_broadcast([P, CH, SEQ]),
                                             ALU.subtract)
                    last.then_inc(sub_ready.sem, 1)

                def invert(u):
                    eng.wait_ge(exp_ready.sem, exp_ready.at(i, u + 1))
                    n = chain(eng.reduce_sum(rs[:, u % 2, :], T[:, u % RING, :, :], AX_X))
                    eng.wait_ge(vec.sem, vec.at(i, n))
                    eng.reciprocal(ri[:, u % RING, :], rs[:, u % 2, :]).then_inc(inv_ready.sem, 1)

                for s in range(LASTSLOT + 2):
                    if s < NU:
                        take_scores(s)
                    if 0 <= s - 2 < NU:
                        invert(s - 2) if not cross else None
                    u = s - 1 if cross else s
                    if 0 <= u < NU:
                        shift(u)
                    if cross and 0 <= s - 2 < NU:
                        invert(s - 2)
                    if s % 4 == 3 and 2 + s // 4 < NK:
                        spread_keys(2 + s // 4)
                    c = (s - TR - 5) // 4
                    if s - TR - 5 == 4 * c and 0 <= c < KC:
                        eng.wait_ge(oh_ready.sem, oh_ready.at(i, c + 1))
                        if sign:
                            eng.scalar_tensor_tensor(ol[:, c, :], OT[c % 2][:, :], vs[:, c:c + 1],
                                                     oh[:, c, :].bitcast(F32), ALU.mult, ALU.subtract)\
                               .then_inc(ol_ready.sem, 1)
                        else:
                            eng.tensor_tensor(ol[:, c, :], OT[c % 2][:, :], oh[:, c, :].bitcast(F32),
                                              ALU.subtract).then_inc(ol_ready.sem, 1)
                for t in range(ST):
                    bank = G[(len(uses) - ST + t) % 2]
                    eng.wait_ge(y_done.sem, y_done.at(i, t + 1))
                    xt = x_tile(X, i, t)
                    if sign:
                        eng.wait_ge(y_added.sem, y_added.at(i, 2 * t))
                        eng.tensor_tensor(ysc[:, :], bank[:, :], osc[:, :], ALU.mult).then_inc(y_added.sem, 1)
                        eng.wait_ge(y_added.sem, y_added.at(i, 2 * t + 1))
                        eng.tensor_tensor(xt, xt, ysc[:, :], ALU.add).then_inc(y_added.sem, 1)
                    else:
                        eng.tensor_tensor(xt, xt, bank[:, :], ALU.add).then_inc(y_added.sem, 1)

        @block.tensor
        def _(eng):
            eng.wait_ge(w_hi.sem, w_hi.at(0, 4))
            if not sign:
                eng.wait_ge(w_lo.sem, w_lo.at(0, 4))
            eng.wait_ge(pre_pool.sem, pre_pool.at(0, 1))
            if sign:
                eng.wait_ge(w_abs.sem, w_abs.at(0, 4))
                for n, raw in ((0, rq), (1, rk), (2, rvw)):
                    for c in range(KC):
                        for k in range(KC):
                            eng.matmul(G[0][:, n * KC + c:n * KC + c + 1],
                                       raw[:, k, c * P:(c + 1) * P], ones[:, 0:1],
                                       start=(k == 0), stop=(k == KC - 1))
                for k in range(KC):
                    last = eng.matmul(G[1][:, :], ones[:, :], ro[:, k, :], start=(k == 0), stop=(k == KC - 1))
                last.then_inc(pre_pe.sem, 1)
                eng.wait_ge(pre.sem, pre.at(0, PRE))
            with eng.Fori(0, NST) as i:
                n = [0]

                def bank():
                    u = n[0]
                    n[0] += 1
                    if u >= 2:
                        sig, k = uses[u - 2]
                        eng.wait_ge(sig.sem, sig.at(i, k))
                    else:
                        eng.wait_ge(y_added.sem, y_added.before(i))
                    return G[u % 2]

                for t in range(ST):
                    ln.tensor_turn(eng, i, t, bank())
                eng.wait_ge(ln.lo_ready.sem, ln.lo_ready.before(i + 1))
                eng.wait_ge(ln.hi_ready.sem, ln.hi_ready.before(i + 1))
                for c in range(KC):
                    b = bank()
                    products(eng, b[:, :], [(pair(Wq, lambda w: w[:, k, c * P:(c + 1) * P]),
                                             (ln.hi[:, k, 0:STOK], ln.lo[:, k, 0:STOK])) for k in range(KC)])\
                        .then_inc(q_done.sem, 1)
                if cross:
                    eng.wait_ge(cth_ready.sem, cth_ready.at(i, 2))
                    eng.wait_ge(ctl_ready.sem, ctl_ready.at(i, 2))

                def keys(c):
                    b = bank()
                    products(eng, b[:, :], [(pair(Wk, lambda w: w[:, k, c * P:(c + 1) * P]),
                                             (kv_hi[:, k, 0:STOK], kv_lo[:, k, 0:STOK])) for k in range(KC)])\
                        .then_inc(k_done.sem, 1)

                for c in range(min(NK, 2)):
                    keys(c)
                for t in range(ST):
                    b = bank()
                    for side in range(2):
                        at = t * P + side * SEQ
                        last = products(eng, b[:, side * P:(side + 1) * P],
                                        [((kv_hi[:, k, at:at + P], kv_lo[:, k, at:at + P]),
                                          pair(Wv, lambda w: w[:, k, :])) for k in range(KC)])
                    last.then_inc(v_done.sem, 1)
                eng.wait_ge(q_ready.sem, q_ready.before(i + 1))
                eng.wait_ge(v_ready.sem, v_ready.before(i + 1))
                for s in range(LASTSLOT):
                    if s < NU:
                        c, t = divmod(s, ST)
                        if t == 0 and c < NK:
                            eng.wait_ge(kbd_pool.sem, kbd_pool.at(i, c + 1))
                            eng.wait_ge(kbd_vec.sem, kbd_vec.at(i, c + 1))
                        free = sub_ready if sign else s_read
                        if s >= 2:
                            eng.wait_ge(free.sem, free.at(i, s - 1))
                        else:
                            eng.wait_ge(free.sem, free.before(i))
                        kb = 0 if alibi else c % NB
                        for b in range(2):
                            last = eng.matmul(S[s % 2][SEQ * b:SEQ * (b + 1), :],
                                              qT[:, c, t * P + SEQ * b:t * P + SEQ * (b + 1)],
                                              Kbd[:, kb, 2 * t + b, :, :], start=True, stop=True)
                        last.then_inc(s_done.sem, 1)
                    if s % 4 == 2 and 2 + s // 4 < NK:
                        keys(2 + s // 4)
                    u = s - TR
                    if 0 <= u < NU:
                        eng.wait_ge(norm_ready.sem, norm_ready.at(i, u + 1))
                        if u >= 2:
                            eng.wait_ge(pt_ready.sem, pt_ready.at(i, u - 1))
                        else:
                            eng.wait_ge(pt_ready.sem, pt_ready.before(i))
                        for j in range(4):
                            last = eng.transpose(TP[u % 2][:, j * P:(j + 1) * P],
                                                 T[:, u % RING, 2 * j:2 * j + 2, :], ident[:, :])
                        last.then_inc(t_done.sem, 1)
                    u = s - TR - 1
                    if 0 <= u < NU:
                        c, t = divmod(u, ST)
                        eng.wait_ge(pt_ready.sem, pt_ready.at(i, u + 1))
                        if t == 0:
                            if c >= 2:
                                eng.wait_ge(ol_ready.sem, ol_ready.at(i, c - 1))
                            else:
                                eng.wait_ge(ol_ready.sem, ol_ready.before(i))
                        for b in range(2):
                            for j in range(4):
                                last = eng.matmul(
                                    OT[c % 2][32 * j:32 * j + 32, t * P + SEQ * b:t * P + SEQ * (b + 1)],
                                    Vbd[:, 2 * t + b, 2 * c + j // 2, :],
                                    PT[:, u % 2, j, SEQ * b:SEQ * (b + 1)], start=True, stop=True,
                                    tile_position=(0, 32 * j))
                        last.then_inc(pv_done.sem, 1)
                eng.wait_ge(oh_ready.sem, oh_ready.before(i + 1))
                eng.wait_ge(ol_ready.sem, ol_ready.before(i + 1))
                for t in range(ST):
                    b = bank()
                    products(eng, b[:, :], [((oh[:, c, t * P:(t + 1) * P], ol[:, c, t * P:(t + 1) * P]),
                                             pair(Wo, lambda w: w[:, c, :])) for c in range(KC)])\
                        .then_inc(y_done.sem, 1)
                assert n[0] == len(uses), (n[0], len(uses))


INTER = 1792
BLK = 32
QW = 448
NQ = INTER // QW
QB = QW // BLK
HK = QW // 4


def sparse_ffn(nc, signals, X, consts, a):
    NU = ST * NQ
    with ExitStack() as ctx:
        mem = Memory(ctx, nc, "ffn", signals)
        W1 = [mem.sb(f"w1_{n}", [P, KC, INTER], F32R) for n in range(2)]
        W2 = [mem.sb(f"w2_{n}", [HK, INTER // HK, D], F32R) for n in range(2)]
        C1 = [mem.sb(f"c1_{n}", [P, KC, 16], F32R) for n in range(2)]
        C2 = mem.sb("c2", [16, INTER])
        rank = mem.sb("block_rank", [P, BLK])
        ln = LayerNorm(mem, X, consts["ident"], consts["eps"])
        rT = mem.sb("rT", [16, STOK])
        bmax = mem.sb("block_max", [P, 2, QB])
        zmax = mem.sb("first_max", [P, 2, QB])
        E1 = mem.sb("one_hot", [P, 3, QB, BLK])
        HM = mem.sb("h_kept", [P, 2, QW])
        hh = mem.sb("hT_hi", [HK, 2, 4 * P], F32R)
        hl = mem.sb("hT_lo", [HK, 2, 4 * P], F32R)
        I = [mem.ps(f"I{n}") for n in range(2)]
        H = [mem.ps(f"H{n}") for n in range(2)]
        TP = [mem.ps(f"TP{n}") for n in range(2)]
        Y = [mem.ps(f"Y{n}") for n in range(2)]
        NP1, NP2 = KC, 4
        room = ln.xn[:, :, :].rearrange("p t d -> p (t d)")
        pieces = []
        for k in range(KC):
            pieces.append((a["w1T"][:, k, :], room[:, 0:INTER], [w[:, k, :] for w in W1]))
        for n in range(4):
            src = a["w2"][:, 4 * n:4 * n + 4, :].rearrange("p j d -> p (j d)")
            pieces.append((src, room[0:HK, 0:4 * D], [w[:, 4 * n:4 * n + 4, :].rearrange("p j d -> p (j d)") for w in W2]))
        c1room = E1[:, 0, :, :].rearrange("p b s -> p (b s)")[:, 0:KC * 16].rearrange("p (k n) -> p k n", k=KC)

        w_raw = mem.sig("weights_landed", 16 * (len(pieces) + 3), 1)
        w_hi = mem.sig("weights_hi", len(pieces) + 1, 1)
        w_lo = mem.sig("weights_lo", len(pieces) + 1, 1)
        r_done = mem.sig("r_product")
        r_ready = mem.sig("r_ready")
        i_done = mem.sig("rank_product", NU)
        h_done = mem.sig("h_product", NU)
        vec = mem.sig("vector_chain", 3 * NU)
        eq_ready = mem.sig("is_block_max", NU)
        z_ready = mem.sig("ranked", NU)
        h_ready = mem.sig("h_kept", NU)
        t_done = mem.sig("h_turned", NU)
        hh_ready = mem.sig("hT_hi_ready", NU)
        hl_ready = mem.sig("hT_lo_ready", NU)
        o_done = mem.sig("h_used", NU)
        y_added = mem.sig("y_added", ST)

        block = ctx.enter_context(nc.Block())

        @block.sync
        def _(eng):
            eng.dma_start(C2[:, :], a["c2T"]).then_inc(w_raw.sem, 16)
            eng.dma_start(rank[:, :], a["block_rank"].partition_broadcast(P)).then_inc(w_raw.sem, 16)
            eng.dma_start(c1room, a["c1T"]).then_inc(w_raw.sem, 16)
            for n, (src, dst, _) in enumerate(pieces):
                if n:
                    eng.wait_ge(w_lo.sem, w_lo.at(0, n + 1))
                eng.dma_start(dst, src).then_inc(w_raw.sem, 16)

        @block.scalar
        def _(eng):
            eng.wait_ge(w_raw.sem, w_raw.at(0, 64))
            eng.activation(C1[0][:, :, :], c1room, ACT.Copy).then_inc(w_hi.sem, 1)
            for n, (_, raw, (hi, _)) in enumerate(pieces):
                eng.wait_ge(w_raw.sem, w_raw.at(0, 48 + 16 * (n + 1)))
                eng.activation(hi, raw, ACT.Copy).then_inc(w_hi.sem, 1)
            with eng.Fori(0, NST) as i:
                ln.scalar_sd(eng, i)
                for t in range(ST):
                    ln.scalar_hi(eng, i, t, I[t % 2])
                eng.wait_ge(r_done.sem, r_done.at(i, 1))
                eng.activation(rT[:, :], H[0][0:16, :], ACT.Copy).then_inc(r_ready.sem, 1)
                for s in range(2, NU + 2):
                    u = s - 2
                    eng.wait_ge(t_done.sem, t_done.at(i, u + 1))
                    if u >= 2:
                        eng.wait_ge(o_done.sem, o_done.at(i, u - 1))
                    else:
                        eng.wait_ge(o_done.sem, o_done.before(i))
                    eng.activation(hh[:, u % 2, :], TP[u % 2][0:HK, :], ACT.Copy).then_inc(hh_ready.sem, 1)

        @block.gpsimd
        def _(eng):
            eng.wait_ge(w_hi.sem, w_hi.at(0, 1))
            eng.tensor_tensor(C1[1][:, :, :], c1room, C1[0][:, :, :].bitcast(F32), ALU.subtract)\
               .then_inc(w_lo.sem, 1)
            for n, (_, raw, (hi, lo)) in enumerate(pieces):
                eng.wait_ge(w_hi.sem, w_hi.at(0, n + 2))
                eng.tensor_tensor(lo, raw, hi.bitcast(F32), ALU.subtract).then_inc(w_lo.sem, 1)
            with eng.Fori(0, NST) as i:
                for u in range(NU):
                    eng.wait_ge(eq_ready.sem, eq_ready.at(i, u + 1))
                    e = E1[:, u % 3, :, :]
                    eng.tensor_tensor(e, e, rank[:, :].unsqueeze(1).to_broadcast([P, QB, BLK]), ALU.mult)\
                       .then_inc(z_ready.sem, 1)

        @block.vector
        def _(eng):
            eng.wait_ge(w_lo.sem, w_lo.at(0, len(pieces) + 1))
            with eng.Fori(0, NST) as i:
                ln.vector_norm(eng, i)
                for t in range(ST):
                    ln.vector_lo(eng, i, t, I[t % 2])
                links = [0]

                def chain(ins):
                    links[0] += 1
                    ins.then_inc(vec.sem, 1)
                    return links[0]

                for s in range(NU + 5):
                    if s < NU:
                        eng.wait_ge(i_done.sem, i_done.at(i, s + 1))
                        src = I[s % 2][:, 0:QW].rearrange("p (b s) -> p b s", s=BLK)
                        n = chain(eng.reduce_max(bmax[:, s % 2, :], src, AX_X))
                        eng.wait_ge(vec.sem, vec.at(i, n))
                        eng.tensor_tensor(E1[:, s % 3, :, :], src,
                                          bmax[:, s % 2, :].unsqueeze(2).to_broadcast([P, QB, BLK]),
                                          ALU.is_equal).then_inc(eq_ready.sem, 1)
                    u = s - 1
                    if 0 <= u < NU:
                        e = E1[:, u % 3, :, :]
                        eng.wait_ge(z_ready.sem, z_ready.at(i, u + 1))
                        n = chain(eng.reduce_max(zmax[:, u % 2, :], e, AX_X))
                        eng.wait_ge(vec.sem, vec.at(i, n))
                        n = chain(eng.tensor_tensor(e, e, zmax[:, u % 2, :].unsqueeze(2)
                                                    .to_broadcast([P, QB, BLK]), ALU.is_equal))
                        eng.wait_ge(h_done.sem, h_done.at(i, u + 1))
                        if u >= 2:
                            eng.wait_ge(t_done.sem, t_done.at(i, u - 1))
                        else:
                            eng.wait_ge(t_done.sem, t_done.before(i))
                        eng.wait_ge(vec.sem, vec.at(i, n))
                        eng.scalar_tensor_tensor(HM[:, u % 2, :], H[u % 2][:, 0:QW], 0.0,
                                                 e.rearrange("p b s -> p (b s)"), ALU.max, ALU.mult)\
                           .then_inc(h_ready.sem, 1)
                    u = s - 3
                    if 0 <= u < NU:
                        eng.wait_ge(hh_ready.sem, hh_ready.at(i, u + 1))
                        eng.tensor_tensor(hl[:, u % 2, :], TP[u % 2][0:HK, :], hh[:, u % 2, :].bitcast(F32),
                                          ALU.subtract).then_inc(hl_ready.sem, 1)
                    t = (s - 8) // NQ
                    if s - 8 == NQ * t and 0 <= t < ST - 1:
                        eng.wait_ge(o_done.sem, o_done.at(i, NQ * (t + 1)))
                        xt = x_tile(X, i, t)
                        eng.tensor_tensor(xt, xt, Y[t % 2][:, :], ALU.add).then_inc(y_added.sem, 1)
                eng.wait_ge(o_done.sem, o_done.before(i + 1))
                xt = x_tile(X, i, ST - 1)
                eng.tensor_tensor(xt, xt, Y[(ST - 1) % 2][:, :], ALU.add).then_inc(y_added.sem, 1)

        def second(eng, i, u):
            t, q = divmod(u, NQ)
            eng.wait_ge(hh_ready.sem, hh_ready.at(i, u + 1))
            eng.wait_ge(hl_ready.sem, hl_ready.at(i, u + 1))
            if q == 0:
                if t >= 2:
                    eng.wait_ge(y_added.sem, y_added.at(i, t - 1))
                else:
                    eng.wait_ge(y_added.sem, y_added.before(i))
            n = 0
            for j in range(4):
                h, l = hh[:, u % 2, j * P:(j + 1) * P], hl[:, u % 2, j * P:(j + 1) * P]
                w, v = W2[0][:, 4 * q + j, :], W2[1][:, 4 * q + j, :]
                for lhs, rhs in ((h, w), (h, v), (l, w)):
                    last = eng.matmul(Y[t % 2][:, :], lhs, rhs, start=(q == 0 and n == 0),
                                      stop=(q == NQ - 1 and n == 11))
                    n += 1
            last.then_inc(o_done.sem, 1)

        @block.tensor
        def _(eng):
            eng.wait_ge(w_hi.sem, w_hi.at(0, len(pieces) + 1))
            eng.wait_ge(w_lo.sem, w_lo.at(0, len(pieces) + 1))
            eng.wait_ge(w_raw.sem, w_raw.at(0, 16 * (len(pieces) + 3)))
            with eng.Fori(0, NST) as i:
                for t in range(ST):
                    if t >= 2:
                        eng.wait_ge(ln.lo_ready.sem, ln.lo_ready.at(i, t - 1))
                    else:
                        eng.wait_ge(eq_ready.sem, eq_ready.before(i))
                    ln.tensor_turn(eng, i, t, I[t % 2])
                eng.wait_ge(ln.lo_ready.sem, ln.lo_ready.before(i + 1))
                eng.wait_ge(ln.hi_ready.sem, ln.hi_ready.before(i + 1))
                eng.wait_ge(h_ready.sem, h_ready.before(i))
                products(eng, H[0][0:16, :], [((C1[0][:, k, :], C1[1][:, k, :]),
                                            (ln.hi[:, k, :], ln.lo[:, k, :])) for k in range(KC)])\
                    .then_inc(r_done.sem, 1)
                eng.wait_ge(r_ready.sem, r_ready.at(i, 1))
                for s in range(NU + 4):
                    if s < NU:
                        t, q = divmod(s, NQ)
                        if s >= 2:
                            eng.wait_ge(eq_ready.sem, eq_ready.at(i, s - 1))
                        eng.matmul(I[s % 2][:, 0:QW], rT[:, t * P:(t + 1) * P], C2[:, q * QW:(q + 1) * QW],
                                   start=True, stop=True).then_inc(i_done.sem, 1)
                        if s >= 2:
                            eng.wait_ge(h_ready.sem, h_ready.at(i, s - 1))
                        products(eng, H[s % 2][:, 0:QW],
                                 [((ln.hi[:, k, t * P:(t + 1) * P], ln.lo[:, k, t * P:(t + 1) * P]),
                                   tuple(w[:, k, q * QW:(q + 1) * QW] for w in W1)) for k in range(KC)])\
                            .then_inc(h_done.sem, 1)
                    u = s - 2
                    if 0 <= u < NU:
                        eng.wait_ge(h_ready.sem, h_ready.at(i, u + 1))
                        if u >= 2:
                            eng.wait_ge(hl_ready.sem, hl_ready.at(i, u - 1))
                        else:
                            eng.wait_ge(hl_ready.sem, hl_ready.before(i))
                        for j in range(4):
                            last = eng.transpose(TP[u % 2][0:HK, j * P:(j + 1) * P],
                                                 HM[:, u % 2, j * HK:(j + 1) * HK], consts["ident"][:, :])
                        last.then_inc(t_done.sem, 1)
                    u = s - 4
                    if 0 <= u < NU:
                        second(eng, i, u)


NE = 8
RANK = 16
GW = 4 * NE
CAPACITY = 3 * TOK // NE


def lora_experts(nc, signals, X, consts, a):
    EW = NE * RANK
    with ExitStack() as ctx:
        mem = Memory(ctx, nc, "moe", signals)
        ident, ones, eps = consts["ident"], consts["ones"], consts["eps"]
        W = [mem.sb(f"W{n}", [P, KC, D], F32R) for n in range(2)]
        WA = [mem.sb(f"WA{n}", [P, KC, EW + GW], F32R) for n in range(2)]
        WB = [mem.sb(f"WB{n}", [P, D], F32R) for n in range(2)]
        rW, rA, rB = mem.sb("rW", [P, KC, D]), mem.sb("rA", [P, KC, EW + GW]), mem.sb("rB", [P, D])
        params = mem.sb("gate_params", [P, 3, GW])
        gb2 = mem.sb("gate_bias2", [P, NE])
        gw2 = mem.sb("gate_w2", [GW, NE])
        rank8 = mem.sb("expert_rank", [P, NE])
        ln = LayerNorm(mem, X, ident, eps)
        tmp = mem.sb("tmp", [P, TILES * EW])
        hg = mem.sb("gate_h", [P, TILES * GW])
        sq = mem.sb("gate_sq", [P, TILES, GW])
        m1, var, sd = mem.sb("g_mean", [P, TILES]), mem.sb("g_var", [P, TILES]), mem.sb("g_sd", [P, TILES])
        hT = mem.sb("gate_hT", [GW, TILES, P])
        g = mem.sb("gates", [P, TILES, NE])
        g2 = mem.sb("gates2", [P, TILES, NE])
        z = mem.sb("gate_z", [P, TILES, NE])
        oh = mem.sb("gate_one_hot", [P, 2, TILES, NE])
        v1, v2, zm = mem.sb("g_v1", [P, TILES]), mem.sb("g_v2", [P, TILES]), mem.sb("g_zm", [P, TILES])
        e, p1, p2 = mem.sb("g_e", [P, TILES]), mem.sb("g_p1", [P, TILES]), mem.sb("g_p2", [P, TILES])
        cnt = mem.sb("counts", [P, 2, NE])
        allowed = mem.sb("allowed", [P, 2, NE])
        wt = mem.sb("expert_weight", [P, TILES * NE])
        tw = mem.sb("tmp_weighted", [P, ST * EW])
        th = mem.sb("tmpT_hi", [P, STOK], F32R)
        tl = mem.sb("tmpT_lo", [P, STOK], F32R)
        B = [mem.ps(f"B{n}") for n in range(8)]
        splits = [(rW, W), (rA, WA), (rB, WB)]
        w_raw = mem.sig("weights_landed", 16 * 9, 1)
        w_hi = mem.sig("weights_hi", 3, 1)
        w_lo = mem.sig("weights_lo", 3, 1)
        y_done = mem.sig("y_product", ST)
        a_done = mem.sig("a_product", ST)
        a_kept = mem.sig("a_kept", 2 * ST)
        y_added = mem.sig("y_added", ST)
        NCHAIN = 35
        gch = mem.sig("gate_chain", NCHAIN, 1)
        g_act = mem.sig("gate_scalar", 1 + 4 + 1, 1)
        g_pe = mem.sig("gate_pe", 4 + 1 + 1, 1)
        tw_ready = mem.sig("weighted")
        tt_done = mem.sig("weighted_turned")
        th_ready = mem.sig("weighted_hi")
        tl_ready = mem.sig("weighted_lo")
        z_done = mem.sig("lora_product", ST)
        z_added = mem.sig("lora_added", ST)

        block = ctx.enter_context(nc.Block())

        @block.sync
        def _(eng):
            for dst, src in ((rW[:, :, :], a["moe_W"]), (rA[:, :, :], a["moe_A"]), (rB[:, :], a["moe_B"]),
                             (params[:, 0, :], a["L1_ffn_gb1"].partition_broadcast(P)),
                             (params[:, 1, :], a["L1_ffn_ln_gamma"].partition_broadcast(P)),
                             (params[:, 2, :], a["L1_ffn_ln_beta"].partition_broadcast(P)),
                             (gb2[:, :], a["L1_ffn_gb2"].partition_broadcast(P)),
                             (gw2[:, :], a["moe_gw2"]),
                             (rank8[:, :], a["expert_rank"].partition_broadcast(P))):
                eng.dma_start(dst, src).then_inc(w_raw.sem, 16)

        @block.gpsimd
        def _(eng):
            for n, (raw, w) in enumerate(splits):
                full = (slice(None),) * len(raw.shape)
                eng.wait_ge(w_hi.sem, w_hi.at(0, n + 1))
                eng.tensor_tensor(w[1][full], raw[full], w[0][full].bitcast(F32), ALU.subtract)\
                   .then_inc(w_lo.sem, 1)

        @block.scalar
        def _(eng):
            eng.wait_ge(w_raw.sem, w_raw.at(0, 16 * 9))
            for raw, w in splits:
                full = (slice(None),) * len(raw.shape)
                eng.activation(w[0][full], raw[full], ACT.Copy).then_inc(w_hi.sem, 1)
            with eng.Fori(0, NST) as i:
                ln.scalar_sd(eng, i)
                for t in range(ST):
                    ln.scalar_hi(eng, i, t, B[t % 2])
            eng.wait_ge(gch.sem, gch.at(0, 6))
            eng.activation(sd[:, :], var[:, :], ACT.Sqrt, bias=eps[:, 0:1], scale=1.0 / GW)\
               .then_inc(g_act.sem, 1)
            for n in range(4):
                eng.wait_ge(g_pe.sem, g_pe.at(0, n + 1))
                eng.activation(hT[:, 4 * n:4 * n + 4, :], B[n][0:GW, :].rearrange("p (t n) -> p t n", t=4),
                               ACT.Copy).then_inc(g_act.sem, 1)
            eng.wait_ge(gch.sem, gch.at(0, 24))
            eng.activation(e[:, :], v2[:, :], ACT.Exp).then_inc(g_act.sem, 1)
            with eng.Fori(0, NST) as i:
                eng.wait_ge(tt_done.sem, tt_done.at(i, 1))
                eng.wait_ge(z_done.sem, z_done.before(i))
                eng.activation(th[:, :], B[0][:, :], ACT.Copy).then_inc(th_ready.sem, 1)

        @block.vector
        def _(eng):
            with eng.Fori(0, NST) as i:
                ln.vector_norm(eng, i)
                for t in range(ST):
                    ln.vector_lo(eng, i, t, B[t % 2])
                for t in range(ST):
                    eng.wait_ge(a_done.sem, a_done.at(i, t + 1))
                    src = B[4 + t % 2]
                    eng.tensor_scalar(tmp[:, bass.ds((i * ST + t) * EW, EW)], src[:, 0:EW], 1.0 / RANK, None,
                                      ALU.mult).then_inc(a_kept.sem, 1)
                    eng.tensor_scalar(hg[:, bass.ds((i * ST + t) * GW, GW)], src[:, EW:EW + GW], 1.0, None,
                                      ALU.mult).then_inc(a_kept.sem, 1)
                    eng.wait_ge(y_done.sem, y_done.at(i, t + 1))
                    xt = x_tile(X, i, t)
                    eng.tensor_tensor(xt, xt, B[2 + t % 2][:, :], ALU.add).then_inc(y_added.sem, 1)
            eng.wait_ge(a_kept.sem, a_kept.before(NST))
            count = [0]

            def step(ins):
                count[0] += 1
                ins.then_inc(gch.sem, 1)
                eng.wait_ge(gch.sem, gch.at(0, count[0]))

            h = hg[:, :].rearrange("p (t n) -> p t n", n=GW)

            def over(x, n):
                return x.unsqueeze(2).to_broadcast([P, TILES, n])

            def par(n):
                return params[:, n, :].unsqueeze(1).to_broadcast([P, TILES, GW])

            step(eng.tensor_tensor(h, h, par(0), ALU.add))
            step(eng.reduce_sum(m1[:, :], h, AX_X))
            step(eng.tensor_scalar(m1[:, :], m1[:, :], 1.0 / GW, None, ALU.mult))
            step(eng.tensor_tensor(h, h, over(m1[:, :], GW), ALU.subtract))
            step(eng.tensor_tensor(sq[:, :, :], h, h, ALU.mult))
            step(eng.reduce_sum(var[:, :], sq[:, :, :], AX_X))
            eng.wait_ge(g_act.sem, g_act.at(0, 1))
            step(eng.reciprocal(m1[:, :], sd[:, :]))
            step(eng.tensor_tensor(h, h, over(m1[:, :], GW), ALU.mult))
            step(eng.tensor_tensor(h, h, par(1), ALU.mult))
            step(eng.tensor_tensor(h, h, par(2), ALU.add))
            step(eng.tensor_scalar(h, h, 0.0, None, ALU.max))
            assert count[0] == 11
            eng.wait_ge(g_pe.sem, g_pe.at(0, 5))
            step(eng.tensor_tensor(g[:, :, :], B[4][:, 0:TILES * NE].rearrange("p (t n) -> p t n", n=NE),
                                   gb2[:, :].unsqueeze(1).to_broadcast([P, TILES, NE]), ALU.add))
            ranks = rank8[:, :].unsqueeze(1).to_broadcast([P, TILES, NE])
            for n, (src, best) in enumerate(((g, v1), (g2, v2))):
                if n:
                    step(eng.scalar_tensor_tensor(g2[:, :, :], oh[:, 0, :, :], -3.0e38, g[:, :, :],
                                                  ALU.mult, ALU.add))
                step(eng.reduce_max(best[:, :], src[:, :, :], AX_X))
                step(eng.tensor_tensor(z[:, :, :], src[:, :, :], over(best[:, :], NE), ALU.is_equal))
                step(eng.tensor_tensor(z[:, :, :], z[:, :, :], ranks, ALU.mult))
                step(eng.reduce_max(zm[:, :], z[:, :, :], AX_X))
                step(eng.tensor_tensor(oh[:, n, :, :], z[:, :, :], over(zm[:, :], NE), ALU.is_equal))
            step(eng.tensor_tensor(v2[:, :], v2[:, :], v1[:, :], ALU.subtract))
            assert count[0] == 24, count[0]
            for n in range(2):
                step(eng.reduce_sum(cnt[:, n, :], oh[:, n, :, :].rearrange("p t n -> p n t"), AX_X))
            eng.wait_ge(g_act.sem, g_act.at(0, 6))
            step(eng.tensor_scalar(p1[:, :], e[:, :], 1.0, None, ALU.add))
            step(eng.reciprocal(p1[:, :], p1[:, :]))
            step(eng.tensor_tensor(p2[:, :], e[:, :], p1[:, :], ALU.mult))
            eng.wait_ge(g_pe.sem, g_pe.at(0, 6))
            step(eng.tensor_scalar(allowed[:, :, :], B[5][:, 0:2 * NE].rearrange("p (k n) -> p k n", n=NE),
                                   float(CAPACITY), None, ALU.is_le))
            w3 = wt[:, :].rearrange("p (t n) -> p t n", n=NE)
            for n, p in enumerate((p1, p2)):
                step(eng.tensor_tensor(oh[:, n, :, :], oh[:, n, :, :],
                                       allowed[:, n, :].unsqueeze(1).to_broadcast([P, TILES, NE]), ALU.mult))
                step(eng.tensor_tensor(oh[:, n, :, :], oh[:, n, :, :], over(p[:, :], NE), ALU.mult))
            step(eng.tensor_tensor(w3, oh[:, 0, :, :], oh[:, 1, :, :], ALU.add))
            assert count[0] == NCHAIN, count[0]
            with eng.Fori(0, NST) as i:
                eng.wait_ge(tt_done.sem, tt_done.before(i))
                eng.tensor_tensor(tw[:, :].rearrange("p (n r) -> p n r", r=RANK),
                                  tmp[:, bass.ds(i * ST * EW, ST * EW)].rearrange("p (n r) -> p n r", r=RANK),
                                  wt[:, bass.ds(i * ST * NE, ST * NE)].unsqueeze(2)
                                  .to_broadcast([P, ST * NE, RANK]), ALU.mult).then_inc(tw_ready.sem, 1)
                eng.wait_ge(th_ready.sem, th_ready.at(i, 1))
                eng.tensor_tensor(tl[:, :], B[0][:, :], th[:, :].bitcast(F32), ALU.subtract)\
                   .then_inc(tl_ready.sem, 1)
                for t in range(ST):
                    eng.wait_ge(z_done.sem, z_done.at(i, t + 1))
                    xt = x_tile(X, i, t)
                    eng.tensor_tensor(xt, xt, B[4 + t][:, :], ALU.add).then_inc(z_added.sem, 1)

        @block.tensor
        def _(eng):
            eng.wait_ge(w_hi.sem, w_hi.at(0, 3))
            eng.wait_ge(w_lo.sem, w_lo.at(0, 3))
            with eng.Fori(0, NST) as i:
                for t in range(ST):
                    if t >= 2:
                        eng.wait_ge(ln.lo_ready.sem, ln.lo_ready.at(i, t - 1))
                    else:
                        eng.wait_ge(ln.lo_ready.sem, ln.lo_ready.before(i))
                    ln.tensor_turn(eng, i, t, B[t % 2])
                eng.wait_ge(ln.hi_ready.sem, ln.hi_ready.before(i + 1))
                eng.wait_ge(ln.lo_ready.sem, ln.lo_ready.before(i + 1))
                for t in range(ST):
                    def xt(k):
                        return ln.hi[:, k, t * P:(t + 1) * P], ln.lo[:, k, t * P:(t + 1) * P]
                    if t >= 2:
                        eng.wait_ge(y_added.sem, y_added.at(i, t - 1))
                        eng.wait_ge(a_kept.sem, a_kept.at(i, 2 * (t - 1)))
                    else:
                        eng.wait_ge(y_added.sem, y_added.before(i))
                        eng.wait_ge(a_kept.sem, a_kept.before(i))
                    products(eng, B[4 + t % 2][:, 0:EW + GW],
                             [(xt(k), (WA[0][:, k, :], WA[1][:, k, :])) for k in range(KC)])\
                        .then_inc(a_done.sem, 1)
                    products(eng, B[2 + t % 2][:, :],
                             [(xt(k), (W[0][:, k, :], W[1][:, k, :])) for k in range(KC)])\
                        .then_inc(y_done.sem, 1)
            eng.wait_ge(gch.sem, gch.at(0, 11))
            eng.wait_ge(y_added.sem, y_added.before(NST))
            for n in range(4):
                for t in range(4):
                    at = (4 * n + t) * GW
                    last = eng.transpose(B[n][0:GW, t * P:(t + 1) * P], hg[:, at:at + GW], ident[:, :])
                last.then_inc(g_pe.sem, 1)
            eng.wait_ge(g_act.sem, g_act.at(0, 5))
            eng.wait_ge(w_raw.sem, w_raw.at(0, 16 * 9))
            for t in range(TILES):
                last = eng.matmul(B[4][:, t * NE:(t + 1) * NE], hT[:, t, :], gw2[:, :], start=True, stop=True)
            last.then_inc(g_pe.sem, 1)
            eng.wait_ge(gch.sem, gch.at(0, 26))
            eng.matmul(B[5][:, 0:2 * NE], ones[:, :], cnt[:, :, :].rearrange("p k n -> p (k n)"),
                       start=True, stop=True).then_inc(g_pe.sem, 1)
            with eng.Fori(0, NST) as i:
                eng.wait_ge(tw_ready.sem, tw_ready.at(i, 1))
                eng.wait_ge(tl_ready.sem, tl_ready.before(i))
                for t in range(ST):
                    last = eng.transpose(B[0][:, t * P:(t + 1) * P], tw[:, t * EW:(t + 1) * EW], ident[:, :])
                last.then_inc(tt_done.sem, 1)
                eng.wait_ge(th_ready.sem, th_ready.at(i, 1))
                eng.wait_ge(tl_ready.sem, tl_ready.at(i, 1))
                eng.wait_ge(z_added.sem, z_added.before(i))
                for t in range(ST):
                    products(eng, B[4 + t][:, :], [((th[:, t * P:(t + 1) * P], tl[:, t * P:(t + 1) * P]),
                                                    (WB[0][:, :], WB[1][:, :]))]).then_inc(z_done.sem, 1)


NG = 8
NH = 4
HALF = 2 * STOK
NHALF = TOK // HALF
RMS_EPS = 1e-5


def cross_attention(nc, signals, X, consts, a):
    ident, eps, ones = consts["ident"], consts["eps"], consts["ones"]
    NU = 2
    ROWS = 2 * NH
    PASSES = NHALF * NG
    with ExitStack() as ctx:
        mem = Memory(ctx, nc, "xat", signals)
        Wq = [mem.sb(f"Wq{n}", [P, KC, D], F32R) for n in range(2)]
        Wk = [mem.sb(f"Wk{n}", [P, KC, P], F32R) for n in range(2)]
        Wv = [mem.sb(f"Wv{n}", [P, KC, P], F32R) for n in range(2)]
        Wo = [mem.sb(f"Wo{n}", [P, NH, D], F32R) for n in range(2)]
        room = mem.sb("weights_raw", [P, KC * (D + 2 * P)])
        ch = mem.sb("ctxT_hi", [P, KC, HALF], F32R)
        cl = mem.sb("ctxT_lo", [P, KC, HALF], F32R)
        qT = mem.sb("qT", [P, NH, STOK])
        kT = mem.sb("kT", [P, STOK])
        krms = mem.sb("k_rms", [P, STOK])
        sq = mem.sb("squares", [P, 2, STOK])
        turn = mem.sb("vT_and_PT", [P, 2, STOK])
        V = mem.sb("V", [P, 2, SB, P])
        T = mem.sb("T", [P, 2 * NU, ROWS, SEQ])
        oh = mem.sb("oT_hi", [P, NH, STOK], F32R)
        ol = mem.sb("oT_lo", [P, NH, STOK], F32R)
        qrms = mem.sb("q_rms", [NH, STOK])
        rq = mem.sb("q_inv_rms", [P, 2, ST, NH])
        mx = mem.sb("row_max", [P, 2, ROWS])
        rs = mem.sb("row_sum", [P, 2, ROWS])
        ri = mem.sb("row_inv", [P, 2 * NU, ROWS])
        mask = mem.sb("mask", [P, SEQ])
        norms = mem.sb("norm_weights", [P, 3])
        sel = mem.sb("head_select", [P, NH, NH])
        ln = LayerNorm(mem, X, ident, eps, width=HALF, passes=2 * NHALF,
                       xn=T[:, :, :, :].rearrange("p u r s -> p (u r s)").rearrange("p (t d) -> p t d", d=D))
        craw = qT
        vT = turn[:, :, :].rearrange("p a n -> p (a n)").rearrange("p (b c s) -> p b c s", c=2, s=SEQ)
        PT = turn[:, :, :].rearrange("p u (j n) -> p u j n", j=4)
        G = [mem.ps(f"G{n}") for n in range(2)]
        S = [mem.ps(f"S{n}") for n in range(2)]
        TP = [mem.ps(f"TP{n}") for n in range(2)]
        OT = [mem.ps(f"OT{n}") for n in range(2)]
        O = [OT, G]

        raw_o = room[:, 0:NH * D].rearrange("p (k n) -> p k n", k=NH)
        raw_q = room[:, 0:KC * D].rearrange("p (k n) -> p k n", k=KC)
        raw_k = room[:, KC * D:KC * (D + P)].rearrange("p (k n) -> p k n", k=KC)
        raw_v = room[:, KC * (D + P):].rearrange("p (k n) -> p k n", k=KC)
        kvq = [(raw_k, Wk), (raw_v, Wv), (raw_q, Wq)]

        pre_dma = mem.sig("weights_landed", 16 * 7, 1)
        pre_hi = mem.sig("weights_hi", 3, 1)
        pre_lo = mem.sig("weights_lo", 3, 1)
        pre = mem.sig("prologue_vector", 2, 1)

        def sig(name, per):
            return mem.sig(name, per, PASSES)

        ctx_landed = mem.sig("ctx_landed", 16, 2 * NHALF)
        ctx_hi = mem.sig("ctx_hi_ready", 1, 2 * NHALF)
        ctx_lo = mem.sig("ctx_lo_ready", 1, 2 * NHALF)
        wo_landed, wqkv_landed = sig("wo_landed", 16), sig("wqkv_landed", 48)
        wo_hi, wo_lo = sig("wo_hi", 1), sig("wo_lo", 1)
        wqkv_hi, wqkv_lo = sig("wqkv_hi", 3), sig("wqkv_lo", 3)
        k_done, v_done, q_done = sig("k_product", 2), sig("v_product", 2), sig("q_product", 2 * NH)
        ms_done = sig("sums_of_squares", 2 * (1 + NH))
        vt_done, rqt_done = sig("v_turned", 2), sig("q_rms_turned", 2)
        kr_ready, vt_ready, q_ready = sig("k_raw_ready", 2), sig("vT_ready", 2), sig("q_ready", 2 * NH)
        sq_ready = sig("squares_ready", 2 * (1 + NH))
        krms_ready, qrms_ready = sig("k_rms_ready", 2), sig("q_rms_ready", 2)
        kn_ready, rqT_ready, rq_ready = sig("k_ready", 2), sig("q_inv_rms_row", 2), sig("q_inv_rms", 2)
        va_ready, vb_ready = sig("V_by_scalar", 2), sig("V_by_vector", 2)
        U = 2 * NU
        s_done, s_read, biased = sig("scores", U), sig("scores_read", U), sig("biased", U)
        sub_ready, exp_ready = sig("shifted", U), sig("exponentials", U)
        inv_ready, norm_ready = sig("inverse_sums", U), sig("probabilities", U)
        t_done, pt_ready, pv_done = sig("probs_turned", U), sig("PT_ready", U), sig("values_product", U)
        oh_ready, ol_ready = sig("oT_hi_ready", U), sig("oT_lo_ready", U)
        y_done, y_added = sig("y_product", 2 * ST), sig("y_added", 2 * ST)
        vec = sig("vector_chain", 2 + 2 * U)

        def load_kvq(eng, g, done):
            for dst, src in ((raw_k, a["Cq_k"]), (raw_v, a["Cq_v"]), (raw_q, a["Cq_q"])):
                n = dst.shape[1] * dst.shape[2]
                eng.dma_start(dst.rearrange("p k n -> p (k n)"), src[:, bass.ds(g * n, n)]).then_inc(done.sem, 16)

        def o_part(x, n, r):
            u = n % 2
            return x[:, r:NH:2, u * 2 * P:(u + 1) * 2 * P]

        def o_bank(n, r):
            return O[n % 2][r][:, :].rearrange("p (h n) -> p h n", h=2)

        block = ctx.enter_context(nc.Block())

        @block.sync
        def _(eng):
            load_kvq(eng, 0, pre_dma)
            for dst, src in ((norms[:, 0:2], a["C_norms"]), (sel[:, :, :].rearrange("p h k -> p (h k)"),
                                                             a["C_select"].partition_broadcast(P)),
                             (mask[0:SEQ, :], a["C_mask"]), (mask[SEQ:P, :], a["C_mask"])):
                eng.dma_start(dst, src).then_inc(pre_dma.sem, 16)
            eng.wait_ge(pre_lo.sem, pre_lo.at(0, 3))
            with eng.Fori(0, NHALF) as hf:
                for st in range(2):
                    i = hf * 2 + st
                    if st == 0:
                        eng.wait_ge(s_done.sem, s_done.before(hf * NG))
                    else:
                        eng.wait_ge(ctx_lo.sem, ctx_lo.before(i))
                    eng.dma_start(craw[:, :, :], a["ctxT"][:, :, bass.ds(i * STOK, STOK)])\
                       .then_inc(ctx_landed.sem, 16)
                with eng.Fori(0, NG) as g:
                    j = hf * NG + g
                    eng.wait_ge(wqkv_lo.sem, wqkv_lo.before(j))
                    eng.dma_start(raw_o.rearrange("p k n -> p (k n)"), a["Cq_o"][:, bass.ds(g * NH * D, NH * D)])\
                       .then_inc(wo_landed.sem, 16)
                    eng.wait_ge(wo_lo.sem, wo_lo.at(j, 1))
                    load_kvq(eng, g + 1, wqkv_landed)

        @block.scalar
        def _(eng):
            eng.wait_ge(pre_dma.sem, pre_dma.at(0, 16 * 7))
            for raw, w in kvq:
                eng.activation(w[0][:, :, :], raw, ACT.Copy).then_inc(pre_hi.sem, 1)
            with eng.Fori(0, NHALF) as hf:
                for st in range(2):
                    i = hf * 2 + st
                    ln.off = st * STOK
                    eng.wait_ge(ctx_landed.sem, ctx_landed.at(i, 16))
                    eng.activation(ch[:, :, st * STOK:(st + 1) * STOK], craw[:, :, :], ACT.Copy)\
                       .then_inc(ctx_hi.sem, 1)
                    ln.scalar_sd(eng, i)
                    for t in range(ST):
                        ln.scalar_hi(eng, i, t, S[t % 2])
                with eng.Fori(0, NG) as g:
                    j = hf * NG + g

                    def square(st, n, src):
                        m = st * (1 + NH) + n
                        eng.wait_ge(ms_done.sem, ms_done.at(j, m - 1) if m >= 2 else ms_done.before(j))
                        eng.activation(sq[:, m % 2, :], src, ACT.Square).then_inc(sq_ready.sem, 1)

                    def project(st):
                        eng.wait_ge(k_done.sem, k_done.at(j, st + 1))
                        eng.activation(kT[:, :], G[0][:, :], ACT.Copy).then_inc(kr_ready.sem, 1)
                        square(st, 0, G[0][:, :])
                        eng.wait_ge(v_done.sem, v_done.at(j, st + 1))
                        src = G[1][:, :].rearrange("p (b s) -> p b s", s=SEQ)
                        eng.activation(vT[:, :, 0, :], src, ACT.Copy)
                        eng.activation(vT[:, :, 1, :], src, ACT.Copy).then_inc(vt_ready.sem, 1)
                        for h in range(NH):
                            bank = G[h % 2]
                            eng.wait_ge(q_done.sem, q_done.at(j, st * NH + h + 1))
                            eng.activation(qT[:, h, :], bank[:, :], ACT.Copy).then_inc(q_ready.sem, 1)
                            square(st, h + 1, bank[:, :])
                            if h == 0:
                                eng.wait_ge(ms_done.sem, ms_done.at(j, st * (1 + NH) + 1))
                                eng.activation(krms[:, :], OT[0][:, :], ACT.Sqrt, bias=eps[:, 0:1],
                                               scale=1.0 / P).then_inc(krms_ready.sem, 1)
                            if h == 1:
                                eng.wait_ge(vt_done.sem, vt_done.at(j, st + 1))
                                eng.activation(V[:, st, 0:4, :], TP[0][:, :].rearrange("p (b d) -> p b d", d=P),
                                               ACT.Copy).then_inc(va_ready.sem, 1)
                        eng.wait_ge(ms_done.sem, ms_done.at(j, (st + 1) * (1 + NH)))
                        eng.activation(qrms[:, :], OT[1][0:NH, :], ACT.Sqrt, bias=eps[0:NH, 0:1],
                                       scale=1.0 / P).then_inc(qrms_ready.sem, 1)

                    def exponent(n):
                        eng.wait_ge(sub_ready.sem, sub_ready.at(j, n + 1))
                        eng.activation(T[:, n, :, :], T[:, n, :, :], ACT.Exp).then_inc(exp_ready.sem, 1)

                    def keep_PT(n):
                        eng.wait_ge(t_done.sem, t_done.at(j, n + 1))
                        eng.activation(PT[:, n % 2, :, :], TP[n % 2][:, :].rearrange("p (c n) -> p c n", c=4),
                                       ACT.Copy).then_inc(pt_ready.sem, 1)

                    def keep_oT(n):
                        eng.wait_ge(pv_done.sem, pv_done.at(j, n + 1))
                        for r in range(2):
                            last = eng.activation(o_part(oh, n, r), o_bank(n, r), ACT.Copy)
                        last.then_inc(oh_ready.sem, 1)

                    project(0)
                    exponent(0)
                    exponent(1)
                    eng.wait_ge(wo_landed.sem, wo_landed.at(j, 16))
                    eng.wait_ge(y_done.sem, y_done.before(j))
                    eng.activation(Wo[0][:, :, :], raw_o, ACT.Copy).then_inc(wo_hi.sem, 1)
                    project(1)
                    keep_PT(0)
                    keep_PT(1)
                    keep_oT(0)
                    exponent(2)
                    keep_oT(1)
                    exponent(3)
                    eng.wait_ge(wqkv_landed.sem, wqkv_landed.at(j, 48))
                    eng.wait_ge(q_done.sem, q_done.at(j, 2 * NH))
                    for raw, w in kvq:
                        eng.activation(w[0][:, :, :], raw, ACT.Copy).then_inc(wqkv_hi.sem, 1)
                    keep_PT(2)
                    keep_PT(3)
                    keep_oT(2)
                    keep_oT(3)

        @block.gpsimd
        def _(eng):
            for n, (raw, w) in enumerate(kvq):
                eng.wait_ge(pre_hi.sem, pre_hi.at(0, n + 1))
                eng.tensor_tensor(w[1][:, :, :], raw, w[0][:, :, :].bitcast(F32), ALU.subtract)\
                   .then_inc(pre_lo.sem, 1)
            with eng.Fori(0, NHALF) as hf:
                for st in range(2):
                    i = hf * 2 + st
                    at = slice(st * STOK, (st + 1) * STOK)
                    eng.wait_ge(ctx_hi.sem, ctx_hi.at(i, 1))
                    eng.tensor_tensor(cl[:, :, at], craw[:, :, :], ch[:, :, at].bitcast(F32), ALU.subtract)\
                       .then_inc(ctx_lo.sem, 1)
                with eng.Fori(0, NG) as g:
                    j = hf * NG + g

                    def bias(n):
                        eng.wait_ge(s_read.sem, s_read.at(j, n + 1))
                        eng.tensor_tensor(T[:, n, :, :], T[:, n, :, :],
                                          mask[:, :].unsqueeze(1).to_broadcast([P, ROWS, SEQ]), ALU.add)\
                           .then_inc(biased.sem, 1)

                    def normalize(n):
                        eng.wait_ge(inv_ready.sem, inv_ready.at(j, n + 1))
                        eng.tensor_tensor(T[:, n, :, :], T[:, n, :, :],
                                          ri[:, n, :].unsqueeze(2).to_broadcast([P, ROWS, SEQ]), ALU.mult)\
                           .then_inc(norm_ready.sem, 1)

                    def low(n):
                        raw, w = kvq[n]
                        eng.wait_ge(wqkv_hi.sem, wqkv_hi.at(j, n + 1))
                        eng.tensor_tensor(w[1][:, :, :], raw, w[0][:, :, :].bitcast(F32), ALU.subtract)\
                           .then_inc(wqkv_lo.sem, 1)

                    bias(0)
                    bias(1)
                    eng.wait_ge(wo_hi.sem, wo_hi.at(j, 1))
                    eng.tensor_tensor(Wo[1][:, :, :], raw_o, Wo[0][:, :, :].bitcast(F32), ALU.subtract)\
                       .then_inc(wo_lo.sem, 1)
                    normalize(0)
                    normalize(1)
                    bias(2)
                    bias(3)
                    low(0)
                    low(1)
                    normalize(2)
                    normalize(3)
                    low(2)

        @block.vector
        def _(eng):
            eng.wait_ge(pre_dma.sem, pre_dma.at(0, 16 * 7))
            eng.tensor_tensor(norms[:, 2:3], norms[:, 0:1], norms[:, 1:2], ALU.mult).then_inc(pre.sem, 1)
            eng.wait_ge(pre.sem, pre.at(0, 1))
            eng.tensor_scalar(norms[:, 2:3], norms[:, 2:3], float(P) ** -0.5, None, ALU.mult)\
               .then_inc(pre.sem, 1)
            eng.wait_ge(pre.sem, pre.at(0, 2))
            with eng.Fori(0, NHALF) as hf:
                for st in range(2):
                    ln.off = st * STOK
                    if st == 0:
                        eng.wait_ge(t_done.sem, t_done.before(hf * NG))
                    ln.vector_norm(eng, hf * 2 + st)
                    for t in range(ST):
                        ln.vector_lo(eng, hf * 2 + st, t, S[t % 2])
                with eng.Fori(0, NG) as g:
                    j = hf * NG + g
                    links = [0]

                    def chain(ins):
                        links[0] += 1
                        ins.then_inc(vec.sem, 1)
                        eng.wait_ge(vec.sem, vec.at(j, links[0]))

                    def project(st):
                        eng.wait_ge(krms_ready.sem, krms_ready.at(j, st + 1))
                        eng.wait_ge(kr_ready.sem, kr_ready.at(j, st + 1))
                        chain(eng.reciprocal(krms[:, :], krms[:, :]))
                        eng.scalar_tensor_tensor(kT[:, :], kT[:, :], norms[:, 2:3], krms[:, :],
                                                 ALU.mult, ALU.mult).then_inc(kn_ready.sem, 1)
                        eng.wait_ge(vt_done.sem, vt_done.at(j, st + 1))
                        eng.tensor_copy(V[:, st, 4:8, :], TP[1][:, :].rearrange("p (b d) -> p b d", d=P))\
                           .then_inc(vb_ready.sem, 1)
                        eng.wait_ge(qrms_ready.sem, qrms_ready.at(j, st + 1))
                        eng.reciprocal(qrms[:, :], qrms[:, :]).then_inc(rqT_ready.sem, 1)
                        eng.wait_ge(rqt_done.sem, rqt_done.at(j, st + 1))
                        eng.tensor_copy(rq[:, st, :, :], OT[0][:, 0:ST * NH].rearrange("p (t h) -> p t h", h=NH))\
                           .then_inc(rq_ready.sem, 1)

                    def take_scores(n):
                        st, u = divmod(n, NU)
                        eng.wait_ge(s_done.sem, s_done.at(j, n + 1))
                        eng.wait_ge(rq_ready.sem, rq_ready.at(j, st + 1))
                        scale = rq[:, st, 2 * u:2 * u + 2, :].rearrange("p t h -> p (t h)")
                        eng.tensor_tensor(T[:, n, :, :], S[u][:, :].rearrange("p (r s) -> p r s", s=SEQ),
                                          scale.unsqueeze(2).to_broadcast([P, ROWS, SEQ]), ALU.mult)\
                           .then_inc(s_read.sem, 1)

                    def shift(n):
                        eng.wait_ge(biased.sem, biased.at(j, n + 1))
                        chain(eng.reduce_max(mx[:, n % 2, :], T[:, n, :, :], AX_X))
                        eng.tensor_tensor(T[:, n, :, :], T[:, n, :, :],
                                          mx[:, n % 2, :].unsqueeze(2).to_broadcast([P, ROWS, SEQ]),
                                          ALU.subtract).then_inc(sub_ready.sem, 1)

                    def invert(n):
                        eng.wait_ge(exp_ready.sem, exp_ready.at(j, n + 1))
                        chain(eng.reduce_sum(rs[:, n % 2, :], T[:, n, :, :], AX_X))
                        eng.reciprocal(ri[:, n, :], rs[:, n % 2, :]).then_inc(inv_ready.sem, 1)

                    def low_oT(n):
                        eng.wait_ge(oh_ready.sem, oh_ready.at(j, n + 1))
                        for r in range(2):
                            last = eng.tensor_tensor(o_part(ol, n, r), o_bank(n, r), o_part(oh, n, r).bitcast(F32),
                                                     ALU.subtract)
                        last.then_inc(ol_ready.sem, 1)

                    def add_y(st):
                        for t in range(ST):
                            eng.wait_ge(y_done.sem, y_done.at(j, st * ST + t + 1))
                            xt = x_tile(X, hf * 2 + st, t)
                            if st == 0 and t == 0:
                                eng.wait_ge(y_added.sem, y_added.before(j))
                            eng.tensor_tensor(xt, xt, TP[t % 2][:, :], ALU.add).then_inc(y_added.sem, 1)

                    project(0)
                    take_scores(0)
                    take_scores(1)
                    shift(0)
                    shift(1)
                    invert(0)
                    invert(1)
                    project(1)
                    take_scores(2)
                    take_scores(3)
                    shift(2)
                    low_oT(0)
                    shift(3)
                    low_oT(1)
                    invert(2)
                    invert(3)
                    add_y(0)
                    low_oT(2)
                    low_oT(3)
                    add_y(1)
                    assert links[0] == vec.per, links[0]

        @block.tensor
        def _(eng):
            eng.wait_ge(pre_dma.sem, pre_dma.at(0, 16 * 7))
            eng.wait_ge(pre_lo.sem, pre_lo.at(0, 3))
            with eng.Fori(0, NHALF) as hf:
                for st in range(2):
                    i = hf * 2 + st
                    for t in range(ST):
                        if t >= 2:
                            eng.wait_ge(ln.lo_ready.sem, ln.lo_ready.at(i, t - 1))
                        else:
                            eng.wait_ge(ln.lo_ready.sem, ln.lo_ready.before(i))
                            eng.wait_ge(s_read.sem, s_read.before(hf * NG))
                        ln.tensor_turn(eng, i, t, S[t % 2])
                with eng.Fori(0, NG) as g:
                    j = hf * NG + g

                    def x_part(st, k):
                        at = slice(st * STOK, (st + 1) * STOK)
                        return ln.hi[:, k, at], ln.lo[:, k, at]

                    def c_part(st, k):
                        at = slice(st * STOK, (st + 1) * STOK)
                        return ch[:, k, at], cl[:, k, at]

                    def project(st):
                        if st == 0:
                            eng.wait_ge(ln.hi_ready.sem, ln.hi_ready.before(hf * 2 + 2))
                            eng.wait_ge(ln.lo_ready.sem, ln.lo_ready.before(hf * 2 + 2))
                            eng.wait_ge(ctx_lo.sem, ctx_lo.before(hf * 2 + 2))
                            eng.wait_ge(wqkv_lo.sem, wqkv_lo.before(j))
                            eng.wait_ge(ol_ready.sem, ol_ready.before(j))
                            eng.wait_ge(y_added.sem, y_added.before(j))
                        else:
                            eng.wait_ge(sq_ready.sem, sq_ready.at(j, 1 + NH))
                            eng.wait_ge(q_ready.sem, q_ready.at(j, NH))
                        products(eng, G[0][:, :], [((Wk[0][:, k, :], Wk[1][:, k, :]), c_part(st, k))
                                                   for k in range(KC)]).then_inc(k_done.sem, 1)
                        products(eng, G[1][:, :], [((Wv[0][:, k, :], Wv[1][:, k, :]), c_part(st, k))
                                                   for k in range(KC)]).then_inc(v_done.sem, 1)

                        def head(h):
                            m = st * (1 + NH) + h
                            if h == 0:
                                eng.wait_ge(kr_ready.sem, kr_ready.at(j, st + 1))
                                eng.wait_ge(sq_ready.sem, sq_ready.at(j, m + 1))
                            elif h == 1:
                                eng.wait_ge(vt_ready.sem, vt_ready.at(j, st + 1))
                            else:
                                eng.wait_ge(q_ready.sem, q_ready.at(j, st * NH + h - 1))
                                eng.wait_ge(sq_ready.sem, sq_ready.at(j, m))
                            products(eng, G[h % 2][:, :],
                                     [(tuple(w[:, k, h * P:(h + 1) * P] for w in Wq), x_part(st, k))
                                      for k in range(KC)]).then_inc(q_done.sem, 1)

                        def q_squares(h):
                            eng.wait_ge(sq_ready.sem, sq_ready.at(j, st * (1 + NH) + h + 2))
                            if h == 0:
                                eng.wait_ge(qrms_ready.sem, qrms_ready.at(j, st))
                            eng.matmul(OT[1][0:NH, :], sel[:, h, :], sq[:, (st * (1 + NH) + h + 1) % 2, :],
                                       start=(h == 0), stop=(h == NH - 1)).then_inc(ms_done.sem, 1)

                        head(0)
                        eng.wait_ge(sq_ready.sem, sq_ready.at(j, st * (1 + NH) + 1))
                        eng.wait_ge(rq_ready.sem, rq_ready.at(j, st))
                        eng.matmul(OT[0][:, :], ones[:, :], sq[:, (st * (1 + NH)) % 2, :], start=True, stop=True)\
                           .then_inc(ms_done.sem, 1)
                        head(1)
                        q_squares(0)
                        eng.wait_ge(va_ready.sem, va_ready.at(j, st))
                        eng.wait_ge(vb_ready.sem, vb_ready.at(j, st))
                        for b in range(SB):
                            last = eng.transpose(TP[b // 4][:, (b % 4) * P:(b % 4 + 1) * P],
                                                 vT[:, b, :, :].rearrange("p c s -> p (c s)"), ident[:, :])
                        last.then_inc(vt_done.sem, 1)
                        head(2)
                        q_squares(1)
                        head(3)
                        q_squares(2)
                        q_squares(3)
                        eng.wait_ge(krms_ready.sem, krms_ready.at(j, st + 1))
                        eng.wait_ge(rqT_ready.sem, rqT_ready.at(j, st + 1))
                        for t in range(ST):
                            last = eng.matmul(OT[0][:, t * NH:(t + 1) * NH], qrms[:, t * P:(t + 1) * P],
                                              ident[0:NH, 0:NH], start=True, stop=True)
                        last.then_inc(rqt_done.sem, 1)

                    def scores(st):
                        eng.wait_ge(q_ready.sem, q_ready.at(j, (st + 1) * NH))
                        eng.wait_ge(kn_ready.sem, kn_ready.at(j, st + 1))
                        for u in range(NU):
                            n = st * NU + u
                            eng.wait_ge(s_read.sem, s_read.at(j, n - 1) if n >= 2 else s_read.before(j))
                            for t in range(2):
                                for h in range(NH):
                                    for b in range(2):
                                        tok = (2 * u + t) * P + b * SEQ
                                        at = (t * NH + h) * SEQ
                                        last = eng.matmul(S[u][b * SEQ:(b + 1) * SEQ, at:at + SEQ],
                                                          qT[:, h, tok:tok + SEQ], kT[:, tok:tok + SEQ],
                                                          start=True, stop=True)
                            last.then_inc(s_done.sem, 1)

                    def values(st):
                        for u in range(NU):
                            n = st * NU + u
                            eng.wait_ge(norm_ready.sem, norm_ready.at(j, n + 1))
                            if st == 0:
                                eng.wait_ge(va_ready.sem, va_ready.at(j, 2))
                                eng.wait_ge(vb_ready.sem, vb_ready.at(j, 2))
                            else:
                                eng.wait_ge(y_added.sem, y_added.at(j, ST))
                            for c in range(4):
                                last = eng.transpose(TP[u][:, c * P:(c + 1) * P],
                                                     T[:, n, 2 * c:2 * c + 2, :].rearrange("p r s -> p (r s)"),
                                                     ident[:, :])
                            last.then_inc(t_done.sem, 1)
                        for u in range(NU):
                            n = st * NU + u
                            eng.wait_ge(pt_ready.sem, pt_ready.at(j, n + 1))
                            if st == 0:
                                eng.wait_ge(q_ready.sem, q_ready.at(j, 2 * NH))
                                eng.wait_ge(sq_ready.sem, sq_ready.at(j, 2 * (1 + NH)))
                                eng.wait_ge(rq_ready.sem, rq_ready.at(j, 2))
                                eng.wait_ge(qrms_ready.sem, qrms_ready.at(j, 2))
                            else:
                                eng.wait_ge(ol_ready.sem, ol_ready.at(j, n - 1))
                            for t in range(2):
                                for b in range(2):
                                    seq = (2 * u + t) * 2 + b
                                    at = t * P + b * SEQ
                                    for r in range(2):
                                        rows = slice(r * SEQ, (r + 1) * SEQ)
                                        last = eng.matmul(
                                            o_bank(n, r)[:, :, at:at + SEQ], V[rows, st, seq, :],
                                            PT[rows, u, 2 * t:2 * t + 2, b * SEQ:(b + 1) * SEQ],
                                            start=True, stop=True)
                            last.then_inc(pv_done.sem, 1)

                    def output(st):
                        if st == 0:
                            eng.wait_ge(wo_lo.sem, wo_lo.at(j, 1))
                        for t in range(ST):
                            n = st * NU + t // 2
                            eng.wait_ge(oh_ready.sem, oh_ready.at(j, n + 1))
                            eng.wait_ge(ol_ready.sem, ol_ready.at(j, n + 1))
                            m = st * ST + t
                            if t < 2:
                                eng.wait_ge(pt_ready.sem, pt_ready.at(j, st * NU + t + 1))
                            else:
                                eng.wait_ge(y_added.sem, y_added.at(j, m - 1))
                            products(eng, TP[t % 2][:, :],
                                     [((oh[:, h, t * P:(t + 1) * P], ol[:, h, t * P:(t + 1) * P]),
                                       (Wo[0][:, h, :], Wo[1][:, h, :])) for h in range(NH)])\
                                .then_inc(y_done.sem, 1)

                    project(0)
                    scores(0)
                    project(1)
                    scores(1)
                    values(0)
                    output(0)
                    values(1)
                    output(1)


def more_arrays(v):
    c1 = v["L0_ffn_c1_w"].T
    lora = v["L1_ffn_lora_A"].transpose(1, 0, 2).reshape(D, NE * RANK)
    wq = v["L0_xattn_Wq"].reshape(NG, NH * P, D)
    wk, wv = v["L0_xattn_Wk"].reshape(NG, P, D), v["L0_xattn_Wv"].reshape(NG, P, D)
    wo = v["L0_xattn_Wo"].T.reshape(NG, NH * P, D)
    order = list(range(NG)) + [0]
    return {
        "Cq_q": np.concatenate([lay(wq[g].T).reshape(P, -1) for g in order], axis=1),
        "Cq_k": np.concatenate([lay(wk[g].T).reshape(P, -1) for g in order], axis=1),
        "Cq_v": np.concatenate([lay(wv[g].T).reshape(P, -1) for g in order], axis=1),
        "Cq_o": np.concatenate([lay(wo[g]).reshape(P, -1) for g in range(NG)], axis=1),
        "C_norms": np.stack([v["L0_xattn_q_norm_w"], v["L0_xattn_k_norm_w"]], axis=1),
        "C_select": np.eye(NH, dtype=np.float32).reshape(-1),
        "C_mask": v["mask_1x1xSxS2_ff0"].reshape(SEQ, SEQ),
        "w1T": lay(v["L0_ffn_w1"].T), "c1T": lay(c1), "c2T": v["L0_ffn_c2_w"].T,
        "w2": v["L0_ffn_w2t"].reshape(INTER // HK, HK, D).transpose(1, 0, 2),
        "block_rank": np.arange(BLK, 0, -1).astype(np.float32),
        "expert_rank": np.arange(NE, 0, -1).astype(np.float32),
        "moe_W": lay(v["L1_ffn_weight"].T),
        "moe_A": lay(np.concatenate([lora, v["L1_ffn_gw1"].T], axis=1)),
        "moe_B": v["L1_ffn_lora_B"].reshape(NE * RANK, D), "moe_gw2": v["L1_ffn_gw2"].T,
        "L1_ffn_gb1": v["L1_ffn_gb1"], "L1_ffn_ln_gamma": v["L1_ffn_ln_gamma"],
        "L1_ffn_ln_beta": v["L1_ffn_ln_beta"], "L1_ffn_gb2": v["L1_ffn_gb2"],
    }


def lay(a):
    k, n = a.shape
    return np.ascontiguousarray(a.reshape(k // P, P, n).transpose(1, 0, 2))


def alibi_table():
    slopes = (2.0 ** (-2.0 ** (-(5 - 3)))) ** np.arange(1, 33, dtype=np.float64)
    slopes = slopes.astype(np.float32)
    q, k = np.arange(SEQ)[:, None, None], np.arange(SEQ)[None, None, :]
    t = slopes[None, :, None] * (k - q).astype(np.float32)
    t = np.where(k <= q, t, np.float32(-1e30)).astype(np.float32)
    return np.ascontiguousarray(t.reshape(SEQ, KC, CH, SEQ))


def head_scales(a):
    a = np.asarray(a).reshape(KC, 2, 1, HD)
    return np.ascontiguousarray(np.broadcast_to(a, (KC, 2, 4, HD)).reshape(KC, P).T)


def per_query_head(wt):
    heads = wt.shape[1] // HD
    reps = 4 if heads > 1 else CH
    a = wt.reshape(D, heads, 1, HD)
    return np.broadcast_to(a, (D, heads, reps, HD)).reshape(D, heads * reps * HD)


SIGNALS = (
    "ln_stat",
    "ln_sd_ready",
    "xn_ready",
    "xn_turned",
    "xnT_hi_ready",
    "xnT_lo_ready",
    "weights_landed",
    "weights_hi",
    "weights_abs",
    "weights_lo",
    "prologue_vector",
    "prologue_pool",
    "prologue_pe",
    "q_product",
    "q_ready",
    "k_product",
    "krep_ready",
    "kbd_by_pool",
    "kbd_by_vector",
    "v_product",
    "v_ready",
    "scores",
    "scores_read",
    "vector_chain",
    "shifted",
    "exponentials",
    "inverse_sums",
    "biased",
    "probabilities",
    "probs_turned",
    "PT_ready",
    "values_product",
    "oT_hi_ready",
    "oT_lo_ready",
    "y_product",
    "y_added",
    "ctx_landed",
    "ctx_hi_ready",
    "ctx_lo_ready",
    "r_product",
    "r_ready",
    "rank_product",
    "h_product",
    "is_block_max",
    "ranked",
    "h_kept",
    "h_turned",
    "hT_hi_ready",
    "hT_lo_ready",
    "h_used",
    "a_product",
    "a_kept",
    "gate_chain",
    "gate_scalar",
    "gate_pe",
    "weighted",
    "weighted_turned",
    "weighted_hi",
    "weighted_lo",
    "lora_product",
    "lora_added",
    "wo_landed",
    "wqkv_landed",
    "wo_hi",
    "wo_lo",
    "wqkv_hi",
    "wqkv_lo",
    "sums_of_squares",
    "v_turned",
    "q_rms_turned",
    "k_raw_ready",
    "vT_ready",
    "squares_ready",
    "k_rms_ready",
    "q_rms_ready",
    "k_ready",
    "q_inv_rms_row",
    "q_inv_rms",
    "V_by_scalar",
    "V_by_vector",
)


def load_constants(nc, signals, X, consts, dram):
    with (nc.semaphore("constants_landed") as landed, nc.semaphore("constants_made") as made,
          nc.Block() as block):
        @block.sync
        def _(eng):
            eng.dma_start(X[:, :].rearrange("p (t d) -> p t d", d=D),
                          dram["x"].rearrange("(t p) d -> p t d", p=P)).then_inc(landed, 16)
            eng.dma_start(consts["ident"][:, :], dram["ident"]).then_inc(landed, 16)
            eng.dma_start(consts["headmask"][:, :], dram["headmask"]).then_inc(landed, 16)
            eng.wait_ge(landed, 48)

        @block.vector
        def _(eng):
            eng.memset(consts["eps"][:, :], LN_EPS).then_inc(made, 1)
            eng.memset(consts["ones"][:, :], 1.0).then_inc(made, 1)
            eng.wait_ge(made, 2)

        @block.gpsimd
        def _(eng):
            for sem in signals.sems.values():
                eng.sem_inc(sem, 1)


def store_result(nc, X, out):
    with nc.semaphore("result_stored") as stored, nc.Block() as block:
        @block.sync
        def _(eng):
            eng.dma_start(out.rearrange("(t p) d -> p t d", p=P),
                          X[:, :].rearrange("p (t d) -> p t d", d=D)).then_inc(stored, 16)
            eng.wait_ge(stored, 16)


PHASES = (0, 1, 2, 3, 4, 5)


def decoder(nc, a, out):
    with ExitStack() as ctx:
        signals = Signals(ctx, nc, SIGNALS)

        def sb(name, shape):
            return ctx.enter_context(nc.sbuf_tensor(name, shape, F32))

        X = sb("X", [P, TILES * D])
        consts = {"ident": sb("ident", [P, P]), "headmask": sb("headmask", [P, CH]),
                  "eps": sb("eps", [P, 1]), "ones": sb("ones", [P, P])}
        load_constants(nc, signals, X, consts, a)
        if 0 in PHASES:
            small_attention(nc, signals, "sign", X, consts,
                            {"q": a["L0q"], "k": a["L0k"], "v": a["L0v"], "o": a["L0o"],
                             "scales": a["L0scales"], "v_rep": a["L0v_rep"], "o_scale": a["L0_attn_o_scale"]}, "gqa")
        if 1 in PHASES:
            cross_attention(nc, signals, X, consts, a)
        if 2 in PHASES:
            sparse_ffn(nc, signals, X, consts, a)
        if 3 in PHASES:
            small_attention(nc, signals, "alibi", X, consts,
                            {"q": a["L1q"], "k": a["L1k"], "v": a["L1v"], "o": a["L1o"],
                             "alibi": a["alibi"]}, "mqa")
        if 4 in PHASES:
            small_attention(nc, signals, "cross", X, consts,
                            {"q": a["Xq"], "k": a["Xk"], "v": a["Xv"], "o": a["Xo"],
                             "ctxT": a["ctxT"], "mask": a["mask_SxS2_bk0"]}, "cga")
        if 5 in PHASES:
            lora_experts(nc, signals, X, consts, a)
        store_result(nc, X, out)


def kernel(**inputs):
    import concourse.bacc as _bacc
    from concourse.bass_utils import run_bass_kernel_spmd as _run

    v = {k: np.asarray(x) for k, x in inputs.items()}
    w = v["L1_attn_Wqkv"]
    arrays = {
        "x": v["x"].reshape(TOK, D),
        "ident": np.eye(P, dtype=np.float32),
        "headmask": np.kron(np.eye(CH, dtype=np.float32), np.ones((HD, 1), np.float32)),
        "L0q": lay(v["L0_attn_q_weight"].T), "L0k": lay(per_query_head(v["L0_attn_k_weight"].T)),
        "L0v_rep": lay(per_query_head(v["L0_attn_v_weight"].T)),
        "L0v": lay(v["L0_attn_v_weight"].T), "L0o": lay(v["L0_attn_o_weight"].T),
        "L0scales": np.stack([np.ascontiguousarray(v["L0_attn_q_scale"].reshape(KC, P).T),
                              head_scales(v["L0_attn_k_scale"]), head_scales(v["L0_attn_v_scale"])]),
        "L0_attn_o_scale": v["L0_attn_o_scale"],
        "L1q": lay(w[:, :D]), "L1k": lay(per_query_head(w[:, D:D + HD])),
        "L1v": lay(per_query_head(w[:, D + HD:])),
        "L1o": lay(v["L1_attn_Wo"]), "alibi": alibi_table(),
        "Xq": lay(v["L1_xattn_w_q"].T), "Xk": lay(per_query_head(v["L1_xattn_w_k"].T)),
        "Xv": lay(v["L1_xattn_w_v"].T), "Xo": lay(v["L1_xattn_w_out"].T),
        "ctxT": lay(v["ctx_4096"].reshape(TOK, D).T), "mask_SxS2_bk0": v["mask_SxS2_bk0"],
    }
    arrays.update(more_arrays(v))
    nc = _bacc.Bacc("TRN2", target_bir_lowering=False, num_devices=1)
    args = {}
    for name, x in arrays.items():
        arrays[name] = x = np.ascontiguousarray(x)
        args[name] = nc.dram_tensor(f"in_{name}", x.shape, mybir.dt.from_np(x.dtype), kind="ExternalInput").ap()
    out = nc.dram_tensor("out", (TOK, D), F32, kind="ExternalOutput").ap()
    decoder(nc, args, out)
    r = _run(nc, [{f"in_{k}": x for k, x in arrays.items()}], core_ids=[0])
    return r.results[0]["out"].reshape(32, SEQ, D)
```

```python
from contextlib import ExitStack

import numpy as np

import concourse.bass as bass
from concourse import mybir

F32 = mybir.dt.float32
F32R = mybir.dt.float32r
U8 = mybir.dt.uint8
ALU = mybir.AluOpType
ACT = mybir.ActivationFunctionType
AX_X = mybir.AxisListType.X

P = 128
D = 512
KC = D // P
TOK = 2048
TILES = TOK // P
ST = 4
STOK = ST * P
NST = TILES // ST
SEQ = 64
SB = STOK // SEQ
HD = 16
CH = P // HD
LN_EPS = 1e-5


class Sig:

    def __init__(self, sem, base, per):
        self.sem, self.base, self.per = sem, base, per

    def at(self, i, k):
        return i * self.per + (self.base + k)

    def before(self, i):
        return i * self.per + self.base


class Signals:

    def __init__(self, ctx, nc, names):
        self.sems = {name: ctx.enter_context(nc.semaphore(name)) for name in names}
        self.total = {name: 1 for name in names}

    def get(self, name, per, passes):
        sig = Sig(self.sems[name], self.total[name], per)
        self.total[name] += per * passes
        return sig


class Memory:

    def __init__(self, ctx, nc, prefix, signals):
        self.ctx, self.nc, self.prefix, self.signals = ctx, nc, prefix, signals

    def sb(self, name, shape, dt=F32):
        return self.ctx.enter_context(self.nc.sbuf_tensor(f"{self.prefix}_{name}", shape, dt))

    def ps(self, name):
        return self.ctx.enter_context(self.nc.psum_tensor(f"{self.prefix}_{name}", [P, 512], F32))

    def sig(self, name, per=1, passes=NST):
        return self.signals.get(name, per, passes)


def products(eng, out, pairs):
    steps = []
    for lhs, rhs in pairs:
        if isinstance(lhs, tuple) and isinstance(rhs, tuple):
            steps += [(lhs[0], rhs[0]), (lhs[0], rhs[1]), (lhs[1], rhs[0])]
        elif isinstance(lhs, tuple):
            steps += [(lhs[0], rhs), (lhs[1], rhs)]
        elif isinstance(rhs, tuple):
            steps += [(lhs, rhs[0]), (lhs, rhs[1])]
        else:
            steps += [(lhs, rhs)]
    for n, (a, b) in enumerate(steps):
        last = eng.matmul(out, a, b, start=(n == 0), stop=(n == len(steps) - 1))
    return last


def x_tile(X, i, t):
    return X[:, bass.ds((i * ST + t) * D, D)]


class LayerNorm:

    def __init__(self, mem, X, ident, eps, wrap=0, width=STOK, xn=None, passes=NST):
        self.X, self.ident, self.eps, self.wrap = X, ident, eps, wrap
        self.stats = mem.sb("ln_stats", [P, ST, 6])
        self.mv = mem.sb("ln_mean_var", [P, ST, 2])
        self.sd = mem.sb("ln_sd", [P, ST])
        self.rstd = mem.sb("ln_rstd", [P, ST])
        self.off = 0
        self.xn = mem.sb("xn", [P, ST, D]) if xn is None else xn
        self.hi = mem.sb("xnT_hi", [P, KC, width + wrap], F32R)
        self.lo = mem.sb("xnT_lo", [P, KC, width + wrap], F32R)
        self.stat = mem.sig("ln_stat", ST + ST + 1)
        self.sd_ready = mem.sig("ln_sd_ready")
        self.xn_ready = mem.sig("xn_ready", ST)
        self.turned = mem.sig("xn_turned", ST)
        self.hi_ready = mem.sig("xnT_hi_ready", ST + (1 if wrap else 0))
        self.lo_ready = mem.sig("xnT_lo_ready", ST + (1 if wrap else 0))

    def vector_norm(self, eng, i):
        for t in range(ST):
            self.vector_stat(eng, i, t)
        self.vector_var(eng, i)
        for t in range(ST):
            self.vector_xn(eng, i, t)

    def vector_stat(self, eng, i, t):
        eng.bn_stats(self.stats[:, t, :], x_tile(self.X, i, t)).then_inc(self.stat.sem, 1)

    def vector_var(self, eng, i):
        eng.wait_ge(self.stat.sem, self.stat.at(i, ST))
        eng.memset(self.rstd[:, :], 0.0)
        for t in range(ST):
            eng.bn_aggr(self.mv[:, t, :], self.stats[:, t, :]).then_inc(self.stat.sem, 1)

    def vector_xn(self, eng, i, t):
        if t == 0:
            eng.wait_ge(self.sd_ready.sem, self.sd_ready.at(i, 1))
            eng.reciprocal(self.rstd[:, :], self.sd[:, :]).then_inc(self.stat.sem, 1)
            eng.wait_ge(self.stat.sem, self.stat.at(i, 2 * ST + 1))
            eng.wait_ge(self.turned.sem, self.turned.before(i))
        eng.tensor_scalar(self.xn[:, t, :], x_tile(self.X, i, t), self.mv[:, t, 0:1],
                          self.rstd[:, t:t + 1], ALU.subtract, ALU.mult).then_inc(self.xn_ready.sem, 1)

    def scalar_sd(self, eng, i):
        eng.wait_ge(self.stat.sem, self.stat.at(i, 2 * ST))
        eng.activation(self.sd[:, :], self.mv[:, :, 1], ACT.Sqrt, bias=self.eps[:, 0:1])\
           .then_inc(self.sd_ready.sem, 1)

    def tensor_turn(self, eng, i, t, bank):
        eng.wait_ge(self.xn_ready.sem, self.xn_ready.at(i, t + 1))
        for k in range(KC):
            last = eng.transpose(bank[:, k * P:(k + 1) * P], self.xn[:, t, k * P:(k + 1) * P],
                                 self.ident[:, :])
        last.then_inc(self.turned.sem, 1)

    def _part(self, a, t):
        return a[:, :, self.off + t * P:self.off + (t + 1) * P]

    def scalar_hi(self, eng, i, t, bank):
        eng.wait_ge(self.turned.sem, self.turned.at(i, t + 1))
        eng.activation(self._part(self.hi, t), bank[:, :].rearrange("p (k n) -> p k n", k=KC),
                       ACT.Copy).then_inc(self.hi_ready.sem, 1)

    def vector_lo(self, eng, i, t, bank):
        eng.wait_ge(self.hi_ready.sem, self.hi_ready.at(i, t + 1))
        eng.tensor_tensor(self._part(self.lo, t), bank[:, :].rearrange("p (k n) -> p k n", k=KC),
                          self._part(self.hi, t).bitcast(F32), ALU.subtract)\
           .then_inc(self.lo_ready.sem, 1)

    def scalar_wrap(self, eng, i):
        eng.wait_ge(self.hi_ready.sem, self.hi_ready.at(i, 1))
        eng.activation(self.hi[:, :, STOK:], self.hi[:, :, 0:self.wrap].bitcast(F32), ACT.Copy)\
           .then_inc(self.hi_ready.sem, 1)

    def vector_wrap(self, eng, i):
        eng.wait_ge(self.lo_ready.sem, self.lo_ready.at(i, 1))
        eng.tensor_copy(self.lo[:, :, STOK:], self.lo[:, :, 0:self.wrap].bitcast(F32))\
           .then_inc(self.lo_ready.sem, 1)


def small_attention(nc, signals, kind, X, consts, dram, prefix):
    ident, eps, ones, headmask = consts["ident"], consts["eps"], consts["ones"], consts["headmask"]
    sign, alibi, cross = kind == "sign", kind == "alibi", kind == "cross"
    KW = P if alibi else D
    NK = 1 if alibi else KC
    NU = KC * ST
    RING = 7
    TR = 5
    LASTSLOT = NU + TR + 2
    with ExitStack() as ctx:
        mem = Memory(ctx, nc, prefix, signals)
        dq, dk, dv, do = dram["q"], dram["k"], dram["v"], dram["o"]
        parts = 1 if sign else 2
        Wq = [mem.sb(f"Wq{n}", [P, KC, D], F32R) for n in range(parts)]
        Wk = [mem.sb(f"Wk{n}", [P, KC, KW], F32R) for n in range(parts)]
        Wv = [mem.sb(f"Wv{n}", [P, KC, P], F32R) for n in range(parts)]
        Wo = [mem.sb(f"Wo{n}", [P, KC, D], F32R) for n in range(parts)]
        ln = LayerNorm(mem, X, ident, eps, wrap=SEQ if not cross else 0)
        if cross:
            cth = mem.sb("ctxT_hi", [P, KC, STOK + SEQ], F32R)
            ctl = mem.sb("ctxT_lo", [P, KC, STOK + SEQ], F32R)
            craw = mem.sb("ctxT_raw", [P, KC, STOK])
            mbias = mem.sb("mask_bias", [P, SEQ])
            mraw = mem.sb("mask_raw", [P, SEQ], U8)
        qT = mem.sb("qT", [P, KC, STOK])
        krep = mem.sb("krep", [P, 2, STOK])
        NB = 1 if alibi else 2
        Kbd = mem.sb("Kbd", [P, NB, SB, CH, SEQ])
        Vbd = mem.sb("Vbd", [P, SB, 8, 2 * HD])
        T = mem.sb("T", [P, RING, CH, SEQ])
        mx = mem.sb("row_max", [P, 4, CH])
        rs = mem.sb("row_sum", [P, 2, CH])
        ri = mem.sb("row_inv", [P, RING, CH])
        PT = mem.sb("PT", [P, 2, 4, P])
        oh = ln.hi if cross else mem.sb("oT_hi", [P, KC, STOK], F32R)
        ol = ln.lo if cross else mem.sb("oT_lo", [P, KC, STOK], F32R)
        if alibi:
            table = mem.sb("alibi", [P, KC, CH, SEQ])
        if sign:
            qs = mem.sb("q_scale", [P, KC])
            ks = mem.sb("k_scale", [P, KC])
            vs = mem.sb("v_scale", [P, KC])
            osc = mem.sb("o_scale", [P, D])
            kmask = mem.sb("k_mask", [P, KC, CH])
            ysc = mem.sb("y_scaled", [P, D])
            scraw = mem.sb("scales_raw", [P, 3, KC])
            scp = mem.sb("scales_mean", [P, 3, KC])
        G = [mem.ps(f"G{n}") for n in range(2)]
        S = [mem.ps(f"S{n}") for n in range(2)]
        TP = [mem.ps(f"TP{n}") for n in range(2)]
        OT = [mem.ps(f"OT{n}") for n in range(2)]

        n_landed = 16 * (5 if sign else 2)
        PRE = 9 if sign else 3 if cross else 1
        w_raw = mem.sig("small_landed", n_landed, 1)
        w_landed = [mem.sig(f"weight_landed_{n}", 16, 1) for n in range(4)]
        w_hi = mem.sig("weights_hi", 4, 1)
        w_sum = mem.sig("weights_summed", 4 if sign else 0, 1)
        w_abs = mem.sig("weights_abs", 4 if sign else 0, 1)
        lo_pool = mem.sig("weights_lo", 0 if sign else 2, 1)
        lo_vec = mem.sig("weights_lo_by_vector", 0 if sign else 2, 1)
        pre = mem.sig("prologue_vector", PRE, 1)
        pre_pool = mem.sig("prologue_pool", 1, 1)
        pre_pe = mem.sig("prologue_pe", 1 if sign else 0, 1)
        q_done = mem.sig("q_product", KC)
        q_ready = mem.sig("q_ready", KC)
        k_done = mem.sig("k_product", NK)
        krep_ready = mem.sig("krep_ready", NK)
        kbd_pool = mem.sig("kbd_by_pool", NK)
        kbd_vec = mem.sig("kbd_by_vector", NK)
        v_done = mem.sig("v_product", ST)
        v_ready = mem.sig("v_ready", ST)
        s_done = mem.sig("scores", NU)
        s_read = mem.sig("scores_read", 0 if sign else NU)
        vec = mem.sig("vector_chain", 2 * NU if sign else NU + NU // 2)
        max_ready = mem.sig("row_max_ready", 0 if sign else NU // 2)
        pool_sub = mem.sig("shifted_by_pool", 0 if sign else NU // 2)
        sub_ready = mem.sig("shifted", NU if sign else NU // 2)
        exp_ready = mem.sig("exponentials", NU)
        inv_ready = mem.sig("inverse_sums", NU)
        norm_ready = mem.sig("probabilities", NU)
        t_done = mem.sig("probs_turned", NU)
        pt_ready = mem.sig("PT_ready", NU)
        pv_done = mem.sig("values_product", NU)
        oh_ready = mem.sig("oT_hi_ready", KC)
        ol_ready = mem.sig("oT_lo_ready", KC)
        y_done = mem.sig("y_product", ST)
        y_added = mem.sig("y_added", ST * (2 if sign else 1))
        if cross:
            ctx_landed = mem.sig("ctx_landed", 16)
            cth_ready = mem.sig("ctx_hi_ready", KC)
            ctl_ready = mem.sig("ctx_lo_ready", KC)

        KbF = Kbd[:, :, :, :, :].rearrange("p a b h s -> p (a b h s)")
        qTF = qT[:, :, :].rearrange("p k n -> p (k n)")
        rq = KbF[:, 0:KC * D].rearrange("p (k n) -> p k n", k=KC)
        ro = KbF[:, KC * D:2 * KC * D].rearrange("p (k n) -> p k n", k=KC)
        kv_room = qTF if alibi else KbF[:, 2 * KC * D:]
        rk = kv_room[:, 0:KC * KW].rearrange("p (k n) -> p k n", k=KC)
        rv = kv_room[:, KC * KW:KC * KW + KC * P].rearrange("p (k n) -> p k n", k=KC)
        Tsum = T[:, 0:4, :, :].rearrange("p r h s -> p r (h s)")
        rvw = qT
        raws = [(rk, Wk, dk), (rq, Wq, dq), (rv, Wv, dv), (ro, Wo, do)]

        def split_low(eng, n, done):
            raw, w, _ = raws[n]
            eng.wait_ge(w_hi.sem, w_hi.at(0, n + 1))
            eng.tensor_tensor(w[1][:, :, :], raw, w[0][:, :, :].bitcast(F32), ALU.subtract).then_inc(done.sem, 1)

        def all_low(eng):
            eng.wait_ge(lo_pool.sem, lo_pool.at(0, 2))
            eng.wait_ge(lo_vec.sem, lo_vec.at(0, 2))

        def pair(w, f):
            return f(w[0]) if sign else (f(w[0]), f(w[1]))

        kv_hi, kv_lo = (cth, ctl) if cross else (ln.hi, ln.lo)

        if cross:
            first = ["x0", "v0", "x1", "v1", "x2", "k1", "x3", "q0"]
            slots = {0: ["v2"], 1: ["v3"], 2: ["q1"], 3: ["q2"], 4: ["k2"], 5: ["q3"], 8: ["k3"], 19: ["k0+"]}
        else:
            first = []
            slots = {0: ["k1"], 1: ["q1"], 2: ["v0", "v1"], 3: ["v2", "v3"], 4: ["k2"], 5: ["q2"], 8: ["k3"],
                     9: ["q3"], 11: ["x0+"], 12: ["x1+"], 13: ["x2+"], 14: ["x3+"], 18: ["k0+"], 20: ["q0+"]}
        if alibi:
            slots = {s: [n for n in names if n[0] != "k" or n == "k0+"] for s, names in slots.items()}
        STATS, NORM, STAGE = 4, 9, 10
        order = first + [n for s in sorted(slots) for n in slots[s]]
        order += [None] * (len(order) % 2) + [f"y{t}" for t in range(ST)]
        entry = [n for n in order if n and n[-1] == "+"]
        if not cross:
            assert len(order) % 2 == 0
        bank_of = {n: G[k % 2] for k, n in enumerate(order) if n}

        def freed(name):
            k = int(name[1]) + 1
            return {"x": (ln.lo_ready, k), "q": (q_ready, k), "k": (krep_ready, k), "v": (v_ready, k),
                    "y": (y_added, k * (2 if sign else 1))}[name[0]]

        block = ctx.enter_context(nc.Block())

        @block.sync
        def _(eng):
            extra = []
            if alibi:
                extra = [(table[0:SEQ, :, :, :], dram["alibi"]), (table[SEQ:P, :, :, :], dram["alibi"])]
            if sign:
                extra = [(scraw[:, n, :], dram["scales"][n]) for n in range(3)]
                extra += [(osc[:, :], dram["o_scale"].partition_broadcast(P)), (rvw[:, :, :], dram["v_rep"])]
            if cross:
                extra = [(mraw[0:SEQ, :], dram["mask"]), (mraw[SEQ:P, :], dram["mask"])]
            for n, (raw, _, d) in enumerate(raws):
                eng.dma_start(raw, d).then_inc(w_landed[n].sem, 16)
                if n == 1:
                    for a, b in extra:
                        eng.dma_start(a, b).then_inc(w_raw.sem, 16)
            if cross:
                with eng.Fori(0, NST) as i:
                    eng.wait_ge(ctl_ready.sem, ctl_ready.before(i))
                    eng.dma_start(craw[:, :, :], dram["ctxT"][:, :, bass.ds(i * STOK, STOK)])\
                       .then_inc(ctx_landed.sem, 16)

        def room_free(eng, i, c):
            if c >= 2:
                eng.wait_ge(s_done.sem, s_done.at(i, 4 * (c - 1)))
            elif c == 0 and not isinstance(i, int):
                eng.wait_ge(s_done.sem, s_done.at(i, -4 if NK > 1 else 0))
            elif c == 1:
                eng.wait_ge(s_done.sem, s_done.before(i))

        def stage_context(i, eng, k, high):
            if high:
                if k == 0:
                    eng.wait_ge(ctx_landed.sem, ctx_landed.at(i, 16))
                    eng.wait_ge(k_done.sem, k_done.before(i))
                eng.activation(cth[:, k, 0:STOK], craw[:, k, :], ACT.Copy)
                eng.activation(cth[:, k, STOK:], craw[:, k, 0:SEQ], ACT.Copy).then_inc(cth_ready.sem, 1)
            else:
                eng.wait_ge(cth_ready.sem, cth_ready.at(i, k + 1))
                eng.tensor_tensor(ctl[:, k, 0:STOK], craw[:, k, :], cth[:, k, 0:STOK].bitcast(F32), ALU.subtract)
                eng.tensor_tensor(ctl[:, k, STOK:], craw[:, k, 0:SEQ], cth[:, k, STOK:].bitcast(F32),
                                  ALU.subtract).then_inc(ctl_ready.sem, 1)

        @block.scalar
        def _(eng):
            def keep(i, name):
                bank, c = bank_of[name], int(name[1])
                if name[0] == "x":
                    ln.scalar_hi(eng, i, c, bank)
                    if c == ST - 1 and not cross:
                        ln.scalar_wrap(eng, i)
                elif name[0] == "q":
                    eng.wait_ge(q_done.sem, q_done.at(i, c + 1))
                    eng.activation(qT[:, c, :], bank[:, :], ACT.Copy,
                                   scale=qs[:, c:c + 1] if sign else HD ** -0.5).then_inc(q_ready.sem, 1)
                elif name[0] == "k":
                    eng.wait_ge(k_done.sem, k_done.at(i, c + 1))
                    if c:
                        eng.wait_ge(kbd_pool.sem, kbd_pool.at(i, max(c - 1, 1)))
                        eng.wait_ge(kbd_vec.sem, kbd_vec.at(i, max(c - 1, 1)))
                    else:
                        eng.wait_ge(kbd_pool.sem, kbd_pool.before(i))
                        eng.wait_ge(kbd_vec.sem, kbd_vec.before(i))
                    eng.activation(krep[:, c % 2, :], bank[:, :], ACT.Copy).then_inc(krep_ready.sem, 1)
                else:
                    eng.wait_ge(v_done.sem, v_done.at(i, c + 1))
                    va = bank[:, 0:P].rearrange("p (g d) -> p g d", d=HD)
                    vb = bank[:, P:2 * P].rearrange("p (g d) -> p g d", d=HD)
                    for lo, hi, src, b, at in ((0, SEQ, va, 2 * c, 0), (SEQ, P, va, 2 * c + 1, HD),
                                               (0, SEQ, vb, 2 * c + 1, 0), (SEQ, P, vb, (2 * c + 2) % SB, HD)):
                        last = eng.activation(Vbd[lo:hi, b, :, at:at + HD], src[lo:hi, :, :], ACT.Copy)
                    last.then_inc(v_ready.sem, 1)

            def scalar_pass(i, more):
                for name in first:
                    keep(i, name)
                for s in range(LASTSLOT + 2):
                    if s < NU:
                        if sign:
                            eng.wait_ge(sub_ready.sem, sub_ready.at(i, s + 1))
                        else:
                            by = pool_sub if s % 2 else sub_ready
                            eng.wait_ge(by.sem, by.at(i, s // 2 + 1))
                        row = T[:, s % RING, :, :]
                        eng.activation(row, row, ACT.Exp).then_inc(exp_ready.sem, 1)
                    u = s - TR
                    if 0 <= u < NU:
                        eng.wait_ge(t_done.sem, t_done.at(i, u + 1))
                        if u >= 2:
                            eng.wait_ge(pv_done.sem, pv_done.at(i, u - 1))
                        else:
                            eng.wait_ge(pv_done.sem, pv_done.before(i))
                        eng.activation(PT[:, u % 2, :, :],
                                       TP[u % 2][:, :].rearrange("p (j n) -> p j n", j=4), ACT.Copy)\
                           .then_inc(pt_ready.sem, 1)
                    for name in slots.get(s, ()):
                        if name in entry and more:
                            keep(i + 1, name)
                        elif name not in entry:
                            keep(i, name)
                    if s == STATS + ST - 1 and more:
                        ln.scalar_sd(eng, i + 1)
                    if cross and more and 0 <= s - STAGE < KC:
                        stage_context(i + 1, eng, s - STAGE, True)
                    c = (s - TR - 5) // 4
                    if s - TR - 5 == 4 * c and 0 <= c < KC:
                        eng.wait_ge(pv_done.sem, pv_done.at(i, 4 * c + 4))
                        eng.activation(oh[:, c, :], OT[c % 2][:, :], ACT.Copy,
                                       scale=vs[:, c:c + 1] if sign else 1.0).then_inc(oh_ready.sem, 1)

            ln.scalar_sd(eng, 0)
            for name in entry:
                if name[0] == "x":
                    keep(0, name)
            for n, (raw, w, _) in enumerate(raws):
                eng.wait_ge(w_landed[n].sem, w_landed[n].at(0, 16))
                eng.activation(w[0][:, :, :], raw, ACT.Sign if sign else ACT.Copy).then_inc(w_hi.sem, 1)
                if sign:
                    eng.wait_ge(w_hi.sem, w_hi.at(0, n + 1))
                    if raw is rv:
                        eng.wait_ge(w_raw.sem, w_raw.at(0, n_landed))
                    src = rvw[:, :, :] if raw is rv else raw
                    eng.activation(src, src, ACT.Abs).then_inc(w_abs.sem, 1)
            if sign:
                eng.wait_ge(pre.sem, pre.at(0, PRE))
            if cross:
                for k in range(KC):
                    stage_context(0, eng, k, True)
            for name in entry:
                if name[0] != "x":
                    keep(0, name)
            with eng.Fori(0, NST - 1) as i:
                scalar_pass(i, True)
            scalar_pass(NST - 1, False)

        @block.gpsimd
        def _(eng):
            eng.memset(Vbd[:, :, :, :], 0.0).then_inc(pre_pool.sem, 1)
            if not sign:
                split_low(eng, 0, lo_pool)
                split_low(eng, 2, lo_pool)
            def spread_keys(i, c):
                eng.wait_ge(krep_ready.sem, krep_ready.at(i, c + 1))
                room_free(eng, i, c)
                if sign:
                    eng.wait_ge(pre.sem, pre.at(0, PRE))
                else:
                    all_low(eng)
                src = krep[:, c % 2, :].rearrange("p (b s) -> p b s", b=SB)
                for h in range(CH // 2):
                    m = kmask[:, c, h:h + 1] if sign else headmask[:, h:h + 1]
                    if h == 0:
                        eng.tensor_tensor(Kbd[:, c % NB, :, h, :], src,
                                          m.unsqueeze(2).to_broadcast([P, SB, SEQ]), ALU.mult)
                        continue
                    last = eng.tensor_scalar(Kbd[:, c % NB, :, h, :], src, m, 0.0, ALU.mult, ALU.add)
                last.then_inc(kbd_pool.sem, 1)

            def pool_pass(i, more):
                if cross:
                    spread_keys(i, 1)
                for s in range(LASTSLOT):
                    if s < NU and s % 2 and not sign:
                        eng.wait_ge(max_ready.sem, max_ready.at(i, s // 2 + 1))
                        row = T[:, s % RING, :, :]
                        eng.tensor_tensor(row, row, mx[:, s % 4, :].unsqueeze(2).to_broadcast([P, CH, SEQ]),
                                          ALU.subtract).then_inc(pool_sub.sem, 1)
                    u = s - 2
                    if 0 <= u < NU:
                        eng.wait_ge(inv_ready.sem, inv_ready.at(i, u + 1))
                        row = T[:, u % RING, :, :]
                        eng.tensor_tensor(row, row, ri[:, u % RING, :].unsqueeze(2).to_broadcast([P, CH, SEQ]),
                                          ALU.mult).then_inc(norm_ready.sem, 1)
                    for name in slots.get(s - 1, ()):
                        if name[0] == "k" and (more or name not in entry):
                            spread_keys(i + 1 if name in entry else i, int(name[1]))
                    if cross and more and 0 <= s - STAGE < KC:
                        stage_context(i + 1, eng, s - STAGE, False)

            if cross:
                for k in range(KC):
                    stage_context(0, eng, k, False)
            spread_keys(0, 0)
            with eng.Fori(0, NST - 1) as i:
                pool_pass(i, True)
            pool_pass(NST - 1, False)

        @block.vector
        def _(eng):
            count = [0]

            def step(ins):
                count[0] += 1
                ins.then_inc(pre.sem, 1)
                eng.wait_ge(pre.sem, pre.at(0, count[0]))

            def spread_keys(i, c):
                eng.wait_ge(krep_ready.sem, krep_ready.at(i, c + 1))
                room_free(eng, i, c)
                if not sign:
                    all_low(eng)
                src = krep[:, c % 2, :].rearrange("p (b s) -> p b s", b=SB)
                for h in range(CH // 2, CH):
                    m = kmask[:, c, h:h + 1] if sign else headmask[:, h:h + 1]
                    last = eng.tensor_scalar(Kbd[:, c % NB, :, h, :], src, m, None, ALU.mult)
                last.then_inc(kbd_vec.sem, 1)

            def take(i, name):
                if name[0] == "x":
                    ln.vector_lo(eng, i, int(name[1]), bank_of[name])
                    if name[1] == "3" and not cross:
                        ln.vector_wrap(eng, i)
                elif name[0] == "k":
                    spread_keys(i, int(name[1]))

            def vector_pass(i, more):
                links = [0]

                def chain(ins):
                    links[0] += 1
                    ins.then_inc(vec.sem, 1)
                    return links[0]

                for name in first:
                    take(i, name)

                def take_scores(u):
                    eng.wait_ge(s_done.sem, s_done.at(i, u + 1))
                    if u >= RING:
                        eng.wait_ge(t_done.sem, t_done.at(i, u - RING + 1))
                    else:
                        eng.wait_ge(t_done.sem, t_done.before(i))
                    if sign:
                        return
                    src = S[u % 2][:, :].rearrange("p (h s) -> p h s", h=CH)
                    row = T[:, u % RING, :, :]
                    extra = table[:, u // ST, :, :] if alibi else mbias[:, :].unsqueeze(1).to_broadcast([P, CH, SEQ])
                    eng.tensor_tensor(row, src, extra, ALU.add).then_inc(s_read.sem, 1)

                def shift(u):
                    row = T[:, u % RING, :, :]
                    src = row
                    if not sign:
                        eng.wait_ge(s_read.sem, s_read.at(i, u + 1))
                    else:
                        src = S[u % 2][:, :].rearrange("p (h s) -> p h s", h=CH)
                    if not sign and u % 2:
                        if u >= 4:
                            eng.wait_ge(pool_sub.sem, pool_sub.at(i, (u - 4) // 2 + 1))
                        else:
                            eng.wait_ge(pool_sub.sem, pool_sub.before(i))
                        eng.reduce_max(mx[:, u % 4, :], src, AX_X).then_inc(max_ready.sem, 1)
                        return
                    n = chain(eng.reduce_max(mx[:, u % 4, :], src, AX_X))
                    eng.wait_ge(vec.sem, vec.at(i, n))
                    last = eng.tensor_tensor(row, src, mx[:, u % 4, :].unsqueeze(2).to_broadcast([P, CH, SEQ]),
                                             ALU.subtract)
                    last.then_inc(sub_ready.sem, 1)

                def invert(u):
                    eng.wait_ge(exp_ready.sem, exp_ready.at(i, u + 1))
                    n = chain(eng.reduce_sum(rs[:, u % 2, :], T[:, u % RING, :, :], AX_X))
                    eng.wait_ge(vec.sem, vec.at(i, n))
                    eng.reciprocal(ri[:, u % RING, :], rs[:, u % 2, :]).then_inc(inv_ready.sem, 1)

                for s in range(LASTSLOT + 2):
                    if s < NU:
                        take_scores(s)
                    if 0 <= s - 2 < NU:
                        invert(s - 2)
                    if s < NU:
                        shift(s)
                    for name in slots.get(s - 1, ()):
                        if more or name not in entry:
                            take(i + 1 if name in entry else i, name)
                    if more and 0 <= s - STATS < ST:
                        ln.vector_stat(eng, i + 1, s - STATS)
                    if more and s == STATS + ST - 1:
                        ln.vector_var(eng, i + 1)
                    if more and 0 <= s - NORM < ST:
                        ln.vector_xn(eng, i + 1, s - NORM)
                    c = (s - TR - 6) // 4
                    if s - TR - 6 == 4 * c and 0 <= c < KC:
                        eng.wait_ge(oh_ready.sem, oh_ready.at(i, c + 1))
                        if sign:
                            eng.scalar_tensor_tensor(ol[:, c, :], OT[c % 2][:, :], vs[:, c:c + 1],
                                                     oh[:, c, :].bitcast(F32), ALU.mult, ALU.subtract)\
                               .then_inc(ol_ready.sem, 1)
                        else:
                            eng.tensor_tensor(ol[:, c, :], OT[c % 2][:, :], oh[:, c, :].bitcast(F32),
                                              ALU.subtract).then_inc(ol_ready.sem, 1)
                for t in range(ST):
                    bank = bank_of[f"y{t}"]
                    eng.wait_ge(y_done.sem, y_done.at(i, t + 1))
                    xt = x_tile(X, i, t)
                    if sign:
                        eng.wait_ge(y_added.sem, y_added.at(i, 2 * t))
                        eng.tensor_tensor(ysc[:, :], bank[:, :], osc[:, :], ALU.mult).then_inc(y_added.sem, 1)
                        eng.wait_ge(y_added.sem, y_added.at(i, 2 * t + 1))
                        eng.tensor_tensor(xt, xt, ysc[:, :], ALU.add).then_inc(y_added.sem, 1)
                    else:
                        eng.tensor_tensor(xt, xt, bank[:, :], ALU.add).then_inc(y_added.sem, 1)

            step(eng.memset(ri[:, :, :], 0.0))
            ln.vector_norm(eng, 0)
            for name in entry:
                if name[0] == "x":
                    take(0, name)
            if sign:
                for n, (raw, _, _) in enumerate(raws):
                    src = rvw[:, :, :] if raw is rv else raw
                    eng.wait_ge(w_abs.sem, w_abs.at(0, n + 1))
                    eng.reduce_sum(Tsum[:, n, :], src.rearrange("p k n -> p n k"), AX_X).then_inc(w_sum.sem, 1)
                eng.wait_ge(pre_pe.sem, pre_pe.at(0, 1))
                qkv = S[0][:, 0:3 * KC].rearrange("p (n c) -> p n c", n=3)
                step(eng.tensor_scalar(scp[:, :, :], qkv, 1.0 / D, 1e-8, ALU.mult, ALU.max))
                step(eng.tensor_tensor(scp[:, :, :], scp[:, :, :], scraw[:, :, :], ALU.mult))
                step(eng.tensor_scalar(qs[:, :], scp[:, 0, :], HD ** -0.5, None, ALU.mult))
                step(eng.tensor_copy(ks[:, :], scp[:, 1, :]))
                step(eng.tensor_copy(vs[:, :], scp[:, 2, :]))
                step(eng.tensor_tensor(kmask[:, :, :], ks[:, :].unsqueeze(2).to_broadcast([P, KC, CH]),
                                       headmask[:, :].unsqueeze(1).to_broadcast([P, KC, CH]), ALU.mult))
                step(eng.tensor_scalar(ysc[:, :], S[1][:, :], 1.0 / D, 1e-8, ALU.mult, ALU.max))
                step(eng.tensor_tensor(osc[:, :], osc[:, :], ysc[:, :], ALU.mult))
            eng.wait_ge(w_raw.sem, w_raw.at(0, n_landed))
            if cross:
                step(eng.tensor_copy(mbias[:, :], mraw[:, :]))
                step(eng.tensor_scalar(mbias[:, :], mbias[:, :], 1.0, float(np.finfo(np.float32).max),
                                       ALU.subtract, ALU.mult))
            assert count[0] == PRE, count[0]
            if not sign:
                split_low(eng, 1, lo_vec)
                split_low(eng, 3, lo_vec)
            for name in entry:
                if name[0] != "x":
                    take(0, name)
            with eng.Fori(0, NST - 1) as i:
                vector_pass(i, True)
            vector_pass(NST - 1, False)

        @block.tensor
        def _(eng):
            def make(i, name, own):
                b, c = bank_of[name], int(name[1])
                at = order.index(name)
                before = [n for n in order[:at] if n and bank_of[n] is b]
                if before:
                    sig, k = freed(before[-1])
                    if before[-1] in entry:
                        eng.wait_ge(sig.sem, sig.at(i, k))
                    elif own is not None:
                        eng.wait_ge(sig.sem, sig.at(own, k))
                else:
                    eng.wait_ge(y_added.sem, y_added.before(i))
                    eng.wait_ge(krep_ready.sem, krep_ready.at(i, 1))
                    if not cross:
                        eng.wait_ge(q_ready.sem, q_ready.at(i, 1))
                if name[0] == "x":
                    ln.tensor_turn(eng, i, c, b)
                elif name[0] == "q":
                    if c == 0:
                        eng.wait_ge(ln.lo_ready.sem, ln.lo_ready.before(i + 1))
                        eng.wait_ge(ln.hi_ready.sem, ln.hi_ready.before(i + 1))
                    products(eng, b[:, :], [(pair(Wq, lambda w: w[:, k, c * P:(c + 1) * P]),
                                             (ln.hi[:, k, 0:STOK], ln.lo[:, k, 0:STOK])) for k in range(KC)])\
                        .then_inc(q_done.sem, 1)
                elif name[0] == "k":
                    if c == 0 and cross:
                        eng.wait_ge(cth_ready.sem, cth_ready.at(i, KC))
                        eng.wait_ge(ctl_ready.sem, ctl_ready.at(i, KC))
                    elif c == 0:
                        eng.wait_ge(ln.lo_ready.sem, ln.lo_ready.before(i + 1))
                        eng.wait_ge(ln.hi_ready.sem, ln.hi_ready.before(i + 1))
                    products(eng, b[:, :], [(pair(Wk, lambda w: w[:, k, c * P:(c + 1) * P]),
                                             (kv_hi[:, k, 0:STOK], kv_lo[:, k, 0:STOK])) for k in range(KC)])\
                        .then_inc(k_done.sem, 1)
                elif name[0] == "v":
                    for side in range(2):
                        at = c * P + side * SEQ
                        last = products(eng, b[:, side * P:(side + 1) * P],
                                        [((kv_hi[:, k, at:at + P], kv_lo[:, k, at:at + P]),
                                          pair(Wv, lambda w: w[:, k, :])) for k in range(KC)])
                    last.then_inc(v_done.sem, 1)
                else:
                    products(eng, b[:, :], [((oh[:, k, c * P:(c + 1) * P], ol[:, k, c * P:(c + 1) * P]),
                                             pair(Wo, lambda w: w[:, k, :])) for k in range(KC)])\
                        .then_inc(y_done.sem, 1)

            def tensor_pass(i, more):
                for name in first:
                    make(i, name, i)
                for s in range(LASTSLOT):
                    if s < NU:
                        c, t = divmod(s, ST)
                        if t == 0:
                            eng.wait_ge(q_ready.sem, q_ready.at(i, c + 1))
                            if c < NK:
                                eng.wait_ge(kbd_pool.sem, kbd_pool.at(i, c + 1))
                                eng.wait_ge(kbd_vec.sem, kbd_vec.at(i, c + 1))
                        free = sub_ready if sign else s_read
                        if s >= 2:
                            eng.wait_ge(free.sem, free.at(i, s - 1))
                        else:
                            eng.wait_ge(free.sem, free.before(i))
                        kb = 0 if alibi else c % NB
                        for b in range(2):
                            last = eng.matmul(S[s % 2][SEQ * b:SEQ * (b + 1), :],
                                              qT[:, c, t * P + SEQ * b:t * P + SEQ * (b + 1)],
                                              Kbd[:, kb, 2 * t + b, :, :], start=True, stop=True)
                        last.then_inc(s_done.sem, 1)
                    for name in slots.get(s, ()):
                        if name in entry and more:
                            make(i + 1, name, i)
                        elif name not in entry:
                            make(i, name, i)
                    u = s - TR
                    if 0 <= u < NU:
                        eng.wait_ge(norm_ready.sem, norm_ready.at(i, u + 1))
                        if u >= 2:
                            eng.wait_ge(pt_ready.sem, pt_ready.at(i, u - 1))
                        else:
                            eng.wait_ge(pt_ready.sem, pt_ready.before(i))
                        for j in range(4):
                            last = eng.transpose(TP[u % 2][:, j * P:(j + 1) * P],
                                                 T[:, u % RING, 2 * j:2 * j + 2, :], ident[:, :])
                        last.then_inc(t_done.sem, 1)
                    u = s - TR - 1
                    if 0 <= u < NU:
                        c, t = divmod(u, ST)
                        eng.wait_ge(pt_ready.sem, pt_ready.at(i, u + 1))
                        if u == 0:
                            eng.wait_ge(v_ready.sem, v_ready.at(i, ST))
                        if t == 0:
                            if c >= 2:
                                eng.wait_ge(ol_ready.sem, ol_ready.at(i, c - 1))
                            else:
                                eng.wait_ge(ol_ready.sem, ol_ready.before(i))
                        for b in range(2):
                            for j in range(4):
                                last = eng.matmul(
                                    OT[c % 2][32 * j:32 * j + 32, t * P + SEQ * b:t * P + SEQ * (b + 1)],
                                    Vbd[:, 2 * t + b, 2 * c + j // 2, :],
                                    PT[:, u % 2, j, SEQ * b:SEQ * (b + 1)], start=True, stop=True,
                                    tile_position=(0, 32 * j))
                        last.then_inc(pv_done.sem, 1)
                eng.wait_ge(oh_ready.sem, oh_ready.before(i + 1))
                eng.wait_ge(ol_ready.sem, ol_ready.before(i + 1))
                for t in range(ST):
                    make(i, f"y{t}", i)

            for name in entry:
                if name[0] == "x":
                    make(0, name, None)
            if not sign:
                all_low(eng)
            eng.wait_ge(w_hi.sem, w_hi.at(0, 2 if sign else 4))
            eng.wait_ge(pre_pool.sem, pre_pool.at(0, 1))
            for name in entry:
                if name[0] != "x":
                    make(0, name, None)
            if sign:
                eng.wait_ge(w_sum.sem, w_sum.at(0, 4))
                for n, at in enumerate((1, 0, 2)):
                    for c in range(KC):
                        eng.matmul(S[0][:, n * KC + c:n * KC + c + 1], Tsum[:, at, c * P:(c + 1) * P],
                                   ones[:, 0:1], start=True, stop=True)
                eng.matmul(S[1][:, :], ones[:, :], Tsum[:, 3, :], start=True, stop=True).then_inc(pre_pe.sem, 1)
                eng.wait_ge(pre.sem, pre.at(0, PRE))
            with eng.Fori(0, NST - 1) as i:
                tensor_pass(i, True)
            tensor_pass(NST - 1, False)


INTER = 1792
BLK = 32
QW = 448
NQ = INTER // QW
QB = QW // BLK
HK = QW // 4


def sparse_ffn(nc, signals, X, consts, a):
    NU = ST * NQ
    NORM = 6
    with ExitStack() as ctx:
        mem = Memory(ctx, nc, "ffn", signals)
        W1 = [mem.sb(f"w1_{n}", [P, KC, INTER], F32R) for n in range(2)]
        W2 = [mem.sb(f"w2_{n}", [HK, INTER // HK, D], F32R) for n in range(2)]
        C1 = [mem.sb(f"c1_{n}", [P, KC, 16], F32R) for n in range(2)]
        C2 = mem.sb("c2", [16, INTER])
        rank = mem.sb("block_rank", [P, BLK])
        ln = LayerNorm(mem, X, consts["ident"], consts["eps"])
        rT = mem.sb("rT", [16, STOK])
        bmax = mem.sb("block_max", [P, 2, QB])
        zmax = mem.sb("first_max", [P, 2, QB])
        E1 = mem.sb("one_hot", [P, 3, QB, BLK])
        HM = mem.sb("h_kept", [P, 2, QW])
        hh = mem.sb("hT_hi", [HK, 2, 4 * P], F32R)
        hl = mem.sb("hT_lo", [HK, 2, 4 * P], F32R)
        I = [mem.ps(f"I{n}") for n in range(2)]
        H = [mem.ps(f"H{n}") for n in range(2)]
        TP = [mem.ps(f"TP{n}") for n in range(2)]
        Y = [mem.ps(f"Y{n}") for n in range(2)]
        xroom = ln.xn[:, :, :].rearrange("p t d -> p (t d)")
        rooms = [xroom[:, 0:2 * D], xroom[:, 2 * D:4 * D], E1[:, :, :, :].rearrange("p a b s -> p (a b s)")]
        ROOMS = len(rooms)
        pieces = []
        for n in range(2 * NQ):
            at = slice(n % 2 * 2, n % 2 * 2 + 2), slice(n // 2 * QW, (n // 2 + 1) * QW)
            pieces.append((P, 2 * QW, a["w1T"][:, at[0], at[1]], [w[:, at[0], at[1]] for w in W1]))
        for n in range(2 * NQ):
            at = slice(2 * n, 2 * n + 2)
            pieces.append((HK, 2 * D, a["w2"][:, at, :], [w[:, at, :] for w in W2]))
        c1room = HM[:, 0, 0:KC * 16].rearrange("p (k n) -> p k n", k=KC)

        def raw(n):
            rows, size, _, (hi, _) = pieces[n]
            return rooms[n % ROOMS][0:rows, 0:size].rearrange("p (k n) -> p k n", k=2)

        def use(n):
            return n // ROOMS + 1

        small = mem.sig("small_landed", 48, 1)
        uses = [len(range(r, len(pieces), ROOMS)) for r in range(ROOMS)]
        landed = [mem.sig(f"room_landed_{r}", 16 * uses[r], 1) for r in range(ROOMS)]
        split_lo = [mem.sig(f"room_split_{r}", uses[r], 1) for r in range(ROOMS)]
        w_hi = mem.sig("weights_hi", len(pieces) + 1, 1)
        c1_lo = mem.sig("weights_lo", 1, 1)

        def low(eng, n):
            hi, lo = pieces[n][3]
            eng.wait_ge(w_hi.sem, w_hi.at(0, n + 2))
            eng.tensor_tensor(lo, raw(n), hi.bitcast(F32), ALU.subtract).then_inc(split_lo[n % ROOMS].sem, 1)

        def all_split(eng):
            for r in range(ROOMS):
                eng.wait_ge(split_lo[r].sem, split_lo[r].at(0, uses[r]))

        r_done = mem.sig("r_product")
        r_ready = mem.sig("r_ready")
        i_done = mem.sig("rank_product", NU)
        h_done = mem.sig("h_product", NU)
        vec = mem.sig("vector_chain", 3 * NU)
        eq_ready = mem.sig("is_block_max", NU)
        z_ready = mem.sig("ranked", NU)
        h_ready = mem.sig("h_kept", NU)
        t_done = mem.sig("h_turned", NU)
        hh_ready = mem.sig("hT_hi_ready", NU)
        hl_ready = mem.sig("hT_lo_ready", NU)
        o_done = mem.sig("h_used", NU)
        y_added = mem.sig("y_added", ST)

        block = ctx.enter_context(nc.Block())

        @block.sync
        def _(eng):
            eng.dma_start(c1room, a["c1T"]).then_inc(small.sem, 16)
            eng.dma_start(C2[:, :], a["c2T"]).then_inc(small.sem, 16)
            eng.dma_start(rank[:, :], a["block_rank"].partition_broadcast(P)).then_inc(small.sem, 16)
            for n, (_, _, src, _) in enumerate(pieces):
                r = n % ROOMS
                if n >= ROOMS:
                    eng.wait_ge(split_lo[r].sem, split_lo[r].at(0, use(n) - 1))
                eng.dma_start(raw(n), src).then_inc(landed[r].sem, 16)

        @block.scalar
        def _(eng):
            eng.wait_ge(small.sem, small.at(0, 48))
            eng.activation(C1[0][:, :, :], c1room, ACT.Copy).then_inc(w_hi.sem, 1)
            for n in range(len(pieces)):
                r = n % ROOMS
                eng.wait_ge(landed[r].sem, landed[r].at(0, 16 * use(n)))
                eng.activation(pieces[n][3][0], raw(n), ACT.Copy).then_inc(w_hi.sem, 1)
            def scalar_pass(i, more):
                for t in range(ST):
                    ln.scalar_hi(eng, i, t, I[t % 2])
                eng.wait_ge(r_done.sem, r_done.at(i, 1))
                eng.activation(rT[:, :], H[0][0:16, :], ACT.Copy).then_inc(r_ready.sem, 1)
                for s in range(2, NU + 2):
                    u = s - 2
                    eng.wait_ge(t_done.sem, t_done.at(i, u + 1))
                    if u >= 2:
                        eng.wait_ge(o_done.sem, o_done.at(i, u - 1))
                    else:
                        eng.wait_ge(o_done.sem, o_done.before(i))
                    eng.activation(hh[:, u % 2, :], TP[u % 2][0:HK, :], ACT.Copy).then_inc(hh_ready.sem, 1)
                    if more and s == NORM + ST - 1:
                        ln.scalar_sd(eng, i + 1)

            ln.scalar_sd(eng, 0)
            with eng.Fori(0, NST - 1) as i:
                scalar_pass(i, True)
            scalar_pass(NST - 1, False)

        @block.gpsimd
        def _(eng):
            for n in range(2, len(pieces), ROOMS):
                low(eng, n)
            eng.wait_ge(small.sem, small.at(0, 48))
            with eng.Fori(0, NST) as i:
                for u in range(NU):
                    eng.wait_ge(eq_ready.sem, eq_ready.at(i, u + 1))
                    e = E1[:, u % 3, :, :]
                    eng.tensor_tensor(e, e, rank[:, :].unsqueeze(1).to_broadcast([P, QB, BLK]), ALU.mult)\
                       .then_inc(z_ready.sem, 1)

        @block.vector
        def _(eng):
            eng.wait_ge(w_hi.sem, w_hi.at(0, 1))
            eng.tensor_tensor(C1[1][:, :, :], c1room, C1[0][:, :, :].bitcast(F32), ALU.subtract)\
               .then_inc(c1_lo.sem, 1)
            for n in range(len(pieces)):
                if n % ROOMS < 2:
                    low(eng, n)
            all_split(eng)
            eng.wait_ge(c1_lo.sem, c1_lo.at(0, 1))
            def vector_pass(i, more):
                for t in range(ST):
                    ln.vector_lo(eng, i, t, I[t % 2])
                links = [0]

                def chain(ins):
                    links[0] += 1
                    ins.then_inc(vec.sem, 1)
                    return links[0]

                for s in range(NU + 5):
                    if s < NU:
                        eng.wait_ge(i_done.sem, i_done.at(i, s + 1))
                        src = I[s % 2][:, 0:QW].rearrange("p (b s) -> p b s", s=BLK)
                        n = chain(eng.reduce_max(bmax[:, s % 2, :], src, AX_X))
                        eng.wait_ge(vec.sem, vec.at(i, n))
                        eng.tensor_tensor(E1[:, s % 3, :, :], src,
                                          bmax[:, s % 2, :].unsqueeze(2).to_broadcast([P, QB, BLK]),
                                          ALU.is_equal).then_inc(eq_ready.sem, 1)
                    u = s - 1
                    if 0 <= u < NU:
                        e = E1[:, u % 3, :, :]
                        eng.wait_ge(z_ready.sem, z_ready.at(i, u + 1))
                        n = chain(eng.reduce_max(zmax[:, u % 2, :], e, AX_X))
                        eng.wait_ge(vec.sem, vec.at(i, n))
                        n = chain(eng.tensor_tensor(e, e, zmax[:, u % 2, :].unsqueeze(2)
                                                    .to_broadcast([P, QB, BLK]), ALU.is_equal))
                        eng.wait_ge(h_done.sem, h_done.at(i, u + 1))
                        if u >= 2:
                            eng.wait_ge(t_done.sem, t_done.at(i, u - 1))
                        else:
                            eng.wait_ge(t_done.sem, t_done.before(i))
                        eng.wait_ge(vec.sem, vec.at(i, n))
                        eng.scalar_tensor_tensor(HM[:, u % 2, :], H[u % 2][:, 0:QW], 0.0,
                                                 e.rearrange("p b s -> p (b s)"), ALU.max, ALU.mult)\
                           .then_inc(h_ready.sem, 1)
                    u = s - 3
                    if 0 <= u < NU:
                        eng.wait_ge(hh_ready.sem, hh_ready.at(i, u + 1))
                        eng.tensor_tensor(hl[:, u % 2, :], TP[u % 2][0:HK, :], hh[:, u % 2, :].bitcast(F32),
                                          ALU.subtract).then_inc(hl_ready.sem, 1)
                    if more and 0 <= s - NORM < ST:
                        ln.vector_stat(eng, i + 1, s - NORM)
                        if s - NORM == ST - 1:
                            ln.vector_var(eng, i + 1)
                    if more and 0 <= s - NORM - ST < ST:
                        ln.vector_xn(eng, i + 1, s - NORM - ST)
                    t = (s - 8) // NQ
                    if s - 8 == NQ * t and 0 <= t < ST - 1:
                        eng.wait_ge(o_done.sem, o_done.at(i, NQ * (t + 1)))
                        xt = x_tile(X, i, t)
                        eng.tensor_tensor(xt, xt, Y[t % 2][:, :], ALU.add).then_inc(y_added.sem, 1)
                eng.wait_ge(o_done.sem, o_done.before(i + 1))
                xt = x_tile(X, i, ST - 1)
                eng.tensor_tensor(xt, xt, Y[(ST - 1) % 2][:, :], ALU.add).then_inc(y_added.sem, 1)

            ln.vector_norm(eng, 0)
            with eng.Fori(0, NST - 1) as i:
                vector_pass(i, True)
            vector_pass(NST - 1, False)

        def second(eng, i, u):
            t, q = divmod(u, NQ)
            eng.wait_ge(hh_ready.sem, hh_ready.at(i, u + 1))
            eng.wait_ge(hl_ready.sem, hl_ready.at(i, u + 1))
            if q == 0:
                if t >= 2:
                    eng.wait_ge(y_added.sem, y_added.at(i, t - 1))
                else:
                    eng.wait_ge(y_added.sem, y_added.before(i))
            n = 0
            for j in range(4):
                h, l = hh[:, u % 2, j * P:(j + 1) * P], hl[:, u % 2, j * P:(j + 1) * P]
                w, v = W2[0][:, 4 * q + j, :], W2[1][:, 4 * q + j, :]
                for lhs, rhs in ((h, w), (h, v), (l, w)):
                    last = eng.matmul(Y[t % 2][:, :], lhs, rhs, start=(q == 0 and n == 0),
                                      stop=(q == NQ - 1 and n == 11))
                    n += 1
            last.then_inc(o_done.sem, 1)

        @block.tensor
        def _(eng):
            eng.wait_ge(small.sem, small.at(0, 48))
            eng.wait_ge(c1_lo.sem, c1_lo.at(0, 1))
            all_split(eng)
            with eng.Fori(0, NST) as i:
                for t in range(ST):
                    if t >= 2:
                        eng.wait_ge(ln.lo_ready.sem, ln.lo_ready.at(i, t - 1))
                    else:
                        eng.wait_ge(eq_ready.sem, eq_ready.before(i))
                    ln.tensor_turn(eng, i, t, I[t % 2])
                eng.wait_ge(ln.lo_ready.sem, ln.lo_ready.before(i + 1))
                eng.wait_ge(ln.hi_ready.sem, ln.hi_ready.before(i + 1))
                eng.wait_ge(h_ready.sem, h_ready.before(i))
                products(eng, H[0][0:16, :], [((C1[0][:, k, :], C1[1][:, k, :]),
                                            (ln.hi[:, k, :], ln.lo[:, k, :])) for k in range(KC)])\
                    .then_inc(r_done.sem, 1)
                eng.wait_ge(r_ready.sem, r_ready.at(i, 1))
                for s in range(NU + 4):
                    if s < NU:
                        t, q = divmod(s, NQ)
                        if s >= 2:
                            eng.wait_ge(eq_ready.sem, eq_ready.at(i, s - 1))
                        eng.matmul(I[s % 2][:, 0:QW], rT[:, t * P:(t + 1) * P], C2[:, q * QW:(q + 1) * QW],
                                   start=True, stop=True).then_inc(i_done.sem, 1)
                        if s >= 2:
                            eng.wait_ge(h_ready.sem, h_ready.at(i, s - 1))
                        products(eng, H[s % 2][:, 0:QW],
                                 [((ln.hi[:, k, t * P:(t + 1) * P], ln.lo[:, k, t * P:(t + 1) * P]),
                                   tuple(w[:, k, q * QW:(q + 1) * QW] for w in W1)) for k in range(KC)])\
                            .then_inc(h_done.sem, 1)
                    u = s - 2
                    if 0 <= u < NU:
                        eng.wait_ge(h_ready.sem, h_ready.at(i, u + 1))
                        if u >= 2:
                            eng.wait_ge(hl_ready.sem, hl_ready.at(i, u - 1))
                        else:
                            eng.wait_ge(hl_ready.sem, hl_ready.before(i))
                        for j in range(4):
                            last = eng.transpose(TP[u % 2][0:HK, j * P:(j + 1) * P],
                                                 HM[:, u % 2, j * HK:(j + 1) * HK], consts["ident"][:, :])
                        last.then_inc(t_done.sem, 1)
                    u = s - 4
                    if 0 <= u < NU:
                        second(eng, i, u)


NE = 8
RANK = 16
GW = 4 * NE
CAPACITY = 3 * TOK // NE


def lora_experts(nc, signals, X, consts, a):
    EW = NE * RANK
    with ExitStack() as ctx:
        mem = Memory(ctx, nc, "moe", signals)
        ident, ones, eps = consts["ident"], consts["ones"], consts["eps"]
        W = [mem.sb(f"W{n}", [P, KC, D], F32R) for n in range(2)]
        WA = [mem.sb(f"WA{n}", [P, KC, EW + GW], F32R) for n in range(2)]
        WB = [mem.sb(f"WB{n}", [P, D], F32R) for n in range(2)]
        rW, rA, rB = mem.sb("rW", [P, KC, D]), mem.sb("rA", [P, KC, EW + GW]), mem.sb("rB", [P, D])
        params = mem.sb("gate_params", [P, 3, GW])
        gb2 = mem.sb("gate_bias2", [P, NE])
        gw2 = mem.sb("gate_w2", [GW, NE])
        rank8 = mem.sb("expert_rank", [P, NE])
        ln = LayerNorm(mem, X, ident, eps)
        tmp = mem.sb("tmp", [P, TILES * EW])
        hg = mem.sb("gate_h", [P, TILES * GW])
        sq = mem.sb("gate_sq", [P, TILES, GW])
        m1, var, sd = mem.sb("g_mean", [P, TILES]), mem.sb("g_var", [P, TILES]), mem.sb("g_sd", [P, TILES])
        hT = mem.sb("gate_hT", [GW, TILES, P])
        g = mem.sb("gates", [P, TILES, NE])
        g2 = mem.sb("gates2", [P, TILES, NE])
        z = mem.sb("gate_z", [P, TILES, NE])
        oh = mem.sb("gate_one_hot", [P, 2, TILES, NE])
        v1, v2, zm = mem.sb("g_v1", [P, TILES]), mem.sb("g_v2", [P, TILES]), mem.sb("g_zm", [P, TILES])
        e, p1, p2 = mem.sb("g_e", [P, TILES]), mem.sb("g_p1", [P, TILES]), mem.sb("g_p2", [P, TILES])
        cnt = mem.sb("counts", [P, 2, NE])
        allowed = mem.sb("allowed", [P, 2, NE])
        wt = mem.sb("expert_weight", [P, TILES * NE])
        tw = mem.sb("tmp_weighted", [P, ST * EW])
        th = mem.sb("tmpT_hi", [P, STOK], F32R)
        tl = mem.sb("tmpT_lo", [P, STOK], F32R)
        B = [mem.ps(f"B{n}") for n in range(8)]
        splits = [(rW, W), (rA, WA), (rB, WB)]
        w_raw = mem.sig("weights_landed", 16 * 9, 1)
        w_hi = mem.sig("weights_hi", 3, 1)
        w_lo = mem.sig("weights_lo", 3, 1)
        y_done = mem.sig("y_product", ST)
        a_done = mem.sig("a_product", ST)
        a_kept = mem.sig("a_kept", 2 * ST)
        y_added = mem.sig("y_added", ST)
        NCHAIN = 35
        gch = mem.sig("gate_chain", NCHAIN, 1)
        g_act = mem.sig("gate_scalar", 1 + 4 + 1, 1)
        g_pe = mem.sig("gate_pe", 4 + 1 + 1, 1)
        tw_ready = mem.sig("weighted")
        tt_done = mem.sig("weighted_turned")
        th_ready = mem.sig("weighted_hi")
        tl_ready = mem.sig("weighted_lo")
        z_done = mem.sig("lora_product", ST)
        z_added = mem.sig("lora_added", ST)

        block = ctx.enter_context(nc.Block())

        @block.sync
        def _(eng):
            for dst, src in ((rW[:, :, :], a["moe_W"]), (rA[:, :, :], a["moe_A"]), (rB[:, :], a["moe_B"]),
                             (params[:, 0, :], a["L1_ffn_gb1"].partition_broadcast(P)),
                             (params[:, 1, :], a["L1_ffn_ln_gamma"].partition_broadcast(P)),
                             (params[:, 2, :], a["L1_ffn_ln_beta"].partition_broadcast(P)),
                             (gb2[:, :], a["L1_ffn_gb2"].partition_broadcast(P)),
                             (gw2[:, :], a["moe_gw2"]),
                             (rank8[:, :], a["expert_rank"].partition_broadcast(P))):
                eng.dma_start(dst, src).then_inc(w_raw.sem, 16)

        @block.gpsimd
        def _(eng):
            for n, (raw, w) in enumerate(splits):
                full = (slice(None),) * len(raw.shape)
                eng.wait_ge(w_hi.sem, w_hi.at(0, n + 1))
                eng.tensor_tensor(w[1][full], raw[full], w[0][full].bitcast(F32), ALU.subtract)\
                   .then_inc(w_lo.sem, 1)

        @block.scalar
        def _(eng):
            ln.scalar_sd(eng, 0)
            eng.wait_ge(w_raw.sem, w_raw.at(0, 16 * 9))
            for raw, w in splits:
                full = (slice(None),) * len(raw.shape)
                eng.activation(w[0][full], raw[full], ACT.Copy).then_inc(w_hi.sem, 1)
            def scalar_pass(i, more):
                for t in range(ST):
                    ln.scalar_hi(eng, i, t, B[t % 2])
                if more:
                    ln.scalar_sd(eng, i + 1)

            with eng.Fori(0, NST - 1) as i:
                scalar_pass(i, True)
            scalar_pass(NST - 1, False)
            eng.wait_ge(gch.sem, gch.at(0, 6))
            eng.activation(sd[:, :], var[:, :], ACT.Sqrt, bias=eps[:, 0:1], scale=1.0 / GW)\
               .then_inc(g_act.sem, 1)
            for n in range(4):
                eng.wait_ge(g_pe.sem, g_pe.at(0, n + 1))
                eng.activation(hT[:, 4 * n:4 * n + 4, :], B[n][0:GW, :].rearrange("p (t n) -> p t n", t=4),
                               ACT.Copy).then_inc(g_act.sem, 1)
            eng.wait_ge(gch.sem, gch.at(0, 24))
            eng.activation(e[:, :], v2[:, :], ACT.Exp).then_inc(g_act.sem, 1)
            with eng.Fori(0, NST) as i:
                eng.wait_ge(tt_done.sem, tt_done.at(i, 1))
                eng.wait_ge(z_done.sem, z_done.before(i))
                eng.activation(th[:, :], B[0][:, :], ACT.Copy).then_inc(th_ready.sem, 1)

        @block.vector
        def _(eng):
            def vector_pass(i, more):
                for t in range(ST):
                    ln.vector_lo(eng, i, t, B[t % 2])
                if more:
                    ln.vector_norm(eng, i + 1)
                for t in range(ST):
                    eng.wait_ge(a_done.sem, a_done.at(i, t + 1))
                    src = B[4 + t % 2]
                    eng.tensor_scalar(tmp[:, bass.ds((i * ST + t) * EW, EW)], src[:, 0:EW], 1.0 / RANK, None,
                                      ALU.mult).then_inc(a_kept.sem, 1)
                    eng.tensor_scalar(hg[:, bass.ds((i * ST + t) * GW, GW)], src[:, EW:EW + GW], 1.0, None,
                                      ALU.mult).then_inc(a_kept.sem, 1)
                    eng.wait_ge(y_done.sem, y_done.at(i, t + 1))
                    xt = x_tile(X, i, t)
                    eng.tensor_tensor(xt, xt, B[2 + t % 2][:, :], ALU.add).then_inc(y_added.sem, 1)

            ln.vector_norm(eng, 0)
            with eng.Fori(0, NST - 1) as i:
                vector_pass(i, True)
            vector_pass(NST - 1, False)
            eng.wait_ge(a_kept.sem, a_kept.before(NST))
            count = [0]

            def step(ins):
                count[0] += 1
                ins.then_inc(gch.sem, 1)
                eng.wait_ge(gch.sem, gch.at(0, count[0]))

            h = hg[:, :].rearrange("p (t n) -> p t n", n=GW)

            def over(x, n):
                return x.unsqueeze(2).to_broadcast([P, TILES, n])

            def par(n):
                return params[:, n, :].unsqueeze(1).to_broadcast([P, TILES, GW])

            step(eng.tensor_tensor(h, h, par(0), ALU.add))
            step(eng.reduce_sum(m1[:, :], h, AX_X))
            step(eng.tensor_scalar(m1[:, :], m1[:, :], 1.0 / GW, None, ALU.mult))
            step(eng.tensor_tensor(h, h, over(m1[:, :], GW), ALU.subtract))
            step(eng.tensor_tensor(sq[:, :, :], h, h, ALU.mult))
            step(eng.reduce_sum(var[:, :], sq[:, :, :], AX_X))
            eng.wait_ge(g_act.sem, g_act.at(0, 1))
            step(eng.reciprocal(m1[:, :], sd[:, :]))
            step(eng.tensor_tensor(h, h, over(m1[:, :], GW), ALU.mult))
            step(eng.tensor_tensor(h, h, par(1), ALU.mult))
            step(eng.tensor_tensor(h, h, par(2), ALU.add))
            step(eng.tensor_scalar(h, h, 0.0, None, ALU.max))
            assert count[0] == 11
            eng.wait_ge(g_pe.sem, g_pe.at(0, 5))
            step(eng.tensor_tensor(g[:, :, :], B[4][:, 0:TILES * NE].rearrange("p (t n) -> p t n", n=NE),
                                   gb2[:, :].unsqueeze(1).to_broadcast([P, TILES, NE]), ALU.add))
            ranks = rank8[:, :].unsqueeze(1).to_broadcast([P, TILES, NE])
            for n, (src, best) in enumerate(((g, v1), (g2, v2))):
                if n:
                    step(eng.scalar_tensor_tensor(g2[:, :, :], oh[:, 0, :, :], -3.0e38, g[:, :, :],
                                                  ALU.mult, ALU.add))
                step(eng.reduce_max(best[:, :], src[:, :, :], AX_X))
                step(eng.tensor_tensor(z[:, :, :], src[:, :, :], over(best[:, :], NE), ALU.is_equal))
                step(eng.tensor_tensor(z[:, :, :], z[:, :, :], ranks, ALU.mult))
                step(eng.reduce_max(zm[:, :], z[:, :, :], AX_X))
                step(eng.tensor_tensor(oh[:, n, :, :], z[:, :, :], over(zm[:, :], NE), ALU.is_equal))
            step(eng.tensor_tensor(v2[:, :], v2[:, :], v1[:, :], ALU.subtract))
            assert count[0] == 24, count[0]
            for n in range(2):
                step(eng.reduce_sum(cnt[:, n, :], oh[:, n, :, :].rearrange("p t n -> p n t"), AX_X))
            eng.wait_ge(g_act.sem, g_act.at(0, 6))
            step(eng.tensor_scalar(p1[:, :], e[:, :], 1.0, None, ALU.add))
            step(eng.reciprocal(p1[:, :], p1[:, :]))
            step(eng.tensor_tensor(p2[:, :], e[:, :], p1[:, :], ALU.mult))
            eng.wait_ge(g_pe.sem, g_pe.at(0, 6))
            step(eng.tensor_scalar(allowed[:, :, :], B[5][:, 0:2 * NE].rearrange("p (k n) -> p k n", n=NE),
                                   float(CAPACITY), None, ALU.is_le))
            w3 = wt[:, :].rearrange("p (t n) -> p t n", n=NE)
            for n, p in enumerate((p1, p2)):
                step(eng.tensor_tensor(oh[:, n, :, :], oh[:, n, :, :],
                                       allowed[:, n, :].unsqueeze(1).to_broadcast([P, TILES, NE]), ALU.mult))
                step(eng.tensor_tensor(oh[:, n, :, :], oh[:, n, :, :], over(p[:, :], NE), ALU.mult))
            step(eng.tensor_tensor(w3, oh[:, 0, :, :], oh[:, 1, :, :], ALU.add))
            assert count[0] == NCHAIN, count[0]
            with eng.Fori(0, NST) as i:
                eng.wait_ge(tt_done.sem, tt_done.before(i))
                eng.tensor_tensor(tw[:, :].rearrange("p (n r) -> p n r", r=RANK),
                                  tmp[:, bass.ds(i * ST * EW, ST * EW)].rearrange("p (n r) -> p n r", r=RANK),
                                  wt[:, bass.ds(i * ST * NE, ST * NE)].unsqueeze(2)
                                  .to_broadcast([P, ST * NE, RANK]), ALU.mult).then_inc(tw_ready.sem, 1)
                eng.wait_ge(th_ready.sem, th_ready.at(i, 1))
                eng.tensor_tensor(tl[:, :], B[0][:, :], th[:, :].bitcast(F32), ALU.subtract)\
                   .then_inc(tl_ready.sem, 1)
                for t in range(ST):
                    eng.wait_ge(z_done.sem, z_done.at(i, t + 1))
                    xt = x_tile(X, i, t)
                    eng.tensor_tensor(xt, xt, B[4 + t][:, :], ALU.add).then_inc(z_added.sem, 1)

        @block.tensor
        def _(eng):
            eng.wait_ge(w_hi.sem, w_hi.at(0, 3))
            eng.wait_ge(w_lo.sem, w_lo.at(0, 3))
            with eng.Fori(0, NST) as i:
                for t in range(ST):
                    if t >= 2:
                        eng.wait_ge(ln.lo_ready.sem, ln.lo_ready.at(i, t - 1))
                    else:
                        eng.wait_ge(ln.lo_ready.sem, ln.lo_ready.before(i))
                    ln.tensor_turn(eng, i, t, B[t % 2])
                eng.wait_ge(ln.hi_ready.sem, ln.hi_ready.before(i + 1))
                eng.wait_ge(ln.lo_ready.sem, ln.lo_ready.before(i + 1))
                for t in range(ST):
                    def xt(k):
                        return ln.hi[:, k, t * P:(t + 1) * P], ln.lo[:, k, t * P:(t + 1) * P]
                    if t >= 2:
                        eng.wait_ge(y_added.sem, y_added.at(i, t - 1))
                        eng.wait_ge(a_kept.sem, a_kept.at(i, 2 * (t - 1)))
                    else:
                        eng.wait_ge(y_added.sem, y_added.before(i))
                        eng.wait_ge(a_kept.sem, a_kept.before(i))
                    products(eng, B[4 + t % 2][:, 0:EW + GW],
                             [(xt(k), (WA[0][:, k, :], WA[1][:, k, :])) for k in range(KC)])\
                        .then_inc(a_done.sem, 1)
                    products(eng, B[2 + t % 2][:, :],
                             [(xt(k), (W[0][:, k, :], W[1][:, k, :])) for k in range(KC)])\
                        .then_inc(y_done.sem, 1)
            eng.wait_ge(gch.sem, gch.at(0, 11))
            eng.wait_ge(y_added.sem, y_added.before(NST))
            for n in range(4):
                for t in range(4):
                    at = (4 * n + t) * GW
                    last = eng.transpose(B[n][0:GW, t * P:(t + 1) * P], hg[:, at:at + GW], ident[:, :])
                last.then_inc(g_pe.sem, 1)
            eng.wait_ge(g_act.sem, g_act.at(0, 5))
            eng.wait_ge(w_raw.sem, w_raw.at(0, 16 * 9))
            for t in range(TILES):
                last = eng.matmul(B[4][:, t * NE:(t + 1) * NE], hT[:, t, :], gw2[:, :], start=True, stop=True)
            last.then_inc(g_pe.sem, 1)
            eng.wait_ge(gch.sem, gch.at(0, 26))
            eng.matmul(B[5][:, 0:2 * NE], ones[:, :], cnt[:, :, :].rearrange("p k n -> p (k n)"),
                       start=True, stop=True).then_inc(g_pe.sem, 1)
            with eng.Fori(0, NST) as i:
                eng.wait_ge(tw_ready.sem, tw_ready.at(i, 1))
                eng.wait_ge(tl_ready.sem, tl_ready.before(i))
                for t in range(ST):
                    last = eng.transpose(B[0][:, t * P:(t + 1) * P], tw[:, t * EW:(t + 1) * EW], ident[:, :])
                last.then_inc(tt_done.sem, 1)
                eng.wait_ge(th_ready.sem, th_ready.at(i, 1))
                eng.wait_ge(tl_ready.sem, tl_ready.at(i, 1))
                eng.wait_ge(z_added.sem, z_added.before(i))
                for t in range(ST):
                    products(eng, B[4 + t][:, :], [((th[:, t * P:(t + 1) * P], tl[:, t * P:(t + 1) * P]),
                                                    (WB[0][:, :], WB[1][:, :]))]).then_inc(z_done.sem, 1)


NG = 8
NH = 4
HALF = 2 * STOK
NHALF = TOK // HALF
RMS_EPS = 1e-5


def cross_attention(nc, signals, X, consts, a):
    ident, eps, ones = consts["ident"], consts["eps"], consts["ones"]
    NU = 2
    ROWS = 2 * NH
    PASSES = NHALF * NG
    NS = ST * NH
    UNITS = (1, 0, 3, 2)
    TURN = {n: k + 1 for k, n in enumerate(UNITS)}
    YT = (2, 3, 0, 1)
    with ExitStack() as ctx:
        mem = Memory(ctx, nc, "xat", signals)
        Wq = [mem.sb(f"Wq{n}", [P, KC, D], F32R) for n in range(2)]
        Wk = [mem.sb(f"Wk{n}", [P, KC, P], F32R) for n in range(2)]
        Wv = [mem.sb(f"Wv{n}", [P, KC, P], F32R) for n in range(2)]
        Wo = [mem.sb(f"Wo{n}", [P, NH, D], F32R) for n in range(2)]
        room = mem.sb("weights_raw", [P, KC * (D + 2 * P)])
        ch = mem.sb("ctxT_hi", [P, KC, HALF], F32R)
        cl = mem.sb("ctxT_lo", [P, KC, HALF], F32R)
        qT = mem.sb("qT", [P, NH, STOK])
        kT = mem.sb("kT", [P, STOK])
        krms = mem.sb("k_rms", [P, STOK])
        sq = mem.sb("squares", [P, 2, STOK])
        turn = mem.sb("vT_and_PT", [P, 2, STOK])
        V = mem.sb("V", [P, 2, SB, P])
        T = mem.sb("T", [P, 2 * NU, ROWS, SEQ])
        oh = mem.sb("oT_hi", [P, NH, STOK], F32R)
        ol = mem.sb("oT_lo", [P, NH, STOK], F32R)
        qrms = mem.sb("q_rms", [NS, P])
        rq = mem.sb("q_inv_rms", [P, 2, ST, NH])
        mx = mem.sb("row_max", [P, 2, ROWS])
        rs = mem.sb("row_sum", [P, 2, ROWS])
        ri = mem.sb("row_inv", [P, 2 * NU, ROWS])
        mask = mem.sb("mask", [P, SEQ])
        norms = mem.sb("norm_weights", [P, 3])
        sel = mem.sb("row_select", [P, NS, NS])
        ln = LayerNorm(mem, X, ident, eps, width=HALF, passes=2 * NHALF,
                       xn=T[:, :, :, :].rearrange("p u r s -> p (u r s)").rearrange("p (t d) -> p t d", d=D))
        craw = qT
        vT = turn[:, :, :].rearrange("p a n -> p (a n)").rearrange("p (b c s) -> p b c s", c=2, s=SEQ)
        PT = turn[:, :, :].rearrange("p u (j n) -> p u j n", j=4)
        G = [mem.ps(f"G{n}") for n in range(2)]
        S = [mem.ps(f"S{n}") for n in range(2)]
        TP = [mem.ps(f"TP{n}") for n in range(2)]
        OT = [mem.ps(f"OT{n}") for n in range(2)]
        Q = [TP[0], G[0], G[1], G[0]]
        O = [OT, G]

        raw_o = room[:, 0:NH * D].rearrange("p (k n) -> p k n", k=NH)
        raw_q = room[:, 0:KC * D].rearrange("p (k n) -> p k n", k=KC)
        raw_k = room[:, KC * D:KC * (D + P)].rearrange("p (k n) -> p k n", k=KC)
        raw_v = room[:, KC * (D + P):].rearrange("p (k n) -> p k n", k=KC)
        kvq = [(raw_k, Wk), (raw_v, Wv), (raw_q, Wq)]

        pre_dma = mem.sig("weights_landed", 16 * 3, 1)
        small = mem.sig("small_landed", 16 * 4, 1)
        pre_hi = mem.sig("weights_hi", 3, 1)
        pre_lo = mem.sig("weights_lo", 3, 1)
        pre = mem.sig("prologue_vector", 2, 1)

        def sig(name, per):
            return mem.sig(name, per, PASSES)

        ctx_landed = mem.sig("ctx_landed", 16, 2 * NHALF)
        ctx_hi = mem.sig("ctx_hi_ready", 1, 2 * NHALF)
        ctx_lo = mem.sig("ctx_lo_ready", 1, 2 * NHALF)
        wo_landed, wqkv_landed = sig("wo_landed", 16), sig("wqkv_landed", 48)
        wo_hi, wo_lo = sig("wo_hi", 1), sig("wo_lo", 1)
        wqkv_hi, wqkv_lo = sig("wqkv_hi", 3), sig("wqkv_lo", 3)
        k_done, v_done, q_done = sig("k_product", 2), sig("v_product", 2), sig("q_product", 2 * NH)
        ms_done = sig("sums_of_squares", 2 * (1 + NH))
        vt_done, rqt_done = sig("v_turned", 2), sig("q_rms_turned", 2)
        kr_ready, vt_ready, q_ready = sig("k_raw_ready", 2), sig("vT_ready", 2), sig("q_ready", 2 * NH)
        sq_ready = sig("squares_ready", 2 * (1 + NH))
        krms_ready, qrms_ready = sig("k_rms_ready", 2), sig("q_rms_ready", 2)
        kn_ready, rq_ready = sig("k_ready", 2), sig("q_inv_rms", 2)
        va_ready, vb_ready = sig("V_by_scalar", 2), sig("V_by_vector", 2)
        U = 2 * NU
        s_done, s_read, biased = sig("scores", U), sig("scores_read", U), sig("biased", U)
        sub_ready, exp_ready = sig("shifted", U), sig("exponentials", U)
        inv_ready, norm_ready = sig("inverse_sums", U), sig("probabilities", U)
        t_done, pt_ready, pv_done = sig("probs_turned", U), sig("PT_ready", U), sig("values_product", U)
        oh_ready, ol_ready = sig("oT_hi_ready", U), sig("oT_lo_ready", U)
        y_done, y_added = sig("y_product", 2 * ST), sig("y_added", 2 * ST)
        vec = sig("vector_chain", 2 + 2 * U)

        def load_kvq(eng, g, done):
            for dst, src in ((raw_k, a["Cq_k"]), (raw_v, a["Cq_v"]), (raw_q, a["Cq_q"])):
                n = dst.shape[1] * dst.shape[2]
                eng.dma_start(dst.rearrange("p k n -> p (k n)"), src[:, bass.ds(g * n, n)]).then_inc(done.sem, 16)

        def o_part(x, n, r):
            u = n % 2
            return x[:, r:NH:2, u * 2 * P:(u + 1) * 2 * P]

        def o_bank(n, r):
            return O[n % 2][r][:, :].rearrange("p (h n) -> p h n", h=2)

        block = ctx.enter_context(nc.Block())

        @block.sync
        def _(eng):
            for dst, src in ((norms[:, 0:2], a["C_norms"]), (sel[:, :, :].rearrange("p m k -> p (m k)"),
                                                             a["C_select"].partition_broadcast(P)),
                             (mask[0:SEQ, :], a["C_mask"]), (mask[SEQ:P, :], a["C_mask"])):
                eng.dma_start(dst, src).then_inc(small.sem, 16)
            load_kvq(eng, 0, pre_dma)
            with eng.Fori(0, NHALF) as hf:
                for st in range(2):
                    i = hf * 2 + st
                    if st == 0:
                        eng.wait_ge(s_done.sem, s_done.before(hf * NG))
                    else:
                        eng.wait_ge(ctx_lo.sem, ctx_lo.before(i))
                    eng.dma_start(craw[:, :, :], a["ctxT"][:, :, bass.ds(i * STOK, STOK)])\
                       .then_inc(ctx_landed.sem, 16)
                with eng.Fori(0, NG) as g:
                    j = hf * NG + g
                    eng.wait_ge(pre_lo.sem, pre_lo.at(0, 3))
                    eng.wait_ge(wqkv_lo.sem, wqkv_lo.before(j))
                    eng.dma_start(raw_o.rearrange("p k n -> p (k n)"), a["Cq_o"][:, bass.ds(g * NH * D, NH * D)])\
                       .then_inc(wo_landed.sem, 16)
                    eng.wait_ge(wo_lo.sem, wo_lo.at(j, 1))
                    load_kvq(eng, g + 1, wqkv_landed)

        @block.scalar
        def _(eng):
            eng.wait_ge(pre_dma.sem, pre_dma.at(0, 16 * 3))
            for raw, w in kvq:
                eng.activation(w[0][:, :, :], raw, ACT.Copy).then_inc(pre_hi.sem, 1)
            with eng.Fori(0, NHALF) as hf:
                def keep_context(st):
                    i = hf * 2 + st
                    eng.wait_ge(ctx_landed.sem, ctx_landed.at(i, 16))
                    eng.activation(ch[:, :, st * STOK:(st + 1) * STOK], craw[:, :, :], ACT.Copy)\
                       .then_inc(ctx_hi.sem, 1)

                for st in range(2):
                    i = hf * 2 + st
                    ln.off = st * STOK
                    ln.scalar_sd(eng, i)
                    if st == 0:
                        keep_context(0)
                    for t in range(ST):
                        ln.scalar_hi(eng, i, t, S[t % 2])
                keep_context(1)
                with eng.Fori(0, NG) as g:
                    j = hf * NG + g

                    def square(st, n, src):
                        m = st * (1 + NH) + n
                        eng.wait_ge(ms_done.sem, ms_done.at(j, m - 1) if m >= 2 else ms_done.before(j))
                        eng.activation(sq[:, m % 2, :], src, ACT.Square).then_inc(sq_ready.sem, 1)

                    def project(st):
                        eng.wait_ge(k_done.sem, k_done.at(j, st + 1))
                        eng.activation(kT[:, :], G[0][:, :], ACT.Copy).then_inc(kr_ready.sem, 1)
                        square(st, 0, G[0][:, :])
                        eng.wait_ge(v_done.sem, v_done.at(j, st + 1))
                        src = G[1][:, :].rearrange("p (b s) -> p b s", s=SEQ)
                        eng.activation(vT[:, :, 0, :], src, ACT.Copy)
                        eng.activation(vT[:, :, 1, :], src, ACT.Copy).then_inc(vt_ready.sem, 1)
                        for h in range(NH):
                            if st == 1 and h < NU:
                                exponent(h)
                            bank = Q[h]
                            eng.wait_ge(q_done.sem, q_done.at(j, st * NH + h + 1))
                            eng.activation(qT[:, h, :], bank[:, :], ACT.Copy).then_inc(q_ready.sem, 1)
                            square(st, h + 1, bank[:, :])
                            if h == 1:
                                eng.wait_ge(ms_done.sem, ms_done.at(j, st * (1 + NH) + 1))
                                eng.activation(krms[:, :], OT[0][:, :], ACT.Sqrt, bias=eps[:, 0:1],
                                               scale=1.0 / P).then_inc(krms_ready.sem, 1)
                                eng.wait_ge(vt_done.sem, vt_done.at(j, st + 1))
                                eng.activation(V[:, st, 0:4, :], TP[0][:, :].rearrange("p (b d) -> p b d", d=P),
                                               ACT.Copy).then_inc(va_ready.sem, 1)
                        if st == 1:
                            keep_PT(0)
                            keep_PT(1)
                        eng.wait_ge(ms_done.sem, ms_done.at(j, (st + 1) * (1 + NH)))
                        eng.activation(qrms[:, :], OT[1][0:NS, 0:P], ACT.Sqrt, bias=eps[0:NS, 0:1],
                                       scale=1.0 / P).then_inc(qrms_ready.sem, 1)

                    def exponent(n):
                        eng.wait_ge(sub_ready.sem, sub_ready.at(j, n + 1))
                        eng.activation(T[:, n, :, :], T[:, n, :, :], ACT.Exp).then_inc(exp_ready.sem, 1)

                    def keep_PT(n):
                        eng.wait_ge(t_done.sem, t_done.at(j, n + 1))
                        bank = (TP if n < NU else S)[n % 2]
                        eng.activation(PT[:, n % 2, :, :], bank[:, :].rearrange("p (c n) -> p c n", c=4),
                                       ACT.Copy).then_inc(pt_ready.sem, 1)

                    def keep_oT(n):
                        eng.wait_ge(pv_done.sem, pv_done.at(j, TURN[n]))
                        if n >= NU:
                            eng.wait_ge(y_done.sem, y_done.at(j, 2 * (TURN[n] - NU)))
                        for r in range(2):
                            last = eng.activation(o_part(oh, n, r), o_bank(n, r), ACT.Copy)
                        last.then_inc(oh_ready.sem, 1)

                    def keep_hi(n):
                        raw, w = kvq[n]
                        eng.activation(w[0][:, :, :], raw, ACT.Copy).then_inc(wqkv_hi.sem, 1)

                    project(0)
                    eng.wait_ge(wo_landed.sem, wo_landed.at(j, 16))
                    eng.wait_ge(y_done.sem, y_done.before(j))
                    eng.activation(Wo[0][:, :, :], raw_o, ACT.Copy).then_inc(wo_hi.sem, 1)
                    project(1)
                    keep_oT(1)
                    keep_oT(0)
                    exponent(2)
                    eng.wait_ge(wqkv_landed.sem, wqkv_landed.at(j, 48))
                    eng.wait_ge(q_done.sem, q_done.at(j, 2 * NH))
                    keep_hi(0)
                    exponent(3)
                    keep_hi(1)
                    keep_PT(2)
                    keep_PT(3)
                    keep_oT(3)
                    keep_oT(2)
                    keep_hi(2)

        @block.gpsimd
        def _(eng):
            eng.wait_ge(small.sem, small.at(0, 16 * 4))
            for n, (raw, w) in enumerate(kvq):
                eng.wait_ge(pre_hi.sem, pre_hi.at(0, n + 1))
                eng.tensor_tensor(w[1][:, :, :], raw, w[0][:, :, :].bitcast(F32), ALU.subtract)\
                   .then_inc(pre_lo.sem, 1)
            with eng.Fori(0, NHALF) as hf:
                for st in range(2):
                    i = hf * 2 + st
                    at = slice(st * STOK, (st + 1) * STOK)
                    eng.wait_ge(ctx_hi.sem, ctx_hi.at(i, 1))
                    eng.tensor_tensor(cl[:, :, at], craw[:, :, :], ch[:, :, at].bitcast(F32), ALU.subtract)\
                       .then_inc(ctx_lo.sem, 1)
                with eng.Fori(0, NG) as g:
                    j = hf * NG + g

                    def bias(n):
                        eng.wait_ge(s_read.sem, s_read.at(j, n + 1))
                        eng.tensor_tensor(T[:, n, :, :], T[:, n, :, :],
                                          mask[:, :].unsqueeze(1).to_broadcast([P, ROWS, SEQ]), ALU.add)\
                           .then_inc(biased.sem, 1)

                    def normalize(n):
                        eng.wait_ge(inv_ready.sem, inv_ready.at(j, n + 1))
                        eng.tensor_tensor(T[:, n, :, :], T[:, n, :, :],
                                          ri[:, n, :].unsqueeze(2).to_broadcast([P, ROWS, SEQ]), ALU.mult)\
                           .then_inc(norm_ready.sem, 1)

                    def low(n):
                        raw, w = kvq[n]
                        eng.wait_ge(wqkv_hi.sem, wqkv_hi.at(j, n + 1))
                        eng.tensor_tensor(w[1][:, :, :], raw, w[0][:, :, :].bitcast(F32), ALU.subtract)\
                           .then_inc(wqkv_lo.sem, 1)

                    bias(0)
                    bias(1)
                    normalize(0)
                    normalize(1)
                    eng.wait_ge(wo_hi.sem, wo_hi.at(j, 1))
                    eng.tensor_tensor(Wo[1][:, :, :], raw_o, Wo[0][:, :, :].bitcast(F32), ALU.subtract)\
                       .then_inc(wo_lo.sem, 1)
                    bias(2)
                    bias(3)
                    low(0)
                    normalize(2)
                    normalize(3)
                    low(1)
                    low(2)

        @block.vector
        def _(eng):
            eng.wait_ge(small.sem, small.at(0, 16 * 4))
            eng.tensor_tensor(norms[:, 2:3], norms[:, 0:1], norms[:, 1:2], ALU.mult).then_inc(pre.sem, 1)
            eng.wait_ge(pre.sem, pre.at(0, 1))
            eng.tensor_scalar(norms[:, 2:3], norms[:, 2:3], float(P) ** -0.5, None, ALU.mult)\
               .then_inc(pre.sem, 1)
            eng.wait_ge(pre.sem, pre.at(0, 2))
            with eng.Fori(0, NHALF) as hf:
                for st in range(2):
                    ln.off = st * STOK
                    if st == 0:
                        eng.wait_ge(t_done.sem, t_done.before(hf * NG))
                    ln.vector_norm(eng, hf * 2 + st)
                    for t in range(ST):
                        ln.vector_lo(eng, hf * 2 + st, t, S[t % 2])
                with eng.Fori(0, NG) as g:
                    j = hf * NG + g
                    links = [0]

                    def chain(ins):
                        links[0] += 1
                        ins.then_inc(vec.sem, 1)
                        eng.wait_ge(vec.sem, vec.at(j, links[0]))

                    def norm_k(st):
                        eng.wait_ge(krms_ready.sem, krms_ready.at(j, st + 1))
                        eng.wait_ge(kr_ready.sem, kr_ready.at(j, st + 1))
                        chain(eng.reciprocal(krms[:, :], krms[:, :]))
                        eng.scalar_tensor_tensor(kT[:, :], kT[:, :], norms[:, 2:3], krms[:, :],
                                                 ALU.mult, ALU.mult).then_inc(kn_ready.sem, 1)

                    def keep_V(st):
                        eng.wait_ge(vt_done.sem, vt_done.at(j, st + 1))
                        eng.tensor_copy(V[:, st, 4:8, :], TP[1][:, :].rearrange("p (b d) -> p b d", d=P))\
                           .then_inc(vb_ready.sem, 1)

                    def invert_q(st):
                        eng.wait_ge(rqt_done.sem, rqt_done.at(j, st + 1))
                        eng.reciprocal(rq[:, st, :, :], OT[0][:, 0:NS].rearrange("p (t h) -> p t h", h=NH))\
                           .then_inc(rq_ready.sem, 1)

                    def take_scores(n):
                        st, u = divmod(n, NU)
                        eng.wait_ge(s_done.sem, s_done.at(j, n + 1))
                        eng.wait_ge(rq_ready.sem, rq_ready.at(j, st + 1))
                        scale = rq[:, st, 2 * u:2 * u + 2, :].rearrange("p t h -> p (t h)")
                        eng.tensor_tensor(T[:, n, :, :], S[u][:, :].rearrange("p (r s) -> p r s", s=SEQ),
                                          scale.unsqueeze(2).to_broadcast([P, ROWS, SEQ]), ALU.mult)\
                           .then_inc(s_read.sem, 1)

                    def shift(n):
                        eng.wait_ge(biased.sem, biased.at(j, n + 1))
                        chain(eng.reduce_max(mx[:, n % 2, :], T[:, n, :, :], AX_X))
                        eng.tensor_tensor(T[:, n, :, :], T[:, n, :, :],
                                          mx[:, n % 2, :].unsqueeze(2).to_broadcast([P, ROWS, SEQ]),
                                          ALU.subtract).then_inc(sub_ready.sem, 1)

                    def invert(n):
                        eng.wait_ge(exp_ready.sem, exp_ready.at(j, n + 1))
                        chain(eng.reduce_sum(rs[:, n % 2, :], T[:, n, :, :], AX_X))
                        eng.reciprocal(ri[:, n, :], rs[:, n % 2, :]).then_inc(inv_ready.sem, 1)

                    def low_oT(n):
                        eng.wait_ge(oh_ready.sem, oh_ready.at(j, TURN[n]))
                        for r in range(2):
                            last = eng.tensor_tensor(o_part(ol, n, r), o_bank(n, r), o_part(oh, n, r).bitcast(F32),
                                                     ALU.subtract)
                        last.then_inc(ol_ready.sem, 1)

                    def add_y(m):
                        eng.wait_ge(y_done.sem, y_done.at(j, m + 1))
                        if m == 0:
                            eng.wait_ge(y_added.sem, y_added.before(j))
                        xt = x_tile(X, hf * 2 + m // ST, YT[m % ST])
                        eng.tensor_tensor(xt, xt, TP[m % 2][:, :], ALU.add).then_inc(y_added.sem, 1)

                    norm_k(0)
                    keep_V(0)
                    invert_q(0)
                    take_scores(0)
                    take_scores(1)
                    shift(0)
                    shift(1)
                    invert(0)
                    invert(1)
                    norm_k(1)
                    keep_V(1)
                    invert_q(1)
                    take_scores(2)
                    low_oT(1)
                    take_scores(3)
                    shift(2)
                    low_oT(0)
                    shift(3)
                    add_y(0)
                    invert(2)
                    add_y(1)
                    invert(3)
                    add_y(2)
                    add_y(3)
                    low_oT(3)
                    low_oT(2)
                    for m in range(ST, 2 * ST):
                        add_y(m)
                    assert links[0] == vec.per, links[0]

        @block.tensor
        def _(eng):
            eng.wait_ge(small.sem, small.at(0, 16 * 4))
            with eng.Fori(0, NHALF) as hf:
                for st in range(2):
                    i = hf * 2 + st
                    for t in range(ST):
                        if t >= 2:
                            eng.wait_ge(ln.lo_ready.sem, ln.lo_ready.at(i, t - 1))
                        else:
                            eng.wait_ge(ln.lo_ready.sem, ln.lo_ready.before(i))
                            eng.wait_ge(s_read.sem, s_read.before(hf * NG))
                        ln.tensor_turn(eng, i, t, S[t % 2])
                with eng.Fori(0, NG) as g:
                    j = hf * NG + g

                    def x_part(st, k):
                        at = slice(st * STOK, (st + 1) * STOK)
                        return ln.hi[:, k, at], ln.lo[:, k, at]

                    def c_part(st, k):
                        at = slice(st * STOK, (st + 1) * STOK)
                        return ch[:, k, at], cl[:, k, at]

                    def project(st):
                        if st == 0:
                            eng.wait_ge(ln.hi_ready.sem, ln.hi_ready.before(hf * 2 + 2))
                            eng.wait_ge(ln.lo_ready.sem, ln.lo_ready.before(hf * 2 + 2))
                            eng.wait_ge(ctx_lo.sem, ctx_lo.before(hf * 2 + 1))
                            eng.wait_ge(pre_lo.sem, pre_lo.at(0, 3))
                            eng.wait_ge(wqkv_lo.sem, wqkv_lo.before(j))
                            eng.wait_ge(ol_ready.sem, ol_ready.before(j))
                        else:
                            eng.wait_ge(sq_ready.sem, sq_ready.at(j, 1 + NH))
                            eng.wait_ge(q_ready.sem, q_ready.at(j, NH))
                        products(eng, G[0][:, :], [((Wk[0][:, k, :], Wk[1][:, k, :]), c_part(st, k))
                                                   for k in range(KC)]).then_inc(k_done.sem, 1)
                        products(eng, G[1][:, :], [((Wv[0][:, k, :], Wv[1][:, k, :]), c_part(st, k))
                                                   for k in range(KC)]).then_inc(v_done.sem, 1)

                        def head(h):
                            if h == 0:
                                if st == 0:
                                    eng.wait_ge(ctx_lo.sem, ctx_lo.before(hf * 2 + 2))
                                    eng.wait_ge(y_added.sem, y_added.before(j))
                                eng.wait_ge(va_ready.sem, va_ready.at(j, st))
                            elif h == 1:
                                eng.wait_ge(kr_ready.sem, kr_ready.at(j, st + 1))
                                eng.wait_ge(sq_ready.sem, sq_ready.at(j, st * (1 + NH) + 1))
                            elif h == 2:
                                eng.wait_ge(vt_ready.sem, vt_ready.at(j, st + 1))
                            else:
                                eng.wait_ge(q_ready.sem, q_ready.at(j, st * NH + 2))
                                eng.wait_ge(sq_ready.sem, sq_ready.at(j, st * (1 + NH) + 3))
                            products(eng, Q[h][:, :],
                                     [(tuple(w[:, k, h * P:(h + 1) * P] for w in Wq), x_part(st, k))
                                      for k in range(KC)]).then_inc(q_done.sem, 1)

                        def q_squares(h):
                            eng.wait_ge(sq_ready.sem, sq_ready.at(j, st * (1 + NH) + h + 2))
                            if h == 0:
                                eng.wait_ge(qrms_ready.sem, qrms_ready.at(j, st))
                            src = sq[:, (st * (1 + NH) + h + 1) % 2, :]
                            for t in range(ST):
                                last = eng.matmul(OT[1][0:NS, 0:P], sel[:, t * NH + h, :], src[:, t * P:(t + 1) * P],
                                                  start=(h == 0 and t == 0), stop=(h == NH - 1 and t == ST - 1))
                            last.then_inc(ms_done.sem, 1)

                        head(0)
                        eng.wait_ge(sq_ready.sem, sq_ready.at(j, st * (1 + NH) + 1))
                        eng.wait_ge(rq_ready.sem, rq_ready.at(j, st))
                        eng.matmul(OT[0][:, :], ones[:, :], sq[:, (st * (1 + NH)) % 2, :], start=True, stop=True)\
                           .then_inc(ms_done.sem, 1)
                        head(1)
                        q_squares(0)
                        eng.wait_ge(q_ready.sem, q_ready.at(j, st * NH + 1))
                        eng.wait_ge(va_ready.sem, va_ready.at(j, st))
                        eng.wait_ge(vb_ready.sem, vb_ready.at(j, st))
                        for b in range(SB):
                            last = eng.transpose(TP[b // 4][:, (b % 4) * P:(b % 4 + 1) * P],
                                                 vT[:, b, :, :].rearrange("p c s -> p (c s)"), ident[:, :])
                        last.then_inc(vt_done.sem, 1)
                        head(2)
                        q_squares(1)
                        head(3)
                        q_squares(2)
                        if st == 1:
                            turn_probs(0)
                            turn_probs(1)
                            q_squares(3)
                            scores(2)
                            turn_rms(1)
                            values(1)
                            scores(3)
                            values(0)
                        else:
                            scores(0)
                            q_squares(3)
                            scores(1)
                            turn_rms(0)

                    def turn_rms(st):
                        eng.wait_ge(krms_ready.sem, krms_ready.at(j, st + 1))
                        eng.wait_ge(qrms_ready.sem, qrms_ready.at(j, st + 1))
                        eng.matmul(OT[0][:, 0:NS], qrms[:, :], ident[0:NS, 0:NS], start=True, stop=True)\
                           .then_inc(rqt_done.sem, 1)

                    def scores(n):
                        st, u = divmod(n, NU)
                        eng.wait_ge(q_ready.sem, q_ready.at(j, (st + 1) * NH))
                        eng.wait_ge(kn_ready.sem, kn_ready.at(j, st + 1))
                        if st == 0:
                            eng.wait_ge(s_read.sem, s_read.before(j))
                            eng.wait_ge(pt_ready.sem, pt_ready.before(j))
                        else:
                            eng.wait_ge(s_read.sem, s_read.at(j, n - 1))
                        for t in range(2):
                            for h in range(NH):
                                for b in range(2):
                                    tok = (2 * u + t) * P + b * SEQ
                                    at = (t * NH + h) * SEQ
                                    last = eng.matmul(S[u][b * SEQ:(b + 1) * SEQ, at:at + SEQ],
                                                      qT[:, h, tok:tok + SEQ], kT[:, tok:tok + SEQ],
                                                      start=True, stop=True)
                        last.then_inc(s_done.sem, 1)

                    def turn_probs(n):
                        eng.wait_ge(norm_ready.sem, norm_ready.at(j, n + 1))
                        if n < NU:
                            eng.wait_ge(va_ready.sem, va_ready.at(j, 2))
                            eng.wait_ge(vb_ready.sem, vb_ready.at(j, 2))
                        else:
                            eng.wait_ge(s_read.sem, s_read.at(j, n + 1))
                        bank = (TP if n < NU else S)[n % 2]
                        for c in range(4):
                            last = eng.transpose(bank[:, c * P:(c + 1) * P],
                                                 T[:, n, 2 * c:2 * c + 2, :].rearrange("p r s -> p (r s)"),
                                                 ident[:, :])
                        last.then_inc(t_done.sem, 1)

                    def values(n):
                        st, u = divmod(n, NU)
                        eng.wait_ge(pt_ready.sem, pt_ready.at(j, n + 1))
                        if n == 1:
                            eng.wait_ge(q_ready.sem, q_ready.at(j, 2 * NH))
                            eng.wait_ge(sq_ready.sem, sq_ready.at(j, 2 * (1 + NH)))
                        elif n == 0:
                            eng.wait_ge(rq_ready.sem, rq_ready.at(j, 2))
                            eng.wait_ge(qrms_ready.sem, qrms_ready.at(j, 2))
                        else:
                            eng.wait_ge(ol_ready.sem, ol_ready.at(j, TURN[n] - 2))
                        for t in range(2):
                            for b in range(2):
                                seq = (2 * u + t) * 2 + b
                                at = t * P + b * SEQ
                                for r in range(2):
                                    rows = slice(r * SEQ, (r + 1) * SEQ)
                                    last = eng.matmul(
                                        o_bank(n, r)[:, :, at:at + SEQ], V[rows, st, seq, :],
                                        PT[rows, u, 2 * t:2 * t + 2, b * SEQ:(b + 1) * SEQ],
                                        start=True, stop=True)
                        last.then_inc(pv_done.sem, 1)

                    def output(m):
                        st, t = m // ST, YT[m % ST]
                        n = TURN[st * NU + t // 2]
                        eng.wait_ge(oh_ready.sem, oh_ready.at(j, n))
                        eng.wait_ge(ol_ready.sem, ol_ready.at(j, n))
                        if m < 2:
                            eng.wait_ge(pt_ready.sem, pt_ready.at(j, m + 1))
                        else:
                            eng.wait_ge(y_added.sem, y_added.at(j, m - 1))
                        products(eng, TP[m % 2][:, :],
                                 [((oh[:, h, t * P:(t + 1) * P], ol[:, h, t * P:(t + 1) * P]),
                                   (Wo[0][:, h, :], Wo[1][:, h, :])) for h in range(NH)])\
                            .then_inc(y_done.sem, 1)

                    project(0)
                    project(1)
                    eng.wait_ge(wo_lo.sem, wo_lo.at(j, 1))
                    output(0)
                    output(1)
                    output(2)
                    turn_probs(2)
                    turn_probs(3)
                    output(3)
                    values(3)
                    values(2)
                    for m in range(ST, 2 * ST):
                        output(m)


def more_arrays(v):
    c1 = v["L0_ffn_c1_w"].T
    lora = v["L1_ffn_lora_A"].transpose(1, 0, 2).reshape(D, NE * RANK)
    wq = v["L0_xattn_Wq"].reshape(NG, NH * P, D)
    wk, wv = v["L0_xattn_Wk"].reshape(NG, P, D), v["L0_xattn_Wv"].reshape(NG, P, D)
    wo = v["L0_xattn_Wo"].T.reshape(NG, NH * P, D)
    order = list(range(NG)) + [0]
    return {
        "Cq_q": np.concatenate([lay(wq[g].T).reshape(P, -1) for g in order], axis=1),
        "Cq_k": np.concatenate([lay(wk[g].T).reshape(P, -1) for g in order], axis=1),
        "Cq_v": np.concatenate([lay(wv[g].T).reshape(P, -1) for g in order], axis=1),
        "Cq_o": np.concatenate([lay(wo[g]).reshape(P, -1) for g in range(NG)], axis=1),
        "C_norms": np.stack([v["L0_xattn_q_norm_w"], v["L0_xattn_k_norm_w"]], axis=1),
        "C_select": np.eye(ST * NH, dtype=np.float32).reshape(-1),
        "C_mask": v["mask_1x1xSxS2_ff0"].reshape(SEQ, SEQ),
        "w1T": lay(v["L0_ffn_w1"].T), "c1T": lay(c1), "c2T": v["L0_ffn_c2_w"].T,
        "w2": v["L0_ffn_w2t"].reshape(INTER // HK, HK, D).transpose(1, 0, 2),
        "block_rank": np.arange(BLK, 0, -1).astype(np.float32),
        "expert_rank": np.arange(NE, 0, -1).astype(np.float32),
        "moe_W": lay(v["L1_ffn_weight"].T),
        "moe_A": lay(np.concatenate([lora, v["L1_ffn_gw1"].T], axis=1)),
        "moe_B": v["L1_ffn_lora_B"].reshape(NE * RANK, D), "moe_gw2": v["L1_ffn_gw2"].T,
        "L1_ffn_gb1": v["L1_ffn_gb1"], "L1_ffn_ln_gamma": v["L1_ffn_ln_gamma"],
        "L1_ffn_ln_beta": v["L1_ffn_ln_beta"], "L1_ffn_gb2": v["L1_ffn_gb2"],
    }


def lay(a):
    k, n = a.shape
    return np.ascontiguousarray(a.reshape(k // P, P, n).transpose(1, 0, 2))


def alibi_table():
    slopes = (2.0 ** (-2.0 ** (-(5 - 3)))) ** np.arange(1, 33, dtype=np.float64)
    slopes = slopes.astype(np.float32)
    q, k = np.arange(SEQ)[:, None, None], np.arange(SEQ)[None, None, :]
    t = slopes[None, :, None] * (k - q).astype(np.float32)
    t = np.where(k <= q, t, np.float32(-1e30)).astype(np.float32)
    return np.ascontiguousarray(t.reshape(SEQ, KC, CH, SEQ))


def head_scales(a):
    a = np.asarray(a).reshape(KC, 2, 1, HD)
    return np.ascontiguousarray(np.broadcast_to(a, (KC, 2, 4, HD)).reshape(KC, P).T)


def per_query_head(wt):
    heads = wt.shape[1] // HD
    reps = 4 if heads > 1 else CH
    a = wt.reshape(D, heads, 1, HD)
    return np.broadcast_to(a, (D, heads, reps, HD)).reshape(D, heads * reps * HD)


SIGNALS = (
    "biased",
    "row_max_ready",
    "shifted_by_pool",
    "small_landed",
    "weight_landed_0",
    "weight_landed_1",
    "weight_landed_2",
    "weight_landed_3",
    "room_landed_0",
    "room_split_0",
    "room_landed_1",
    "room_split_1",
    "room_landed_2",
    "room_split_2",
    "ln_stat",
    "ln_sd_ready",
    "xn_ready",
    "xn_turned",
    "xnT_hi_ready",
    "xnT_lo_ready",
    "weights_landed",
    "weights_hi",
    "weights_abs",
    "weights_lo",
    "weights_lo_by_vector",
    "weights_summed",
    "prologue_vector",
    "prologue_pool",
    "prologue_pe",
    "q_product",
    "q_ready",
    "k_product",
    "krep_ready",
    "kbd_by_pool",
    "kbd_by_vector",
    "v_product",
    "v_ready",
    "scores",
    "scores_read",
    "vector_chain",
    "shifted",
    "exponentials",
    "inverse_sums",
    "probabilities",
    "probs_turned",
    "PT_ready",
    "values_product",
    "oT_hi_ready",
    "oT_lo_ready",
    "y_product",
    "y_added",
    "ctx_landed",
    "ctx_hi_ready",
    "ctx_lo_ready",
    "r_product",
    "r_ready",
    "rank_product",
    "h_product",
    "is_block_max",
    "ranked",
    "h_kept",
    "h_turned",
    "hT_hi_ready",
    "hT_lo_ready",
    "h_used",
    "a_product",
    "a_kept",
    "gate_chain",
    "gate_scalar",
    "gate_pe",
    "weighted",
    "weighted_turned",
    "weighted_hi",
    "weighted_lo",
    "lora_product",
    "lora_added",
    "wo_landed",
    "wqkv_landed",
    "wo_hi",
    "wo_lo",
    "wqkv_hi",
    "wqkv_lo",
    "sums_of_squares",
    "v_turned",
    "q_rms_turned",
    "k_raw_ready",
    "vT_ready",
    "squares_ready",
    "k_rms_ready",
    "q_rms_ready",
    "k_ready",
    "q_inv_rms",
    "V_by_scalar",
    "V_by_vector",
)


def load_constants(nc, signals, X, consts, dram):
    with (nc.semaphore("constants_landed") as landed, nc.semaphore("constants_made") as made,
          nc.Block() as block):
        @block.sync
        def _(eng):
            eng.dma_start(X[:, :].rearrange("p (t d) -> p t d", d=D),
                          dram["x"].rearrange("(t p) d -> p t d", p=P)).then_inc(landed, 16)
            eng.dma_start(consts["ident"][:, :], dram["ident"]).then_inc(landed, 16)
            eng.dma_start(consts["headmask"][:, :], dram["headmask"]).then_inc(landed, 16)
            eng.wait_ge(landed, 48)

        @block.vector
        def _(eng):
            eng.memset(consts["eps"][:, :], LN_EPS).then_inc(made, 1)
            eng.memset(consts["ones"][:, :], 1.0).then_inc(made, 1)
            eng.wait_ge(made, 2)

        @block.gpsimd
        def _(eng):
            for sem in signals.sems.values():
                eng.sem_inc(sem, 1)


def store_result(nc, X, out):
    with nc.semaphore("result_stored") as stored, nc.Block() as block:
        @block.sync
        def _(eng):
            eng.dma_start(out.rearrange("(t p) d -> p t d", p=P),
                          X[:, :].rearrange("p (t d) -> p t d", d=D)).then_inc(stored, 16)
            eng.wait_ge(stored, 16)


def decoder(nc, a, out):
    with ExitStack() as ctx:
        signals = Signals(ctx, nc, SIGNALS)

        def sb(name, shape):
            return ctx.enter_context(nc.sbuf_tensor(name, shape, F32))

        X = sb("X", [P, TILES * D])
        consts = {"ident": sb("ident", [P, P]), "headmask": sb("headmask", [P, CH]),
                  "eps": sb("eps", [P, 1]), "ones": sb("ones", [P, P])}
        load_constants(nc, signals, X, consts, a)
        small_attention(nc, signals, "sign", X, consts,
                        {"q": a["L0q"], "k": a["L0k"], "v": a["L0v"], "o": a["L0o"],
                         "scales": a["L0scales"], "v_rep": a["L0v_rep"], "o_scale": a["L0_attn_o_scale"]}, "gqa")
        cross_attention(nc, signals, X, consts, a)
        sparse_ffn(nc, signals, X, consts, a)
        small_attention(nc, signals, "alibi", X, consts,
                        {"q": a["L1q"], "k": a["L1k"], "v": a["L1v"], "o": a["L1o"],
                         "alibi": a["alibi"]}, "mqa")
        small_attention(nc, signals, "cross", X, consts,
                        {"q": a["Xq"], "k": a["Xk"], "v": a["Xv"], "o": a["Xo"],
                         "ctxT": a["ctxT"], "mask": a["mask_SxS2_bk0"]}, "cga")
        lora_experts(nc, signals, X, consts, a)
        store_result(nc, X, out)


def kernel(**inputs):
    import concourse.bacc as _bacc
    from concourse.bass_utils import run_bass_kernel_spmd as _run

    v = {k: np.asarray(x) for k, x in inputs.items()}
    w = v["L1_attn_Wqkv"]
    arrays = {
        "x": v["x"].reshape(TOK, D),
        "ident": np.eye(P, dtype=np.float32),
        "headmask": np.kron(np.eye(CH, dtype=np.float32), np.ones((HD, 1), np.float32)),
        "L0q": lay(v["L0_attn_q_weight"].T), "L0k": lay(per_query_head(v["L0_attn_k_weight"].T)),
        "L0v_rep": lay(per_query_head(v["L0_attn_v_weight"].T)),
        "L0v": lay(v["L0_attn_v_weight"].T), "L0o": lay(v["L0_attn_o_weight"].T),
        "L0scales": np.stack([np.ascontiguousarray(v["L0_attn_q_scale"].reshape(KC, P).T),
                              head_scales(v["L0_attn_k_scale"]), head_scales(v["L0_attn_v_scale"])]),
        "L0_attn_o_scale": v["L0_attn_o_scale"],
        "L1q": lay(w[:, :D]), "L1k": lay(per_query_head(w[:, D:D + HD])),
        "L1v": lay(per_query_head(w[:, D + HD:])),
        "L1o": lay(v["L1_attn_Wo"]), "alibi": alibi_table(),
        "Xq": lay(v["L1_xattn_w_q"].T), "Xk": lay(per_query_head(v["L1_xattn_w_k"].T)),
        "Xv": lay(v["L1_xattn_w_v"].T), "Xo": lay(v["L1_xattn_w_out"].T),
        "ctxT": lay(v["ctx_4096"].reshape(TOK, D).T), "mask_SxS2_bk0": v["mask_SxS2_bk0"],
    }
    arrays.update(more_arrays(v))
    nc = _bacc.Bacc("TRN2", target_bir_lowering=False, num_devices=1)
    args = {}
    for name, x in arrays.items():
        arrays[name] = x = np.ascontiguousarray(x)
        args[name] = nc.dram_tensor(f"in_{name}", x.shape, mybir.dt.from_np(x.dtype), kind="ExternalInput").ap()
    out = nc.dram_tensor("out", (TOK, D), F32, kind="ExternalOutput").ap()
    decoder(nc, args, out)
    r = _run(nc, [{f"in_{k}": x for k, x in arrays.items()}], core_ids=[0])
    return r.results[0]["out"].reshape(32, SEQ, D)
```
